# Optimizing a Trainium2 kernel written in Bass

```python
import numpy as np
import jax
import jax.numpy as jnp

def _softmax(x, axis=-1):
    return jax.nn.softmax(x, axis=axis)

def _gelu(x):
    return jax.nn.gelu(x, approximate=True)

def _silu(x):
    return jax.nn.silu(x)

def _sigmoid(x):
    return jax.nn.sigmoid(x)

def _layernorm(x, axis=-1, eps=1e-05):
    m = jnp.mean(x, axis=axis, keepdims=True)
    v = jnp.var(x, axis=axis, keepdims=True)
    return (x - m) / jnp.sqrt(v + eps)

def _scatter_add(tgt, idx, src, axis=0):
    return tgt.at[idx].add(src)

def _segment_sum(src, seg, n):
    return jax.ops.segment_sum(src, seg, n)
kernel_name = 'mk_decoder_preln_d2_seqx_r2_93de48'

def setup_inputs(seed: int=0):
    np.random.seed(seed)
    _w = jnp.asarray

    def _rec_inputs():
        import jax
        import jax.numpy as jnp
        _rk = jax.random.key(seed)
        x = -0.0002928 + 1 * jax.random.normal(jax.random.fold_in(_rk, 1), (2, 2048, 512), jnp.float32)
        _lenS = 2048 - jax.random.randint(jax.random.fold_in(_rk, 7), (2,), 0, max(1, 2048 // 4) + 1, jnp.int32)
        _lenS2 = 77 - jax.random.randint(jax.random.fold_in(_rk, 8), (2,), 0, max(1, 77 // 4) + 1, jnp.int32)
        _ctx_1024P = jax.random.normal(jax.random.fold_in(_rk, 11), (2, 16, 512), jnp.float32)
        _ctx_1024c = jax.random.dirichlet(jax.random.fold_in(_rk, 511), 0.3 * jnp.ones((16,), jnp.float32), (2, 77))
        _ctx_1024t = jnp.einsum('bsk,bkd->bsd', _ctx_1024c, _ctx_1024P)
        _ctx_1024t = _ctx_1024t * jax.lax.rsqrt(jnp.mean(jnp.square(_ctx_1024t)) + 1e-12) * 0.953939
        ctx_1024 = -1.39393e-06 + 0.999914 * (_ctx_1024t + 0.3 * jax.random.normal(jax.random.fold_in(_rk, 611), (2, 77, 512), jnp.float32))
        _validS = jnp.arange(2048)[None, :] < _lenS[:, None]
        _validS2 = jnp.arange(77)[None, :] < _lenS2[:, None]
        _causal = jnp.tril(jnp.ones((2048, 2048), dtype=bool))
        mask_BxSxS2_ff1 = jnp.where(jnp.ones((2, 2048, 77), dtype=bool), 1.0, 0.0).astype(jnp.float32)
        return (x, ctx_1024, mask_BxSxS2_ff1)
    x, ctx_1024, mask_BxSxS2_ff1 = _rec_inputs()

    def _L0_attn_setup():
        import jax, jax.numpy as jnp
        import numpy as np
        B, T, D = (8, 1024, 512)
        K_SIZE = 512
        key = jax.random.key(seed)
        ks = jax.random.split(key, 4)
        s = 0.02
        return {'minibatch': jax.random.normal(ks[0], (B, T, D), dtype=jnp.float32), 'Wq': jax.random.normal(ks[1], (D, K_SIZE), dtype=jnp.float32) * s, 'bq': jnp.zeros((K_SIZE,), dtype=jnp.float32), 'Wk': jax.random.normal(ks[2], (D, K_SIZE), dtype=jnp.float32) * s, 'bk': jnp.zeros((K_SIZE,), dtype=jnp.float32), 'Wv': jax.random.normal(ks[3], (D, D), dtype=jnp.float32) * s, 'bv': jnp.zeros((D,), dtype=jnp.float32)}
    _L0_attn_all = _L0_attn_setup()
    _L0_attn_in = {k: v for k, v in _L0_attn_all.items() if k in ('Wq', 'bq', 'Wk', 'bk', 'Wv', 'bv')}
    del _L0_attn_all

    def _L0_xattn_setup():
        import jax, jax.numpy as jnp
        import numpy as np
        HIDDEN = 512
        NUM_HEADS = 16
        HEAD_DIM = HIDDEN // NUM_HEADS
        B, LQ, LK = (2, 1024, 1024)

        def _split_heads(x):
            b, l, _ = x.shape
            return x.reshape(b, l, NUM_HEADS, HEAD_DIM).transpose(0, 2, 1, 3)
        key = jax.random.key(seed)
        ks = jax.random.split(key, 9)
        s = 1.0 / np.sqrt(HIDDEN)
        return {'hidden_states_query': jax.random.normal(ks[0], (B, LQ, HIDDEN), jnp.float32), 'hidden_states_key': jax.random.normal(ks[1], (B, LK, HIDDEN), jnp.float32), 'attention_mask': jnp.ones((B, LQ, LK), jnp.float32), 'Wq': jax.random.normal(ks[2], (HIDDEN, HIDDEN), jnp.float32) * s, 'bq': jax.random.normal(ks[3], (HIDDEN,), jnp.float32) * s, 'Wk': jax.random.normal(ks[4], (HIDDEN, HIDDEN), jnp.float32) * s, 'bk': jax.random.normal(ks[5], (HIDDEN,), jnp.float32) * s, 'Wv': jax.random.normal(ks[6], (HIDDEN, HIDDEN), jnp.float32) * s, 'bv': jax.random.normal(ks[7], (HIDDEN,), jnp.float32) * s}
    _L0_xattn_all = _L0_xattn_setup()
    _L0_xattn_in = {k: v for k, v in _L0_xattn_all.items() if k in ('Wq', 'bq', 'Wk', 'bk', 'Wv', 'bv')}
    del _L0_xattn_all

    def _L0_ffn_setup():
        import jax, jax.numpy as jnp
        import numpy as np
        GROUP = 16
        EPS = 1e-05

        def _dequant(q, scale):
            w = q.astype(jnp.float32) / 7.5 - 1.0
            return w * jnp.repeat(scale, GROUP, axis=1)

        def _qlora_linear(x, q, scale, bias, la, lb):
            w = _dequant(q, scale)
            base = jnp.einsum('btd,od->bto', x, w) + bias
            lora = jnp.einsum('btr,or->bto', jnp.einsum('btd,rd->btr', x, la), lb)
            return base + lora

        def _layernorm(x, g, b):
            mu = jnp.mean(x, axis=-1, keepdims=True)
            var = jnp.mean(jnp.square(x - mu), axis=-1, keepdims=True)
            return (x - mu) * jax.lax.rsqrt(var + EPS) * g + b
        key = jax.random.key(seed)
        ks = jax.random.split(key, 6)
        D, R, B, T = (512, 32, 8, 2048)
        x = jax.random.normal(ks[0], (B, T, D), dtype=jnp.float32)
        qweights = jax.random.randint(ks[1], (6, D, D), 0, 16, dtype=jnp.int32)
        scales = jax.random.uniform(ks[2], (6, D, D // GROUP), dtype=jnp.float32)
        biases = jax.random.normal(ks[3], (6, D), dtype=jnp.float32) * 0.02
        lora_a = jax.random.normal(ks[4], (6, R, D), dtype=jnp.float32) * 0.02
        lora_b = jax.random.normal(ks[5], (6, D, R), dtype=jnp.float32) * 0.02
        ln_gamma = jnp.ones((3, D), dtype=jnp.float32)
        ln_beta = jnp.zeros((3, D), dtype=jnp.float32)
        return {'x': x, 'qweights': qweights, 'scales': scales, 'biases': biases, 'lora_a': lora_a, 'lora_b': lora_b, 'ln_gamma': ln_gamma, 'ln_beta': ln_beta}
    _L0_ffn_all = _L0_ffn_setup()
    _L0_ffn_in = {k: v for k, v in _L0_ffn_all.items() if k in ('qweights', 'scales', 'biases', 'lora_a', 'lora_b', 'ln_gamma', 'ln_beta')}
    del _L0_ffn_all

    def _L1_attn_setup():
        import jax, jax.numpy as jnp
        import numpy as np
        B, L, DM = (4, 1024, 512)
        key = jax.random.key(seed)
        ks = jax.random.split(key, 13)
        n = lambda k, shape, s=1.0: jax.random.normal(k, shape, dtype=jnp.float32) * s
        W_SCALE = 0.02
        K_SCALE = 0.02
        return {'u': n(ks[0], (B, L, DM)), 'Wq': n(ks[1], (DM, DM), W_SCALE), 'bq': n(ks[2], (DM,), W_SCALE), 'Wk': n(ks[3], (DM, DM), W_SCALE), 'bk': n(ks[4], (DM,), W_SCALE), 'Wv': n(ks[5], (DM, DM), W_SCALE), 'bv': n(ks[6], (DM,), W_SCALE), 'k_kernel': n(ks[7], (DM, L), K_SCALE), 'k_D': n(ks[8], (DM,)), 'ssm_kernel': n(ks[9], (DM, L), K_SCALE), 'D': n(ks[10], (DM,)), 'Wo': n(ks[11], (DM, DM), W_SCALE), 'bo': n(ks[12], (DM,), W_SCALE)}
    _L1_attn_all = _L1_attn_setup()
    _L1_attn_in = {k: v for k, v in _L1_attn_all.items() if k in ('Wq', 'bq', 'Wk', 'bk', 'Wv', 'bv', 'k_kernel', 'k_D', 'ssm_kernel', 'D', 'Wo', 'bo')}
    del _L1_attn_all

    def _L1_xattn_setup():
        import jax, jax.numpy as jnp
        import numpy as np
        EMBED_DIM = 512
        NUM_HEADS = 16
        HEAD_DIM = EMBED_DIM // NUM_HEADS
        key = jax.random.key(seed)
        ks = jax.random.split(key, 7)
        B, S, E = (2, 1024, EMBED_DIM)
        scale = 1.0 / np.sqrt(E)
        return {'query': jax.random.normal(ks[0], (B, S, E), dtype=jnp.float32), 'key': jax.random.normal(ks[1], (B, S, E), dtype=jnp.float32), 'value': jax.random.normal(ks[2], (B, S, E), dtype=jnp.float32), 'Wq': jax.random.normal(ks[3], (E, E), dtype=jnp.float32) * scale, 'Wk': jax.random.normal(ks[4], (E, E), dtype=jnp.float32) * scale, 'Wv': jax.random.normal(ks[5], (E, E), dtype=jnp.float32) * scale, 'Wo': jax.random.normal(ks[6], (E, E), dtype=jnp.float32) * scale}
    _L1_xattn_all = _L1_xattn_setup()
    _L1_xattn_in = {k: v for k, v in _L1_xattn_all.items() if k in ('Wq', 'Wk', 'Wv', 'Wo')}
    del _L1_xattn_all

    def _L1_ffn_setup():
        import jax, jax.numpy as jnp
        import numpy as np
        NUM_EXPERTS = 64
        TOP_K = 2
        B, S, EMB, MLP = (4, 1024, 512, 1024)
        key = jax.random.key(seed)
        k1, k2, k3, k4, k5 = jax.random.split(key, 5)
        inputs = jax.random.normal(k1, (B, S, EMB), dtype=jnp.float32)
        gate_kernel = jax.random.normal(k2, (EMB, NUM_EXPERTS), dtype=jnp.float32) / np.sqrt(EMB)
        w0 = jax.random.normal(k3, (NUM_EXPERTS, EMB, MLP), dtype=jnp.float32) / np.sqrt(EMB)
        w1 = jax.random.normal(k4, (NUM_EXPERTS, EMB, MLP), dtype=jnp.float32) / np.sqrt(EMB)
        wo = jax.random.normal(k5, (NUM_EXPERTS, MLP, EMB), dtype=jnp.float32) / np.sqrt(MLP)
        return {'inputs': inputs, 'gate_kernel': gate_kernel, 'w0': w0, 'w1': w1, 'wo': wo}
    _L1_ffn_all = _L1_ffn_setup()
    _L1_ffn_in = {k: v for k, v in _L1_ffn_all.items() if k in ('gate_kernel', 'w0', 'w1', 'wo')}
    del _L1_ffn_all
    return {'x': x, 'ctx_1024': ctx_1024, 'mask_BxSxS2_ff1': mask_BxSxS2_ff1, 'L0_attn_Wq': _L0_attn_in['Wq'], 'L0_attn_bq': _L0_attn_in['bq'], 'L0_attn_Wk': _L0_attn_in['Wk'], 'L0_attn_bk': _L0_attn_in['bk'], 'L0_attn_Wv': _L0_attn_in['Wv'], 'L0_attn_bv': _L0_attn_in['bv'], 'L0_xattn_Wq': _L0_xattn_in['Wq'], 'L0_xattn_bq': _L0_xattn_in['bq'], 'L0_xattn_Wk': _L0_xattn_in['Wk'], 'L0_xattn_bk': _L0_xattn_in['bk'], 'L0_xattn_Wv': _L0_xattn_in['Wv'], 'L0_xattn_bv': _L0_xattn_in['bv'], 'L0_ffn_qweights': _L0_ffn_in['qweights'], 'L0_ffn_scales': _L0_ffn_in['scales'], 'L0_ffn_biases': _L0_ffn_in['biases'], 'L0_ffn_lora_a': _L0_ffn_in['lora_a'], 'L0_ffn_lora_b': _L0_ffn_in['lora_b'], 'L0_ffn_ln_gamma': _L0_ffn_in['ln_gamma'], 'L0_ffn_ln_beta': _L0_ffn_in['ln_beta'], 'L1_attn_Wq': _L1_attn_in['Wq'], 'L1_attn_bq': _L1_attn_in['bq'], 'L1_attn_Wk': _L1_attn_in['Wk'], 'L1_attn_bk': _L1_attn_in['bk'], 'L1_attn_Wv': _L1_attn_in['Wv'], 'L1_attn_bv': _L1_attn_in['bv'], 'L1_attn_k_kernel': _L1_attn_in['k_kernel'], 'L1_attn_k_D': _L1_attn_in['k_D'], 'L1_attn_ssm_kernel': _L1_attn_in['ssm_kernel'], 'L1_attn_D': _L1_attn_in['D'], 'L1_attn_Wo': _L1_attn_in['Wo'], 'L1_attn_bo': _L1_attn_in['bo'], 'L1_xattn_Wq': _L1_xattn_in['Wq'], 'L1_xattn_Wk': _L1_xattn_in['Wk'], 'L1_xattn_Wv': _L1_xattn_in['Wv'], 'L1_xattn_Wo': _L1_xattn_in['Wo'], 'L1_ffn_gate_kernel': _L1_ffn_in['gate_kernel'], 'L1_ffn_w0': _L1_ffn_in['w0'], 'L1_ffn_w1': _L1_ffn_in['w1'], 'L1_ffn_wo': _L1_ffn_in['wo']}

def reference(x, ctx_1024, mask_BxSxS2_ff1, L0_attn_Wq, L0_attn_bq, L0_attn_Wk, L0_attn_bk, L0_attn_Wv, L0_attn_bv, L0_xattn_Wq, L0_xattn_bq, L0_xattn_Wk, L0_xattn_bk, L0_xattn_Wv, L0_xattn_bv, L0_ffn_qweights, L0_ffn_scales, L0_ffn_biases, L0_ffn_lora_a, L0_ffn_lora_b, L0_ffn_ln_gamma, L0_ffn_ln_beta, L1_attn_Wq, L1_attn_bq, L1_attn_Wk, L1_attn_bk, L1_attn_Wv, L1_attn_bv, L1_attn_k_kernel, L1_attn_k_D, L1_attn_ssm_kernel, L1_attn_D, L1_attn_Wo, L1_attn_bo, L1_xattn_Wq, L1_xattn_Wk, L1_xattn_Wv, L1_xattn_Wo, L1_ffn_gate_kernel, L1_ffn_w0, L1_ffn_w1, L1_ffn_wo):
    import jax
    import jax.numpy as jnp

    def _L0_attn_ref(minibatch, Wq, bq, Wk, bk, Wv, bv):
        import jax, jax.numpy as jnp
        import numpy as np
        B, T, D = (8, 1024, 512)
        K_SIZE = 512
        queries = minibatch @ Wq + bq
        keys = minibatch @ Wk + bk
        values = minibatch @ Wv + bv
        logits = jnp.einsum('bik,bjk->bij', queries, keys)
        t = logits.shape[1]
        causal = jnp.triu(jnp.ones((t, t), dtype=bool), k=1)
        logits = jnp.where(causal[None, :, :], -jnp.inf, logits)
        sqrt_k = jnp.sqrt(jnp.asarray(Wq.shape[1], dtype=logits.dtype))
        probs = jax.nn.softmax(logits, axis=1) / sqrt_k
        read = jnp.einsum('bij,bjv->biv', probs, values)
        return minibatch + read

    def _L0_xattn_ref(hidden_states_query, hidden_states_key, attention_mask, Wq, bq, Wk, bk, Wv, bv):
        import jax, jax.numpy as jnp
        import numpy as np
        HIDDEN = 512
        NUM_HEADS = 16
        HEAD_DIM = HIDDEN // NUM_HEADS
        B, LQ, LK = (2, 1024, 1024)

        def _split_heads(x):
            b, l, _ = x.shape
            return x.reshape(b, l, NUM_HEADS, HEAD_DIM).transpose(0, 2, 1, 3)
        q = _split_heads(hidden_states_query @ Wq.T + bq)
        k = _split_heads(hidden_states_key @ Wk.T + bk)
        v = _split_heads(hidden_states_key @ Wv.T + bv)
        scale = 1.0 / np.sqrt(HEAD_DIM)
        scores = jnp.einsum('bhqd,bhkd->bhqk', q * scale, k)
        scores = scores + ((1.0 - attention_mask) * -10000.0)[:, None, :, :]
        probs = jax.nn.softmax(scores, axis=-1)
        ctx = jnp.einsum('bhqk,bhkd->bhqd', probs, v)
        b, h, lq, d = ctx.shape
        return ctx.transpose(0, 2, 1, 3).reshape(b, lq, h * d)

    def _L0_ffn_ref(x, qweights, scales, biases, lora_a, lora_b, ln_gamma, ln_beta):
        import jax, jax.numpy as jnp
        import numpy as np
        GROUP = 16
        EPS = 1e-05

        def _dequant(q, scale):
            w = q.astype(jnp.float32) / 7.5 - 1.0
            return w * jnp.repeat(scale, GROUP, axis=1)

        def _qlora_linear(x, q, scale, bias, la, lb):
            w = _dequant(q, scale)
            base = jnp.einsum('btd,od->bto', x, w) + bias
            lora = jnp.einsum('btr,or->bto', jnp.einsum('btd,rd->btr', x, la), lb)
            return base + lora

        def _layernorm(x, g, b):
            mu = jnp.mean(x, axis=-1, keepdims=True)
            var = jnp.mean(jnp.square(x - mu), axis=-1, keepdims=True)
            return (x - mu) * jax.lax.rsqrt(var + EPS) * g + b
        h = x
        for blk in range(3):
            i0, i1 = (2 * blk, 2 * blk + 1)
            y = _qlora_linear(h, qweights[i0], scales[i0], biases[i0], lora_a[i0], lora_b[i0])
            y = _layernorm(y, ln_gamma[blk], ln_beta[blk])
            y = jax.nn.gelu(y, approximate=False)
            y = _qlora_linear(y, qweights[i1], scales[i1], biases[i1], lora_a[i1], lora_b[i1])
            h = y + h
        return h

    def _L1_attn_ref(u, Wq, bq, Wk, bk, Wv, bv, k_kernel, k_D, ssm_kernel, D, Wo, bo):
        import jax, jax.numpy as jnp
        import numpy as np
        B, L, DM = (4, 1024, 512)
        Lseq = u.shape[1]
        fft_size = 2 * Lseq
        q = jnp.einsum('blh,dh->bdl', u, Wq) + bq[None, :, None]
        k = jnp.einsum('blh,dh->bdl', u, Wk) + bk[None, :, None]
        v = jnp.einsum('blh,dh->bdl', u, Wv) + bv[None, :, None]
        k_kernel_f = jnp.fft.rfft(k_kernel, n=fft_size)
        k_f = jnp.fft.rfft(k, n=fft_size)
        shift_k = jnp.fft.irfft(k_kernel_f[None] * k_f, n=fft_size)[..., :Lseq]
        k = shift_k + k_D[None, :, None] * k
        kv = k * v
        kv_f = jnp.fft.rfft(kv, n=fft_size)
        ssm_kernel_f = jnp.fft.rfft(ssm_kernel, n=fft_size)
        y = jnp.fft.irfft(kv_f * ssm_kernel_f[None], n=fft_size)[..., :Lseq]
        y = y + kv * D[None, :, None]
        y = y * q
        y = jnp.swapaxes(y, 1, 2)
        return jnp.einsum('blh,oh->blo', y, Wo) + bo

    def _L1_xattn_ref(query, key, value, Wq, Wk, Wv, Wo):
        import jax, jax.numpy as jnp
        import numpy as np
        EMBED_DIM = 512
        NUM_HEADS = 16
        HEAD_DIM = EMBED_DIM // NUM_HEADS
        B, Sq, E = query.shape
        Sk = key.shape[1]
        H, D = (NUM_HEADS, HEAD_DIM)

        def split_heads(x, S):
            return x.reshape(B, S, H, D).transpose(0, 2, 1, 3)
        Q = split_heads(query @ Wq.T, Sq)
        K = split_heads(key @ Wk.T, Sk)
        V = split_heads(value @ Wv.T, Sk)
        scores = jnp.einsum('bhqd,bhkd->bhqk', Q, K) / jnp.sqrt(jnp.float32(D))
        causal = jnp.tril(jnp.ones((Sq, Sk), dtype=bool))
        scores = jnp.where(causal[None, None, :, :], scores, -jnp.inf)
        attn = jax.nn.softmax(scores, axis=-1)
        attn = jnp.nan_to_num(attn, nan=0.0)
        out = jnp.einsum('bhqk,bhkd->bhqd', attn, V)
        out = out.transpose(0, 2, 1, 3).reshape(B, Sq, E)
        return out @ Wo.T

    def _L1_ffn_ref(inputs, gate_kernel, w0, w1, wo):
        import jax, jax.numpy as jnp
        import numpy as np
        NUM_EXPERTS = 64
        TOP_K = 2
        B, S, EMB, MLP = (4, 1024, 512, 1024)
        b, s, e = inputs.shape
        x = inputs.reshape(b * s, e)
        gate_logits = jnp.einsum('te,ex->tx', x, gate_kernel)
        weights, selected = jax.lax.top_k(gate_logits, TOP_K)
        weights = jax.nn.softmax(weights.astype(jnp.float32), axis=-1)
        flat_experts = selected.reshape(-1)
        sort_idx = jnp.argsort(flat_experts)
        token_idx = sort_idx // TOP_K
        sorted_x = jnp.take(x, token_idx, axis=0)
        group_sizes = jnp.bincount(flat_experts, length=NUM_EXPERTS).astype(jnp.int32)
        h0 = jax.lax.ragged_dot(sorted_x, w0, group_sizes)
        h1 = jax.lax.ragged_dot(sorted_x, w1, group_sizes)
        inter = jax.nn.silu(h0) * h1
        out_sorted = jax.lax.ragged_dot(inter, wo, group_sizes)
        unsorted = jnp.take(out_sorted, jnp.argsort(sort_idx), axis=0)
        per_tok = unsorted.reshape(b * s, TOP_K, e)
        out = jnp.einsum('BKE,BK->BE', per_tok.astype(jnp.float32), weights)
        return out.reshape(b, s, e)
    x = x + _L0_attn_ref(_layernorm(x, axis=-1), L0_attn_Wq, L0_attn_bq, L0_attn_Wk, L0_attn_bk, L0_attn_Wv, L0_attn_bv)
    x = x + _L0_xattn_ref(_layernorm(x, axis=-1), ctx_1024, mask_BxSxS2_ff1, L0_xattn_Wq, L0_xattn_bq, L0_xattn_Wk, L0_xattn_bk, L0_xattn_Wv, L0_xattn_bv)
    x = x + _L0_ffn_ref(_layernorm(x, axis=-1), L0_ffn_qweights, L0_ffn_scales, L0_ffn_biases, L0_ffn_lora_a, L0_ffn_lora_b, L0_ffn_ln_gamma, L0_ffn_ln_beta)
    x = x + _L1_attn_ref(_layernorm(x, axis=-1), L1_attn_Wq, L1_attn_bq, L1_attn_Wk, L1_attn_bk, L1_attn_Wv, L1_attn_bv, L1_attn_k_kernel, L1_attn_k_D, L1_attn_ssm_kernel, L1_attn_D, L1_attn_Wo, L1_attn_bo)
    x = x + _L1_xattn_ref(_layernorm(x, axis=-1), ctx_1024, ctx_1024, L1_xattn_Wq, L1_xattn_Wk, L1_xattn_Wv, L1_xattn_Wo)
    x = x + _L1_ffn_ref(_layernorm(x, axis=-1), L1_ffn_gate_kernel, L1_ffn_w0, L1_ffn_w1, L1_ffn_wo)
    return x

_drawn_inputs = setup_inputs


def setup_inputs(seed=0):
    import zlib

    import numpy as np

    out = dict(_drawn_inputs(seed))
    spreads = {'L0_attn_bq': (0.0, 0.1),
     'L0_attn_bk': (0.0, 0.1),
     'L0_attn_bv': (0.0, 0.1),
     'L0_ffn_ln_gamma': (1.0, 0.2),
     'L0_ffn_ln_beta': (0.0, 0.1)}
    factors = {}
    for name, (base, spread) in spreads.items():
        noise = np.random.default_rng([zlib.crc32(name.encode()), seed]).standard_normal(out[name].shape)
        drawn = base * np.exp(spread * noise) if base else spread * noise
        out[name] = jnp.asarray(drawn.astype(out[name].dtype))
    for name, factor in factors.items():
        out[name] = (out[name] * factor).astype(out[name].dtype)
    return out
```

```python
import numpy as np
import concourse.bass as bass
from concourse import mybir
from contextlib import ExitStack

F32 = mybir.dt.float32
I32 = mybir.dt.int32
U32 = mybir.dt.uint32
ALU = mybir.AluOpType
ACT = mybir.ActivationFunctionType
AX = mybir.AxisListType

P = 128
B, S, D = 2, 2048, 512
N = B * S
KD = D // P
TJ = 4
CH = TJ * P
NC = N // CH
CB = S // CH
SK = 77
H, HD = 16, 32
EPS = 1e-5
NEG = -1e30


class Count:

    def __init__(self, st, name, per, unit=1, lead=1):
        self.sem = st.sem(name)
        self.per, self.unit, self.lead = per, unit, lead

    def start(self, eng):
        eng.sem_inc(self.sem, self.lead * self.per * self.unit)

    def __call__(self, c, k=None):
        k = self.per if k is None else k
        return self.sem, (c * self.per + (self.lead * self.per + k)) * self.unit


class Stage:

    def __init__(self, nc, name):
        self.nc, self.name, self.ctx, self.sems = nc, name, ExitStack(), []
        self.passed = self.sem("passed")

    def __enter__(self):
        return self

    def __exit__(self, *a):
        self.ctx.close()
        self.nc.clear_and_free_semaphores(self.sems)
        self.nc.all_engine_barrier()

    def sb(self, name, shape, dt=F32):
        return self.ctx.enter_context(self.nc.sbuf_tensor(f"{self.name}_{name}", shape, dt))

    def banks(self):
        return self.ctx.enter_context(self.nc.psum_tensor(f"{self.name}_ps", [P, 8, 512], F32))

    def sem(self, name):
        self.sems.append(self.nc.alloc_semaphore(f"{self.name}_{name}"))
        return self.sems[-1]

    def plain(self, eng):
        eng.sem_inc(self.passed, 1)

    def count(self, name, per, unit=1, lead=1):
        return Count(self, name, per, unit, lead)


def chunk_rows(t, c):
    v = t.rearrange("(c j p) d -> c p j d", p=P, j=TJ)
    if isinstance(c, int):
        return v[c]
    return v[bass.ds(c, 1)].rearrange("o p j d -> p (o j) d")


def over_chunks(eng, n, front, main):
    if front:
        front(0, 0)
    with eng.Fori(0, n // 2 - 1) as i:
        for p in range(2):
            if front:
                front(i * 2 + (p + 1), 1 - p)
            if main:
                main(i * 2 + p, p)
    if front:
        front(n - 1, 1)
    for p in range(2):
        if main:
            main(n - 2 + p, p)


def weight_view(w):
    return w.rearrange("(k p) n -> p k n", p=P)


class Front:

    def __init__(self, st, ps, bank, src, x=None, xn=None, xT=None, norm=True):
        self.st, self.src, self.norm = st, src, norm
        self.x = x if x is not None else st.sb("x", [P, 2, TJ, D])
        self.xn = (xn if xn is not None else st.sb("xn", [P, 2, TJ, D])) if norm else self.x
        self.xT = xT if xT is not None else st.sb("xT", [P, 2, KD, CH])
        self.bank, self.ps = bank, ps
        self.bn = st.sb("bn", [P, 2, TJ, 6])
        self.mv = st.sb("mv", [P, 2, TJ, 2])
        self.rs = st.sb("rs", [P, 2, TJ])
        self.half = st.sb("mhalf", [P, TJ])
        self.half_set = st.sem("half_set")
        self.x_in = [st.sem("x_in0"), st.sem("x_in1")]
        self.bn_done = st.count("bn_done", TJ)
        self.mv_done = st.count("mv_done", TJ)
        self.var_done = st.count("var_done", 1)
        self.rs_done = st.count("rs_done", 1)
        self.xn_done = st.count("xn_done", TJ)
        self.tp_done = st.count("tp_done", TJ)
        self.xT_done = st.count("xT_done", TJ)

    def start_dve(self, dve):
        for c in (self.bn_done, self.mv_done, self.xn_done):
            c.start(dve)

    def start_pool(self, pool):
        for c in (self.var_done, self.rs_done):
            c.start(pool)
        pool.memset(self.half[:, :], -0.5).then_inc(self.half_set, 1)

    def load(self, sp, c, p):
        self.st.plain(sp)
        sp.dma_start(self.x[:, p], chunk_rows(self.src, c)).then_inc(self.x_in[p], 16)

    def x_ready(self, c, p):
        if isinstance(c, int):
            return self.x_in[p], 16 * (c // 2 + 1)
        return self.x_in[p], (c - p) * 8 + 16

    def stats(self, dve, c, p):
        dve.wait_ge(*self.x_ready(c, p))
        dve.wait_ge(*self.mv_done(c - 2))
        for j in range(TJ):
            dve.bn_stats(self.bn[:, p, j, :], self.x[:, p, j, :]).then_inc(self.bn_done.sem, 1)
        dve.wait_ge(*self.var_done(c - 2))
        dve.wait_ge(*self.xn_done(c - 2))
        for j in range(TJ):
            dve.wait_ge(*self.bn_done(c, j + 1))
            self.st.plain(dve)
            dve.bn_aggr(self.mv[:, p, j, :], self.bn[:, p, j, :]).then_inc(self.mv_done.sem, 1)

    def rstd(self, pool, c, p):
        pool.wait_ge(*self.mv_done(c))
        pool.wait_ge(*self.xn_done(c - 2))
        self.st.plain(pool)
        pool.tensor_scalar(self.rs[:, p], self.mv[:, p, :, 1], EPS, None, ALU.add).then_inc(self.var_done.sem, 1)
        pool.wait_ge(*self.var_done(c))
        pool.wait_ge(self.half_set, 1)
        pool.tensor_tensor(self.rs[:, p], self.rs[:, p], self.half[:, :], ALU.pow).then_inc(self.rs_done.sem, 1)

    def normalise(self, dve, c, p, extra=()):
        dve.wait_ge(*self.rs_done(c))
        dve.wait_ge(*self.tp_done(c - 2))
        for w in extra:
            dve.wait_ge(*w)
        for j in range(TJ):
            dve.tensor_scalar(self.xn[:, p, j, :], self.x[:, p, j, :], self.mv[:, p, j, 0:1],
                              self.rs[:, p, j:j + 1], ALU.subtract, ALU.mult).then_inc(self.xn_done.sem, 1)

    def turn(self, pe, c, p, ident, nb=2):
        for j in range(TJ):
            if self.norm:
                pe.wait_ge(*self.xn_done(c, j + 1))
            elif j == 0:
                pe.wait_ge(*self.x_ready(c, p))
            pe.wait_ge(*self.xT_done(c, j + 1 - nb))
            bank = self.ps[:, self.bank + j % nb, :]
            for k in range(KD):
                i = pe.transpose(bank[:, k * P:(k + 1) * P], self.xn[:, p, j, k * P:(k + 1) * P], ident[:, :])
            i.then_inc(self.tp_done.sem, 1)

    def keep(self, act, c, p, used, nb=2):
        act.wait_ge(*used)
        for j in range(TJ):
            act.wait_ge(*self.tp_done(c, j + 1))
            act.activation(self.xT[:, p, :, j * P:(j + 1) * P],
                           self.ps[:, self.bank + j % nb, :].rearrange("p (k t) -> p k t", k=KD),
                           ACT.Copy).then_inc(self.xT_done.sem, 1)


def stage_attention(nc, x_in, x_out, ident_d, tri_d, wq, wk, wv, bq, bk, bv):
    NJ = S // P
    with Stage(nc, "at") as st:
        ps = st.banks()
        ident = st.sb("ident", [P, P])
        tri = st.sb("tri", [P, P])
        bqT = st.sb("bqT", [P, KD])
        bkT = st.sb("bkT", [P, KD])
        bvB = st.sb("bvB", [P, D])
        qT = st.sb("qT", [P, KD, S])
        kT = st.sb("kT", [P, KD, S])
        v = st.sb("v", [P, NJ, D])
        acc = st.sb("acc", [P, NJ, D])
        region = st.sb("region", [P, 18 * 1024])
        cut = lambda i, n: region[:, i * 1024:(i + n) * 1024]
        xb = cut(0, 4).rearrange("p (b j d) -> p b j d", b=2, j=TJ)
        xnb = cut(4, 4).rearrange("p (b j d) -> p b j d", b=2, j=TJ)
        xTb = cut(8, 4).rearrange("p (b k t) -> p b k t", b=2, k=KD)
        w_sb = [cut(12 + 2 * i, 2).rearrange("p (k n) -> p k n", k=KD) for i in range(3)]
        prob = [cut(0, 8).rearrange("p (j i) -> p j i", j=4), cut(8, 6).rearrange("p (j i) -> p j i", j=4)]
        nmax = st.sb("nmax", [P, NJ])
        rmax = st.sb("rmax", [P, NJ])
        rsum = st.sb("rsum", [P, NJ])
        rinv = st.sb("rinv", [P, NJ])
        f = Front(st, ps, 6, x_in, xb, xnb, xTb)
        consts_in = st.sem("consts_in")
        w_in = st.sem("w_in")
        qk_mm = st.count("qk_mm", 12)
        qk_done = st.count("qk_done", 8)
        v_done = st.count("v_done", TJ)
        m_done = st.count("m_done", 1)
        PV = [(g, it) for g in range(4) for it in range(4 * g, NJ)]
        s_mm = st.count("s_mm", NJ)
        tri_done = st.count("tri_done", NJ)
        max_done = st.count("max_done", NJ)
        nmax_done = st.count("nmax_done", NJ)
        exp_done = st.count("exp_done", NJ)
        inv_done = st.count("inv_done", NJ)
        vs_done = st.count("vs_done", NJ)
        pv_mm = st.count("pv_mm", len(PV))
        acc_done = st.count("acc_done", len(PV))
        out_done = st.count("out_done", CB, 16)

        def pv_after(j):
            g, jj = j // 4 - 1, j % 4
            if g < 0:
                return []
            mine = [n for n, (gg, _) in enumerate(PV) if gg == g]
            if j == NJ:
                return mine
            q = len(mine) // 4
            return mine[q * jj:q * jj + q]

        rinv_done = st.sem("rinv_done")

        block = st.ctx.enter_context(nc.Block())

        @block.sync
        def _(sp):
            out_done.start(sp)
            for dst, src in ((ident, ident_d), (tri, tri_d)):
                sp.dma_start(dst[:, :], src).then_inc(consts_in, 16)
            sp.dma_start(bqT[:, :], bq.rearrange("(k p) -> p k", p=P), allow_slow_non_contiguous=True).then_inc(consts_in, 16)
            sp.dma_start(bkT[:, :], bk.rearrange("(k p) -> p k", p=P), allow_slow_non_contiguous=True).then_inc(consts_in, 16)
            sp.dma_start(bvB[:, :], bv.rearrange("(o n) -> o n", o=1).to_broadcast([P, D])).then_inc(consts_in, 16)
            with sp.Fori(0, B) as b:
                sp.wait_ge(*pv_mm(b - 1))
                for ci in range(CB):
                    if ci >= 2:
                        sp.wait_ge(*f.xn_done(b * CB + (ci - 2)))
                        st.plain(sp)
                        sp.wait_ge(*m_done(b * CB + (ci - 2)))
                    f.load(sp, b * CB + ci, ci % 2)
                    if ci == 0:
                        for i, w in enumerate((wq, wk, wv)):
                            sp.dma_start(w_sb[i], weight_view(w)).then_inc(w_in, 16)
                for ci in range(CB):
                    sp.wait_ge(*acc_done(b, PV.index((ci, 4 * ci + 3)) + 1))
                    st.plain(sp)
                    sp.dma_start(chunk_rows(x_out, b * CB + ci), acc[:, 4 * ci:4 * ci + 4, :]).then_inc(out_done.sem, 16)
            sp.wait_ge(*out_done(B - 1))

        @block.gpsimd
        def _(pool):
            f.start_pool(pool)
            m_done.start(pool)
            with pool.Fori(0, B) as b:
                pool.wait_ge(*out_done(b - 1))
                for ci in range(CB):
                    c = b * CB + ci
                    f.rstd(pool, c, ci % 2)
                    pool.wait_ge(*f.xn_done(c))
                    pool.tensor_tensor(acc[:, 4 * ci:4 * ci + 4, :], f.x[:, ci % 2], f.xn[:, ci % 2],
                                       ALU.add).then_inc(m_done.sem, 1)

        @block.vector
        def _(dve):
            f.start_dve(dve)
            for s in (v_done, tri_done, max_done, nmax_done, inv_done, vs_done, acc_done):
                s.start(dve)
            dve.wait_ge(consts_in, 16 * 5)
            with dve.Fori(0, B) as b:
                def front(ci):
                    c = b * CB + ci
                    f.stats(dve, c, ci % 2)
                    f.normalise(dve, c, ci % 2, extra=[m_done(c - 2)])

                front(0)
                for ci in range(CB):
                    if ci + 1 < CB:
                        front(ci + 1)
                    for j in range(TJ):
                        dve.wait_ge(*qk_mm(b * CB + ci, 8 + j + 1))
                        dve.tensor_tensor(v[:, TJ * ci + j, :], ps[:, j, :], bvB[:, :], ALU.add).then_inc(v_done.sem, 1)

                def add_out(n):
                    g, it = PV[n]
                    dve.wait_ge(*pv_mm(b, n + 1))
                    if g == 0 and it % TJ == 0:
                        dve.wait_ge(*m_done(b * CB + it // TJ))
                    if g:
                        dve.wait_ge(*acc_done(b, PV.index((g - 1, it)) + 1))
                    dve.tensor_tensor(acc[:, it, :], acc[:, it, :], ps[:, 4 + n % 4, :], ALU.add).then_inc(acc_done.sem, 1)

                for j in range(NJ):
                    row = ps[:, 0:4, :].rearrange("p b i -> p (b i)")
                    dve.wait_ge(*s_mm(b, j + 1))
                    diag = row[:, j * P:(j + 1) * P]
                    dve.tensor_tensor(diag, diag, tri[:, :], ALU.add).then_inc(tri_done.sem, 1)
                    dve.wait_ge(*tri_done(b, j + 1))
                    dve.tensor_reduce(rmax[:, j:j + 1], row[:, j * P:], AX.X, ALU.max).then_inc(max_done.sem, 1)
                    dve.wait_ge(*max_done(b, j + 1))
                    dve.tensor_scalar(nmax[:, j:j + 1], rmax[:, j:j + 1], -1.0, None, ALU.mult).then_inc(nmax_done.sem, 1)
                    for n in pv_after(j):
                        add_out(n)
                    dve.wait_ge(*exp_done(b, j + 1))
                    dve.tensor_scalar(rsum[:, j:j + 1], rsum[:, j:j + 1], float(D) ** 0.5, None,
                                      ALU.mult).then_inc(inv_done.sem, 1)
                    dve.wait_ge(*inv_done(b, j + 1))
                    dve.reciprocal(rinv[:, j:j + 1], rsum[:, j:j + 1]).then_inc(rinv_done, 1)
                    dve.wait_ge(rinv_done, b * NJ + (j + 1))
                    dve.tensor_scalar(v[:, j, :], v[:, j, :], rinv[:, j:j + 1], None, ALU.mult).then_inc(vs_done.sem, 1)
                for n in pv_after(NJ):
                    add_out(n)


        @block.scalar
        def _(act):
            for s in (f.xT_done, qk_done, exp_done):
                s.start(act)
            act.wait_ge(consts_in, 16 * 5)
            with act.Fori(0, B) as b:
                front = lambda ci: f.keep(act, b * CB + ci, ci % 2, qk_mm(b * CB + (ci - 2)))
                front(0)
                for ci in range(CB):
                    if ci + 1 < CB:
                        front(ci + 1)
                    for u in range(8):
                        dst, bias = ((qT, bqT), (kT, bkT))[u // 4]
                        m = u % 4
                        act.wait_ge(*qk_mm(b * CB + ci, u + 1))
                        act.activation(dst[:, m, ci * CH:(ci + 1) * CH], ps[:, u % 4, :], ACT.Identity,
                                       bias=bias[:, m:m + 1]).then_inc(qk_done.sem, 1)
                for j in range(NJ):
                    g, jj = j // 4, j % 4
                    row = ps[:, 0:4, :].rearrange("p b i -> p (b i)")
                    act.wait_ge(*nmax_done(b, j + 1))
                    if j == 0:
                        act.wait_ge(*m_done(b * CB + (CB - 1)))
                    if g >= 2 and jj == 0:
                        act.wait_ge(*pv_mm(b, PV.index((g - 2, NJ - 1)) + 1))
                    act.activation(prob[g % 2][:, jj, (j - 4 * g) * P:S - 4 * g * P], row[:, j * P:], ACT.Exp,
                                   bias=nmax[:, j:j + 1], accum_out=rsum[:, j:j + 1]).then_inc(exp_done.sem, 1)

        @block.tensor
        def _(pe):
            for s in (f.tp_done, qk_mm, s_mm, pv_mm):
                s.start(pe)
            pe.wait_ge(consts_in, 16 * 5)
            with pe.Fori(0, B) as b:
                f.turn(pe, b * CB, 0, ident)
                pe.wait_ge(w_in, (b + 1) * 48)
                for ci in range(CB):
                    c = b * CB + ci
                    if ci + 1 < CB:
                        f.turn(pe, c + 1, (ci + 1) % 2, ident)
                    pe.wait_ge(*f.xT_done(c))
                    for u in range(12):
                        if u < 4:
                            pe.wait_ge(*v_done(c - 1, u + 1))
                        else:
                            pe.wait_ge(*qk_done(c, u - 4 + 1))
                        for k in range(KD):
                            if u < 8:
                                i = pe.matmul(ps[:, u % 4, :], w_sb[u // 4][:, k, (u % 4) * P:(u % 4 + 1) * P],
                                              f.xT[:, ci % 2, k, :], start=k == 0, stop=k == KD - 1)
                            else:
                                i = pe.matmul(ps[:, u % 4, :], f.xT[:, ci % 2, k, (u % 4) * P:(u % 4 + 1) * P],
                                              w_sb[2][:, k, :], start=k == 0, stop=k == KD - 1)
                        i.then_inc(qk_mm.sem, 1)

                def product(n):
                    g, it = PV[n]
                    if n >= 4:
                        pe.wait_ge(*acc_done(b, n - 3))
                    js = [j for j in range(4 * g, 4 * g + 4) if j <= it]
                    pe.wait_ge(*vs_done(b, js[-1] + 1))
                    for j in js:
                        i = pe.matmul(ps[:, 4 + n % 4, :], prob[g % 2][:, j % 4, (it - 4 * g) * P:(it - 4 * g + 1) * P],
                                      v[:, j, :], start=j == js[0], stop=j == js[-1])
                    i.then_inc(pv_mm.sem, 1)

                for j in range(NJ):
                    if j == 0:
                        pe.wait_ge(*v_done(b * CB + (CB - 1)))
                        pe.wait_ge(*qk_done(b * CB + (CB - 1)))
                        pe.wait_ge(*f.xT_done(b * CB + (CB - 1)))
                    else:
                        pe.wait_ge(*exp_done(b, j))
                    for ic in range(j // 4, 4):
                        lo = max(ic * CH, j * P)
                        for k in range(KD):
                            i = pe.matmul(ps[:, ic, lo - ic * CH:], kT[:, k, j * P:(j + 1) * P],
                                          qT[:, k, lo:(ic + 1) * CH], start=k == 0, stop=k == KD - 1)
                    i.then_inc(s_mm.sem, 1)
                    for n in pv_after(j):
                        product(n)
                for n in pv_after(NJ):
                    product(n)


def pick(t, b):
    if isinstance(b, int):
        return t[:, b]
    v = t[:, bass.ds(b, 1)]
    n = len(v.shape)
    rest = [f"d{i}" for i in range(n - 2)]
    return v.rearrange(f"p o {' '.join(rest)} -> p (o {rest[0]}) {' '.join(rest[1:])}")


def stage_cross(nc, tag, x_in, x_out, ident_d, ctxT_d, mask_d, wq, wk, wv, bq=None, bk=None, bv=None, wo=None):
    HB = H // 2
    U = 2 * TJ
    W4 = 4 * SK
    scale = 1.0 / float(np.sqrt(HD))
    biased = bq is not None
    with Stage(nc, tag) as st:
        ps = st.banks()
        ident = st.sb("ident", [P, P])
        wq_s = st.sb("wq", [P, KD, D])
        wk_s = st.sb("wk", [P, KD, D])
        wv_s = st.sb("wv", [P, KD, D])
        wo_s = st.sb("wo", [P, KD, D]) if wo is not None else None
        ctxT = st.sb("ctxT", [P, KD, B * SK])
        kblk = st.sb("kblk", [P, B, KD, W4])
        v1 = st.sb("v1", [SK, B, H, HD + 1])
        bias = st.sb("bias", [P, 3, KD])
        bvB = st.sb("bvB", [SK, D])
        mask = st.sb("mask", [P, 2, TJ, SK])
        qT = st.sb("qT", [P, 2, KD, CH])
        s_sb = st.sb("s", [P, 2, HB, SK])
        mx = st.sb("mx", [P, 2, HB])
        rec = st.sb("rec", [P, 2, HB])
        pT = st.sb("pT", [SK, 2, HB, P])
        o = st.sb("o", [P, 2, TJ, D])
        y = st.sb("y", [P, 2, TJ, D])
        oT = st.sb("oT", [P, 2, KD, P]) if wo is not None else None
        f = Front(st, ps, 5, x_in)
        loads = 5 + (3 if biased else 0) + (1 if wo is not None else 0)
        consts_in = st.sem("consts_in")
        kv_mm = st.sem("kv_mm")
        zeroed = st.sem("zeroed")
        bias_set = st.sem("bias_set")
        kv_set = st.sem("kv_set")
        mask_in = [st.sem("mask_in0"), st.sem("mask_in1")]
        mask_set = st.count("mask_set", 1)
        q_mm = st.count("q_mm", KD)
        q_done = st.count("q_done", KD)
        s_mm = st.count("s_mm", U)
        add_done = st.count("add_done", U)
        max_done = st.count("max_done", U)
        sub_done = st.count("sub_done", U)
        exp_done = st.count("exp_done", U)
        p_mm = st.count("p_mm", U)
        pT_done = st.count("pT_done", U)
        pv_mm = st.count("pv_mm", U)
        rec_done = st.count("rec_done", U)
        o_done = st.count("o_done", U)
        y_done = st.count("y_done", TJ)
        oT_mm = st.count("oT_mm", TJ)
        oT_done = st.count("oT_done", TJ)
        wo_mm = st.count("wo_mm", TJ)
        stored = st.count("stored", 1, 16)
        counted_dve = [add_done, max_done, rec_done, o_done, mask_set] + ([y_done] if wo is not None else [])

        block = st.ctx.enter_context(nc.Block())

        @block.sync
        def _(sp):
            stored.start(sp)
            for dst, src in ((wk_s, wk), (wv_s, wv), (wq_s, wq), (ctxT, ctxT_d)) + (((wo_s, wo),) if wo is not None else ()):
                sp.dma_start(dst[:, :, :], weight_view(src)).then_inc(consts_in, 16)
            sp.dma_start(ident[:, :], ident_d).then_inc(consts_in, 16)
            if biased:
                for i, v in enumerate((bq, bk)):
                    sp.dma_start(bias[:, i, :], v.rearrange("(k p) -> p k", p=P), allow_slow_non_contiguous=True).then_inc(consts_in, 16)
                sp.dma_start(bvB[:, :], bv.rearrange("(o n) -> o n", o=1).to_broadcast([SK, D])).then_inc(consts_in, 16)

            def front(c, p):
                sp.wait_ge(*f.xn_done(c - 2))
                sp.wait_ge(*y_done(c - 2))
                f.load(sp, c, p)
                sp.wait_ge(*add_done(c - 2))
                sp.wait_ge(*mask_set(c - 2))
                st.plain(sp)
                sp.dma_start(mask[:, p], chunk_rows(mask_d, c)).then_inc(mask_in[p], 16)

            def main(c, p):
                sp.wait_ge(*y_done(c))
                st.plain(sp)
                sp.dma_start(chunk_rows(x_out, c), y[:, p]).then_inc(stored.sem, 16)

            over_chunks(sp, NC, front, main)
            sp.wait_ge(*stored(NC - 1))

        @block.gpsimd
        def _(pool):
            f.start_pool(pool)
            sub_done.start(pool)
            pool.memset(kblk[:, :, :, :], 0.0).then_inc(zeroed, 1)
            pool.memset(v1[:, :, :, HD:HD + 1], 1.0).then_inc(zeroed, 1)
            if wo is None:
                y_done.start(pool)

            def main(c, p):
                for u in range(U + 2):
                    if u < U:
                        pool.wait_ge(*max_done(c, u + 1))
                        s3 = s_sb[:, u % 2]
                        pool.tensor_tensor(s3, s3, mx[:, u % 2].unsqueeze(2).to_broadcast([P, HB, SK]),
                                           ALU.subtract).then_inc(sub_done.sem, 1)
                    if wo is None and u >= 3 and u % 2 == 1:
                        j = (u - 3) // 2
                        pool.wait_ge(*o_done(c, 2 * j + 2))
                        if j == 0:
                            pool.wait_ge(*stored(c - 2))
                        pool.tensor_tensor(y[:, p, j, :], f.x[:, p, j, :], o[:, p, j, :], ALU.add).then_inc(y_done.sem, 1)

            over_chunks(pool, NC, lambda c, p: f.rstd(pool, c, p), main)

        @block.vector
        def _(dve):
            f.start_dve(dve)
            for s in counted_dve:
                s.start(dve)
            dve.wait_ge(consts_in, 16 * loads)
            for b in range(B):
                dve.wait_ge(kv_mm, KD + b + 1)
                src = ps[0:SK, 4 + b, :].rearrange("s (h d) -> s h d", h=H)
                if biased:
                    dve.tensor_tensor(v1[:, b, :, 0:HD], src, bvB[:, :].rearrange("s (h d) -> s h d", h=H),
                                      ALU.add).then_inc(kv_set, 1)
                else:
                    dve.tensor_copy(v1[:, b, :, 0:HD], src).then_inc(kv_set, 1)

            def front(c, p):
                f.stats(dve, c, p)
                f.normalise(dve, c, p)
                dve.wait_ge(mask_in[p], 16 * (c // 2 + 1) if isinstance(c, int) else (c - p) * 8 + 16)
                if biased:
                    dve.tensor_scalar(mask[:, p], mask[:, p], 10000.0, -10000.0, ALU.mult, ALU.add).then_inc(mask_set.sem, 1)
                else:
                    dve.sem_inc(mask_set.sem, 1)

            def main(c, p):
                for u in range(U + 4):
                    j, half = u // 2, u % 2
                    if u < U:
                        dve.wait_ge(*s_mm(c, u + 1))
                        if u == 0:
                            dve.wait_ge(*mask_set(c))
                        dve.wait_ge(*p_mm(c, u - 1))
                        dve.tensor_tensor(s_sb[:, u % 2].rearrange("p (m h) s -> p m h s", m=2),
                                          ps[:, 0:2, 0:W4].rearrange("p m (h s) -> p m h s", h=4),
                                          mask[:, p, j].unsqueeze(1).unsqueeze(1).to_broadcast([P, 2, 4, SK]),
                                          ALU.add).then_inc(add_done.sem, 1)
                        dve.wait_ge(*add_done(c, u + 1))
                        dve.wait_ge(*sub_done(c, u - 1))
                        dve.tensor_reduce(mx[:, u % 2], s_sb[:, u % 2], AX.X, ALU.max).then_inc(max_done.sem, 1)
                    v = u - 2
                    if 0 <= v < U:
                        j, half = v // 2, v % 2
                        pv = ps[:, 4, 0:HB * (HD + 1)].rearrange("p (h d) -> p h d", h=HB)
                        dve.wait_ge(*pv_mm(c, v + 1))
                        dve.wait_ge(*o_done(c, v - 1))
                        dve.reciprocal(rec[:, v % 2], pv[:, :, HD]).then_inc(rec_done.sem, 1)
                        dve.wait_ge(*rec_done(c, v + 1))
                        if v == 0:
                            dve.wait_ge(*(y_done if wo is None else oT_mm)(c - 2))
                        dve.tensor_tensor(o[:, p, j, half * 256:half * 256 + 256].rearrange("p (h d) -> p h d", h=HB),
                                          pv[:, :, 0:HD], rec[:, v % 2].unsqueeze(2).to_broadcast([P, HB, HD]),
                                          ALU.mult).then_inc(o_done.sem, 1)
                    if wo is not None and u >= 5 and u % 2 == 1:
                        j = (u - 5) // 2
                        dve.wait_ge(*wo_mm(c, j + 1))
                        if j == 0:
                            dve.wait_ge(*stored(c - 2))
                        dve.tensor_tensor(y[:, p, j, :], ps[:, 6 + j % 2, :], f.x[:, p, j, :], ALU.add).then_inc(y_done.sem, 1)

            over_chunks(dve, NC, front, main)

        @block.scalar
        def _(act):
            for s in (f.xT_done, q_done, exp_done, pT_done) + ((oT_done,) if wo is not None else ()):
                s.start(act)
            act.wait_ge(consts_in, 16 * loads)
            act.wait_ge(zeroed, 2)
            if biased:
                act.activation(bias[:, 2, :], bias[:, 0, :], ACT.Copy, scale=scale).then_inc(bias_set, 1)
            for m in range(KD):
                act.wait_ge(kv_mm, m + 1)
                for h in range(4):
                    q = slice(h * HD, (h + 1) * HD)
                    dst = kblk[q, :, m, h * SK:(h + 1) * SK]
                    src = ps[q, m, 0:B * SK].rearrange("p (b s) -> p b s", b=B)
                    if biased:
                        i = act.activation(dst, src, ACT.Identity, bias=bias[q, 1, m:m + 1])
                    else:
                        i = act.activation(dst, src, ACT.Copy)
                i.then_inc(kv_set, 1)
            if biased:
                act.wait_ge(bias_set, 1)

            def main(c, p):
                act.wait_ge(*s_mm(c - 2))
                for m in range(KD):
                    act.wait_ge(*q_mm(c, m + 1))
                    if biased:
                        i = act.activation(qT[:, p, m, :], ps[:, 6 + m % 2, :], ACT.Identity, bias=bias[:, 2, m:m + 1], scale=scale)
                    else:
                        i = act.activation(qT[:, p, m, :], ps[:, 6 + m % 2, :], ACT.Copy, scale=scale)
                    i.then_inc(q_done.sem, 1)
                for u in range(U + 3):
                    if u < U:
                        act.wait_ge(*sub_done(c, u + 1))
                        act.activation(s_sb[:, u % 2], s_sb[:, u % 2], ACT.Exp).then_inc(exp_done.sem, 1)
                    v = u - 1
                    if 0 <= v < U:
                        act.wait_ge(*p_mm(c, v + 1))
                        act.wait_ge(*pv_mm(c, v - 1))
                        act.activation(pT[:, v % 2].rearrange("s (b h) t -> s b h t", b=2),
                                       ps[0:SK, 2:4, :].rearrange("s b (h t) -> s b h t", h=4),
                                       ACT.Copy).then_inc(pT_done.sem, 1)
                    if wo is not None and u >= 4 and u % 2 == 0:
                        j = (u - 4) // 2
                        act.wait_ge(*oT_mm(c, j + 1))
                        act.wait_ge(*wo_mm(c, j - 1))
                        act.activation(oT[:, j % 2], ps[:, 5, :].rearrange("p (k t) -> p k t", k=KD), ACT.Copy).then_inc(oT_done.sem, 1)

            over_chunks(act, NC, lambda c, p: f.keep(act, c, p, q_mm(c - 2), nb=1), main)

        @block.tensor
        def _(pe):
            for s in (f.tp_done, q_mm, s_mm, p_mm, pv_mm) + ((oT_mm, wo_mm) if wo is not None else ()):
                s.start(pe)
            pe.wait_ge(consts_in, 16 * loads)
            for m in range(KD):
                for k in range(KD):
                    i = pe.matmul(ps[:, m, 0:B * SK], wk_s[:, k, m * P:(m + 1) * P], ctxT[:, k, :], start=k == 0, stop=k == KD - 1)
                i.then_inc(kv_mm, 1)
            for b in range(B):
                for k in range(KD):
                    i = pe.matmul(ps[0:SK, 4 + b, :], ctxT[:, k, b * SK:(b + 1) * SK], wv_s[:, k, :], start=k == 0, stop=k == KD - 1)
                i.then_inc(kv_mm, 1)
            pe.wait_ge(kv_set, KD + B)

            def front(c, p):
                if wo is not None:
                    pe.wait_ge(*oT_done(c - 2))
                f.turn(pe, c, p, ident, nb=1)

            def main(c, p):
                b = c // CB
                pe.wait_ge(*f.xT_done(c))
                for m in range(KD):
                    if m >= 2:
                        pe.wait_ge(*q_done(c, m - 1))
                    elif wo is not None:
                        pe.wait_ge(*y_done(c - 1))
                    else:
                        pe.wait_ge(*q_done(c - 1))
                    for k in range(KD):
                        i = pe.matmul(ps[:, 6 + m % 2, :], wq_s[:, k, m * P:(m + 1) * P], f.xT[:, p, k, :], start=k == 0, stop=k == KD - 1)
                    i.then_inc(q_mm.sem, 1)
                pe.wait_ge(*q_done(c))
                for u in range(U + 4):
                    if u < U:
                        j, half = u // 2, u % 2
                        pe.wait_ge(*add_done(c, u))
                        for mm in range(2):
                            m = 2 * half + mm
                            i = pe.matmul(ps[:, mm, 0:W4], qT[:, p, m, j * P:(j + 1) * P], pick(kblk, b)[:, m, :], start=True, stop=True)
                        i.then_inc(s_mm.sem, 1)
                    v = u - 1
                    if 0 <= v < U:
                        pe.wait_ge(*exp_done(c, v + 1))
                        pe.wait_ge(*pT_done(c, v))
                        for h in range(HB):
                            i = pe.transpose(ps[0:SK, 2 + h // 4, (h % 4) * P:(h % 4 + 1) * P], s_sb[:, v % 2, h, :], ident[:, :])
                        i.then_inc(p_mm.sem, 1)
                    v = u - 2
                    if 0 <= v < U:
                        pe.wait_ge(*pT_done(c, v + 1))
                        pe.wait_ge(*o_done(c, v))
                        for h in range(HB):
                            i = pe.matmul(ps[:, 4, h * (HD + 1):(h + 1) * (HD + 1)], pT[:, v % 2, h, :],
                                          pick(v1, b)[:, (v % 2) * HB + h, :], start=True, stop=True)
                        i.then_inc(pv_mm.sem, 1)
                    if wo is not None and u >= 4 and u % 2 == 0 and (u - 4) // 2 < TJ:
                        j = (u - 4) // 2
                        pe.wait_ge(*o_done(c, 2 * j + 2))
                        if j:
                            pe.wait_ge(*oT_done(c, j))
                        elif not (isinstance(c, int) and c == NC - 1):
                            pe.wait_ge(*f.xT_done(c + 1))
                        for k in range(KD):
                            i = pe.transpose(ps[:, 5, k * P:(k + 1) * P], o[:, p, j, k * P:(k + 1) * P], ident[:, :])
                        i.then_inc(oT_mm.sem, 1)
                    if wo is not None and u >= 5 and u % 2 == 1 and (u - 5) // 2 < TJ:
                        j = (u - 5) // 2
                        pe.wait_ge(*oT_done(c, j + 1))
                        if j >= 2:
                            pe.wait_ge(*y_done(c, j - 1))
                        for k in range(KD):
                            i = pe.matmul(ps[:, 6 + j % 2, :], oT[:, j % 2, k, :], wo_s[:, k, :], start=k == 0, stop=k == KD - 1)
                        i.then_inc(wo_mm.sem, 1)

            over_chunks(pe, NC, front, main)


def stage_ffn(nc, tag, x_in, x_out, ident_d, qw, scT, la, lbT, bias, gamma, beta, first, add_to=None):
    R = la.shape[1]
    with Stage(nc, tag) as st:
        ps = st.banks()
        ident = st.sb("ident", [P, P])
        w = st.sb("w", [P, 2, KD, D])
        qi = st.sb("qi", [P, KD, D], I32)
        sc = st.sb("sc", [P, KD, D])
        la_s = st.sb("la", [R, 2, D])
        lb_s = st.sb("lb", [R, 2, D])
        b0 = st.sb("b0", [P, D])
        b1 = st.sb("b1", [P, D])
        gam = st.sb("gam", [P, D])
        bet = st.sb("bet", [P, D])
        y = st.sb("y", [P, TJ, D])
        gT = st.sb("gT", [P, 2, KD, P])
        hb = st.sb("hb", [P, TJ, D])
        r = st.sb("r", [P, TJ, D]) if add_to is not None else None
        out = st.sb("out", [P, TJ, D])
        bn = st.sb("bn2", [P, TJ, 6])
        mv = st.sb("mv2", [P, TJ, 2])
        rs = st.sb("rs2", [P, TJ])
        f = Front(st, ps, 6, x_in, norm=first)
        consts_in = st.sem("consts_in")
        q_in = st.sem("q_in")
        lora_mm = st.sem("lora_mm")
        deq_done = st.sem("deq_done")
        scaled = st.sem("scaled")
        w_done = st.sem("w_done")
        r_in = st.sem("r_in")
        y_mm = st.count("y_mm", TJ)
        y_done = st.count("y_done", TJ)
        bn_done = st.count("bn_done2", TJ)
        mv_done = st.count("mv_done2", TJ)
        var_done = st.count("var_done2", TJ)
        rs_done = st.count("rs_done2", TJ)
        z_done = st.count("z_done", TJ)
        gam_done = st.count("gam_done", TJ)
        bet_done = st.count("bet_done", TJ)
        gelu_done = st.count("gelu_done", TJ)
        gT_mm = st.count("gT_mm", TJ)
        gT_done = st.count("gT_done", TJ)
        hb_done = st.count("hb_done", 1)
        hr_done = st.count("hr_done", 1)
        o_mm = st.count("o_mm", TJ)
        o_done = st.count("o_done", TJ)
        stored = st.count("stored", 1, 16)
        NCONST = 7
        block = st.ctx.enter_context(nc.Block())
        row = lambda v, n: v.rearrange("(o n) -> o n", o=1).to_broadcast([P, n])

        @block.sync
        def _(sp):
            stored.start(sp)
            for i in range(2):
                if i:
                    sp.wait_ge(scaled, 1)
                sp.dma_start(qi[:, :, :], weight_view(qw[i])).then_inc(q_in, 16)
                for k in range(KD):
                    sp.dma_start(sc[:, k, :], scT[i][8 * k:8 * k + 8, :].unsqueeze(1).to_broadcast([8, 16, D])).then_inc(q_in, 16)
                if i == 0:
                    sp.dma_start(la_s[:, :, :], la.rearrange("i r d -> r i d")).then_inc(consts_in, 16)
                    sp.dma_start(lb_s[:, :, :], lbT.rearrange("i r d -> r i d")).then_inc(consts_in, 16)
                    sp.dma_start(ident[:, :], ident_d).then_inc(consts_in, 16)
                    for dst, v in ((b0, bias[0]), (b1, bias[1]), (gam, gamma), (bet, beta)):
                        sp.dma_start(dst[:, :], row(v, D)).then_inc(consts_in, 16)

            def front(c, p):
                if first:
                    sp.wait_ge(*f.xn_done(c - 2))
                else:
                    sp.wait_ge(*f.tp_done(c - 2))
                    st.plain(sp)
                    sp.wait_ge(*hb_done(c - 2))
                f.load(sp, c, p)

            def main(c, p):
                if add_to is not None:
                    sp.wait_ge(*hr_done(c - 1))
                    st.plain(sp)
                    sp.dma_start(r[:, :, :], chunk_rows(add_to, c)).then_inc(r_in, 16)
                sp.wait_ge(*o_done(c))
                st.plain(sp)
                sp.dma_start(chunk_rows(x_out, c), out[:, :, :]).then_inc(stored.sem, 16)

            over_chunks(sp, NC, front, main)
            sp.wait_ge(*stored(NC - 1))

        @block.gpsimd
        def _(pool):
            f.start_pool(pool)
            for s in (var_done, rs_done, gam_done, bet_done, hb_done, hr_done):
                s.start(pool)
            pool.wait_ge(consts_in, 16 * NCONST)
            pool.wait_ge(f.half_set, 1)

            def main(c, p):
                for j in range(TJ + 1):
                    if j < TJ:
                        pool.wait_ge(*mv_done(c, j + 1))
                        pool.wait_ge(*z_done(c - 1, j + 1))
                        st.plain(pool)
                        pool.tensor_scalar(rs[:, j:j + 1], mv[:, j, 1:2], EPS, None, ALU.add).then_inc(var_done.sem, 1)
                        pool.wait_ge(*var_done(c, j + 1))
                        pool.tensor_tensor(rs[:, j:j + 1], rs[:, j:j + 1], f.half[:, 0:1], ALU.pow).then_inc(rs_done.sem, 1)
                    if j:
                        pool.wait_ge(*z_done(c, j))
                        pool.tensor_tensor(y[:, j - 1, :], y[:, j - 1, :], gam[:, :], ALU.mult).then_inc(gam_done.sem, 1)
                        pool.wait_ge(*gam_done(c, j))
                        pool.tensor_tensor(y[:, j - 1, :], y[:, j - 1, :], bet[:, :], ALU.add).then_inc(bet_done.sem, 1)
                if first:
                    pool.wait_ge(*f.xn_done(c))
                else:
                    pool.wait_ge(*f.x_ready(c, p))
                pool.wait_ge(*o_done(c - 1))
                pool.tensor_tensor(hb[:, :, :], f.xn[:, p], b1[:, :].unsqueeze(1).to_broadcast([P, TJ, D]), ALU.add).then_inc(hb_done.sem, 1)
                if add_to is not None:
                    pool.wait_ge(r_in, c * 16 + 16)
                    pool.wait_ge(*hb_done(c))
                    pool.tensor_tensor(hb[:, :, :], hb[:, :, :], r[:, :, :], ALU.add).then_inc(hr_done.sem, 1)

            over_chunks(pool, NC, (lambda c, p: f.rstd(pool, c, p)) if first else (lambda c, p: None), main)

        @block.vector
        def _(dve):
            f.start_dve(dve)
            for s in (y_done, bn_done, mv_done, z_done, o_done):
                s.start(dve)
            dve.wait_ge(consts_in, 16 * NCONST)
            for i in range(2):
                dve.wait_ge(q_in, 16 * (1 + KD) * (i + 1))
                dve.tensor_scalar(w[:, i], qi[:, :, :], 1.0 / 7.5, -1.0, ALU.mult, ALU.add).then_inc(deq_done, 1)
                dve.wait_ge(deq_done, i + 1)
                dve.tensor_tensor(w[:, i], w[:, i], sc[:, :, :], ALU.mult).then_inc(scaled, 1)
                dve.wait_ge(scaled, i + 1)
                dve.wait_ge(lora_mm, i + 1)
                dve.tensor_tensor(w[:, i], w[:, i], ps[:, 4 * i:4 * i + 4, :], ALU.add).then_inc(w_done, 1)

            def front(c, p):
                if first:
                    f.stats(dve, c, p)
                    f.normalise(dve, c, p, extra=[hb_done(c - 2)])

            def main(c, p):
                for j in range(TJ + 1):
                    if j < TJ:
                        dve.wait_ge(*y_mm(c, j + 1))
                        dve.wait_ge(*gT_mm(c - 1, j + 1))
                        dve.tensor_tensor(y[:, j, :], ps[:, j % 2, :], b0[:, :], ALU.add).then_inc(y_done.sem, 1)
                        dve.wait_ge(*y_done(c, j + 1))
                        dve.bn_stats(bn[:, j, :], y[:, j, :]).then_inc(bn_done.sem, 1)
                        dve.wait_ge(*bn_done(c, j + 1))
                        dve.wait_ge(*var_done(c - 1, j + 1))
                        st.plain(dve)
                        dve.bn_aggr(mv[:, j, :], bn[:, j, :]).then_inc(mv_done.sem, 1)
                    if j:
                        dve.wait_ge(*rs_done(c, j))
                        dve.tensor_scalar(y[:, j - 1, :], y[:, j - 1, :], mv[:, j - 1, 0:1], rs[:, j - 1:j],
                                          ALU.subtract, ALU.mult).then_inc(z_done.sem, 1)
                dve.wait_ge(*(hb_done if add_to is None else hr_done)(c))
                dve.wait_ge(*stored(c - 1))
                for j in range(TJ):
                    dve.wait_ge(*o_mm(c, j + 1))
                    dve.tensor_tensor(out[:, j, :], ps[:, 4 + j % 2, :], hb[:, j, :], ALU.add).then_inc(o_done.sem, 1)

            over_chunks(dve, NC, front, main)

        @block.scalar
        def _(act):
            for s in (f.xT_done, gelu_done, gT_done):
                s.start(act)

            def main(c, p):
                for j in range(TJ):
                    act.wait_ge(*bet_done(c, j + 1))
                    act.activation(y[:, j, :], y[:, j, :], ACT.Gelu).then_inc(gelu_done.sem, 1)
                    if j:
                        keep(c, j - 1)
                keep(c, TJ - 1)

            def keep(c, j):
                act.wait_ge(*gT_mm(c, j + 1))
                act.wait_ge(*o_mm(c, j - 1))
                act.activation(gT[:, j % 2], ps[:, 2 + j % 2, :].rearrange("p (k t) -> p k t", k=KD), ACT.Copy).then_inc(gT_done.sem, 1)

            over_chunks(act, NC, lambda c, p: f.keep(act, c, p, y_mm(c - 2)), main)

        @block.tensor
        def _(pe):
            for s in (f.tp_done, y_mm, gT_mm, o_mm):
                s.start(pe)
            pe.wait_ge(consts_in, 16 * NCONST)
            for i in range(2):
                for k in range(KD):
                    m = pe.matmul(ps[:, 4 * i + k, :], la_s[:, i, k * P:(k + 1) * P], lb_s[:, i, :], start=True, stop=True)
                m.then_inc(lora_mm, 1)
            pe.wait_ge(w_done, 2)

            def main(c, p):
                pe.wait_ge(*f.xT_done(c))
                for j in range(TJ):
                    pe.wait_ge(*y_done(c, j - 1))
                    for k in range(KD):
                        i = pe.matmul(ps[:, j % 2, :], f.xT[:, p, k, j * P:(j + 1) * P], w[:, 0, k, :], start=k == 0, stop=k == KD - 1)
                    i.then_inc(y_mm.sem, 1)

                def turn(j):
                    pe.wait_ge(*gelu_done(c, j + 1))
                    pe.wait_ge(*gT_done(c, j - 1))
                    for k in range(KD):
                        i = pe.transpose(ps[:, 2 + j % 2, k * P:(k + 1) * P], y[:, j, k * P:(k + 1) * P], ident[:, :])
                    i.then_inc(gT_mm.sem, 1)

                turn(0)
                for j in range(TJ):
                    if j + 1 < TJ:
                        turn(j + 1)
                    pe.wait_ge(*gT_done(c, j + 1))
                    pe.wait_ge(*o_done(c, j - 1))
                    for k in range(KD):
                        i = pe.matmul(ps[:, 4 + j % 2, :], gT[:, j % 2, k, :], w[:, 1, k, :], start=k == 0, stop=k == KD - 1)
                    i.then_inc(o_mm.sem, 1)

            over_chunks(pe, NC, lambda c, p: f.turn(pe, c, p, ident), main)


def stage_project(nc, tag, x_in, outs, ident_d, ws, biases):
    M = len(ws)
    with Stage(nc, tag) as st:
        ps = st.banks()
        ident = st.sb("ident", [P, P])
        w = st.sb("w", [P, M, KD, D])
        bias = st.sb("bias", [P, M, D])
        y = st.sb("y", [P, 2, M, TJ, D])
        f = Front(st, ps, 6, x_in)
        consts_in = st.sem("consts_in")
        y_mm = st.count("y_mm", M * TJ)
        y_done = st.count("y_done", M * TJ)
        stored = st.count("stored", M, 16)
        block = st.ctx.enter_context(nc.Block())

        @block.sync
        def _(sp):
            stored.start(sp)
            for i in range(M):
                sp.dma_start(w[:, i], weight_view(ws[i])).then_inc(consts_in, 16)
                sp.dma_start(bias[:, i], biases[i].rearrange("(o n) -> o n", o=1).to_broadcast([P, D])).then_inc(consts_in, 16)
            sp.dma_start(ident[:, :], ident_d).then_inc(consts_in, 16)

            def front(c, p):
                sp.wait_ge(*f.xn_done(c - 2))
                f.load(sp, c, p)

            def main(c, p):
                for i in range(M):
                    sp.wait_ge(*y_done(c, (i + 1) * TJ))
                    st.plain(sp)
                    sp.dma_start(chunk_rows(outs[i], c), y[:, p, i]).then_inc(stored.sem, 16)

            over_chunks(sp, NC, front, main)
            sp.wait_ge(*stored(NC - 1))

        @block.gpsimd
        def _(pool):
            f.start_pool(pool)
            over_chunks(pool, NC, lambda c, p: f.rstd(pool, c, p), None)

        @block.vector
        def _(dve):
            f.start_dve(dve)
            y_done.start(dve)
            dve.wait_ge(consts_in, 16 * (2 * M + 1))

            def front(c, p):
                f.stats(dve, c, p)
                f.normalise(dve, c, p)

            def main(c, p):
                dve.wait_ge(*stored(c - 2))
                for u in range(M * TJ):
                    dve.wait_ge(*y_mm(c, u + 1))
                    dve.tensor_tensor(y[:, p, u // TJ, u % TJ, :], ps[:, u % 4, :], bias[:, u // TJ, :], ALU.add).then_inc(y_done.sem, 1)

            over_chunks(dve, NC, front, main)

        @block.scalar
        def _(act):
            f.xT_done.start(act)
            over_chunks(act, NC, lambda c, p: f.keep(act, c, p, y_mm(c - 2)), None)

        @block.tensor
        def _(pe):
            f.tp_done.start(pe)
            y_mm.start(pe)
            pe.wait_ge(consts_in, 16 * (2 * M + 1))

            def main(c, p):
                pe.wait_ge(*f.xT_done(c))
                for u in range(M * TJ):
                    pe.wait_ge(*y_done(c, u - 3))
                    for k in range(KD):
                        i = pe.matmul(ps[:, u % 4, :], f.xT[:, p, k, (u % TJ) * P:(u % TJ + 1) * P], w[:, u // TJ, k, :],
                                      start=k == 0, stop=k == KD - 1)
                    i.then_inc(y_mm.sem, 1)

            over_chunks(pe, NC, lambda c, p: f.turn(pe, c, p, ident), main)


SEG = 1024
QUAD = [-2.0 * float(np.cos((2 * g + 1) * np.pi / 8)) for g in range(4)]


def transform_tables():
    n = np.arange(512)
    fwd, inv = [], []
    for g in range(4):
        theta = 2 * np.pi * (g + 8 * np.arange(256) + 0.5) / 2048
        c, s = np.cos(np.outer(n, theta)), np.sin(np.outer(n, theta))
        fwd.append(np.concatenate([c, -s], 1))
        inv.append(np.concatenate([c, -s], 1).T / 1024)
    return np.stack(fwd).astype(np.float32), np.stack(inv).astype(np.float32)


def stage_conv(nc, k_in, v_in, y_out, kkT, ssT, kd, dd, fwd_d, inv_d):
    CW = 256
    NH = D // CW
    TS = SEG // P
    ORDER = [0, 3, 1, 2]
    SIGN = [1.0, -1.0, 1.0, -1.0]
    STEPS = 16
    with Stage(nc, "cv") as st:
        ps = st.banks()
        fwd = st.sb("fwd", [P, 4, 4, 512])
        inv = st.sb("inv", [P, 4, 4, 512])
        hat = st.sb("hat", [P, 2, 4, 4, CW])
        prev = st.sb("prev", [P, 4, 4, CW])
        kb = st.sb("kb", [P, 2, TS, CW])
        vb = st.sb("vb", [P, 2, TS, CW])
        acc = st.sb("acc", [P, 2, TS, CW])
        gain = st.sb("gain", [P, 2, CW])
        e = st.sb("e", [P, 2, CW])
        ff = st.sb("ff", [P, 2, CW])
        r = st.sb("r", [P, 2, 4, CW])
        zb = st.sb("z", [P, 2, 4, CW])
        yb = st.sb("y", [P, 2, 4, CW])
        q = st.sb("q", [P, 4, CW])
        x = st.sb("x", [P, 4, CW])
        tab_in = st.sem("tab_in")
        gain_in = st.sem("gain_in")
        k_ld = [st.sem("k_ld0"), st.sem("k_ld1")]
        v_ld = [st.sem("v_ld0"), st.sem("v_ld1")]
        ef_done = st.count("ef_done", 3)
        res_done = st.count("res_done", 1)
        r0_done = st.sem("r0_done")
        fwd_mm = st.count("fwd_mm", 1)
        kept = st.count("kept", 1)
        z_done = st.count("z_done", 1, lead=3)
        q_done = st.count("q_done", 1)
        x_done = st.count("x_done", 1)
        yr_done = st.count("yr_done", 1)
        y_done = st.count("y_done", 1)
        inv_mm = st.count("inv_mm", 1)
        part = st.count("part", 4)
        last = st.count("last", 1)
        gained = st.count("gained", 1)
        summed = st.count("summed", 1)
        post = st.count("post", 4)
        y_st = [st.count("y_st0", 1, 16), st.count("y_st1", 1, 16)]
        block = st.ctx.enter_context(nc.Block())

        def seg_view(t, b, s, hh):
            v = t.rearrange("(b s j p) (h d) -> p b s h j d", b=B, s=2, p=P, h=NH)
            return v[:, bass.ds(b, 1), s, bass.ds(hh, 1)].rearrange("p b h j d -> p (b h j) d")

        def kernel_view(t, hh):
            return t.rearrange("(j p) (h d) -> p h j d", p=P, h=NH)[:, bass.ds(hh, 1)].rearrange("p h j d -> p (h j) d")

        batch = lambda hh, b: hh * B + b
        fstep = lambda hh, b, n: hh * (8 + B * STEPS) + (b * STEPS + 8 + n) if b is not None else hh * (8 + B * STEPS) + n
        tstep = lambda hh, b, n: batch(hh, b) * STEPS + n
        kstep = lambda hh, b, n: hh * (8 + B * 8) + (b * 8 + 8 + (n // 8) * 4 + n % 4) if b is not None else hh * (8 + B * 8) + n
        zstep = lambda hh, b, n: batch(hh, b) * 8 + ((n // 8) * 4 + n % 4)
        item = lambda hh, b, m: hh * (2 + B * 4) + (b * 4 + 2 + m) if b is not None else hh * (2 + B * 4) + m

        @block.sync
        def _(sp):
            for dst, src in ((fwd, fwd_d), (inv, inv_d)):
                for g in range(4):
                    sp.dma_start(dst[:, g], weight_view(src[g])).then_inc(tab_in, 16)
            with sp.Fori(0, NH) as hh:
                for i, t in enumerate((kkT, ssT)):
                    sp.wait_ge(*post(batch(hh, -1)))
                    st.plain(sp)
                    sp.dma_start(vb[:, i], kernel_view(t, hh)).then_inc(v_ld[i], 16)
                for i, t in enumerate((kd, dd)):
                    sp.dma_start(gain[:, i], t.rearrange("(h o d) -> h o d", h=NH, o=1)[bass.ds(hh, 1)]
                                 .rearrange("h o d -> (h o) d").to_broadcast([P, CW])).then_inc(gain_in, 16)
                with sp.Fori(0, B) as b:
                    for s in range(2):
                        sp.wait_ge(*post(batch(hh, b) - 1, 3 + s))
                        st.plain(sp)
                        sp.dma_start(kb[:, s], seg_view(k_in, b, s, hh)).then_inc(k_ld[s], 16)
                    for s in range(2):
                        sp.wait_ge(*post(batch(hh, b) - 1, 1 + s))
                        st.plain(sp)
                        sp.wait_ge(*res_done(fstep(hh, None, 4 * s + 3)))
                        st.plain(sp)
                        sp.dma_start(vb[:, s], seg_view(v_in, b, s, hh)).then_inc(v_ld[s], 16)

        @block.scalar
        def _(act):
            kept.start(act)
            for c in y_st:
                c.start(act)

            def keep(dst, f, n):
                act.wait_ge(*fwd_mm(f))
                act.activation(dst, ps[:, 2 * (n % 2):2 * (n % 2) + 2, :].rearrange("p b (m d) -> p (b m) d", m=2),
                               ACT.Copy).then_inc(kept.sem, 1)

            with act.Fori(0, NH) as hh:
                act.wait_ge(*y_done(tstep(hh, 0, -1)))
                for n in range(8):
                    keep(hat[:, n // 4, ORDER[n % 4]], fstep(hh, None, n), n)
                with act.Fori(0, B) as b:
                    for n in range(STEPS):
                        if (n // 4) % 2 == 0:
                            act.wait_ge(*z_done(zstep(hh, b, n) - 4))
                            act.wait_ge(*y_done(tstep(hh, b, n) - 1))
                            keep(prev[:, ORDER[n % 4]], fstep(hh, b, n), n)
                    for s in range(2):
                        act.wait_ge(*post(batch(hh, b), 3 + s))
                        act.dma_start(seg_view(y_out, b, s, hh), acc[:, s]).then_inc(y_st[s].sem, 16)
            for s in range(2):
                act.wait_ge(*y_st[s](NH * B - 1))

        @block.tensor
        def _(pe):
            for c in (fwd_mm, inv_mm):
                c.start(pe)
            pe.wait_ge(tab_in, 16 * 8)

            def forward(f, n, free):
                pe.wait_ge(*res_done(f))
                for w in free:
                    pe.wait_ge(*w)
                for m in range(4):
                    for k in range(4):
                        i = pe.matmul(ps[:, 2 * (n % 2) + m // 2, (m % 2) * CW:(m % 2 + 1) * CW],
                                      fwd[:, ORDER[n % 4], k, m * P:(m + 1) * P], r[:, n % 2, k, :], start=k == 0, stop=k == 3)
                i.then_inc(fwd_mm.sem, 1)

            def inverse(t, n):
                pe.wait_ge(*y_done(t))
                pe.wait_ge(*part(t - 2))
                for m in range(4):
                    for k in range(4):
                        i = pe.matmul(ps[:, 4 + 2 * (n % 2) + m // 2, (m % 2) * CW:(m % 2 + 1) * CW],
                                      inv[:, ORDER[n % 4], k, m * P:(m + 1) * P], yb[:, n % 2, k, :], start=k == 0, stop=k == 3)
                i.then_inc(inv_mm.sem, 1)

            def free_of(hh, b, n):
                if n < 2:
                    return [kept(kstep(hh, b, 0) - 1), z_done(zstep(hh, b, 0) - 1)]
                n -= 2
                return [kept(kstep(hh, b, n))] if (n // 4) % 2 == 0 else [z_done(zstep(hh, b, n))]

            with pe.Fori(0, NH) as hh:
                for n in range(8):
                    forward(fstep(hh, None, n), n, [kept(kstep(hh, None, n - 2)) if n >= 2 else z_done(zstep(hh, 0, 0) - 1)])
                with pe.Fori(0, B) as b:
                    forward(fstep(hh, b, 0), 0, free_of(hh, b, 0))
                    for n in range(STEPS):
                        if n + 1 < STEPS:
                            forward(fstep(hh, b, n + 1), n + 1, free_of(hh, b, n + 1))
                        inverse(tstep(hh, b, n), n)

        @block.vector
        def _(dve):
            for c in (ef_done, res_done, z_done, q_done, yr_done, y_done, part, last):
                c.start(dve)

            def residue(src, ready, i, f, n):
                gi = n % 4
                a = QUAD[ORDER[gi]]
                xq = [src[:, 2 * m:2 * m + 2, :] for m in range(4)]
                if gi % 2 == 0:
                    dve.wait_ge(*res_done(f - 1))
                if gi == 0:
                    for w in ready:
                        dve.wait_ge(*w)
                    dve.tensor_tensor(e[:, :, :], xq[0], xq[2], ALU.subtract).then_inc(ef_done.sem, 1)
                if gi % 2 == 0:
                    dve.scalar_tensor_tensor(ff[:, :, :], xq[3], a * a - 1.0, xq[1], ALU.mult, ALU.add).then_inc(ef_done.sem, 1)
                dve.wait_ge(*ef_done(i, 2 + gi // 2))
                dve.wait_ge(*fwd_mm(f - 2))
                dve.scalar_tensor_tensor(r[:, n % 2, 0:2], xq[3], a, e[:, :, :], ALU.mult, ALU.add).then_inc(r0_done, 1)
                dve.scalar_tensor_tensor(r[:, n % 2, 2:4], xq[2], -a, ff[:, :, :], ALU.mult, ALU.add).then_inc(res_done.sem, 1)

            def spectrum(hh, b, n):
                g, conv, seg = ORDER[n % 4], n // 8, (n // 4) % 2
                t = tstep(hh, b, n)
                if seg == 0:
                    z = prev[:, g]
                    dve.wait_ge(*kept(kstep(hh, b, n)))
                else:
                    z = zb[:, n % 2]
                    d = ps[:, 2 * (n % 2):2 * (n % 2) + 2, :].rearrange("p b (m d) -> p b m d", m=2)
                    dve.wait_ge(*fwd_mm(fstep(hh, b, n)))
                    dve.wait_ge(*x_done(t - 2))
                    re = (ALU.subtract, ALU.add) if SIGN[g] > 0 else (ALU.add, ALU.subtract)
                    dve.tensor_tensor(z[:, 0:2], d[:, 0], prev[:, g, 2:4], re[0]).then_inc(r0_done, 1)
                    dve.tensor_tensor(z[:, 2:4], d[:, 1], prev[:, g, 0:2], re[1]).then_inc(z_done.sem, 1)
                    dve.wait_ge(*z_done(zstep(hh, b, n)))
                dve.wait_ge(*y_done(t - 1))
                dve.tensor_tensor(q[:, :, :], z, hat[:, conv, g], ALU.mult).then_inc(q_done.sem, 1)
                dve.wait_ge(*q_done(t))
                dve.wait_ge(*x_done(t))
                dve.wait_ge(*inv_mm(t - 2))
                dve.tensor_tensor(yb[:, n % 2, 0:2], q[:, 0:2], q[:, 2:4], ALU.subtract).then_inc(yr_done.sem, 1)
                dve.tensor_tensor(yb[:, n % 2, 2:4], x[:, 0:2], x[:, 2:4], ALU.add).then_inc(y_done.sem, 1)

            def sums(hh, b, n):
                gi, it = n % 4, n // 4
                a = QUAD[ORDER[gi]]
                t = tstep(hh, b, n)
                d = ps[:, 4 + 2 * (n % 2):6 + 2 * (n % 2), :].rearrange("p b (m d) -> p (b m) d", m=2)
                A, Bk, C = acc[:, it % 2, 0:4], acc[:, it % 2, 4:6], acc[:, it % 2, 6:8]
                dve.wait_ge(*inv_mm(t))
                if gi == 0:
                    if it >= 2:
                        dve.wait_ge(*post(batch(hh, b), it - 1))
                    else:
                        dve.wait_ge(*y_st[it](batch(hh, b) - 1))
                    dve.tensor_copy(A, d).then_inc(part.sem, 1)
                    dve.tensor_scalar(Bk, d[:, 2:4], -a, None, ALU.mult).then_inc(part.sem, 1)
                    dve.tensor_scalar(C, d[:, 0:2], a, None, ALU.mult).then_inc(part.sem, 1)
                else:
                    dve.wait_ge(*part(t - 1))
                    dve.tensor_tensor(A, d, A, ALU.add).then_inc(part.sem, 1)
                    dve.scalar_tensor_tensor(Bk, d[:, 2:4], -a, Bk, ALU.mult, ALU.add).then_inc(part.sem, 1)
                    dve.scalar_tensor_tensor(C, d[:, 0:2], a, C, ALU.mult, ALU.add).then_inc(part.sem, 1)
                dve.wait_ge(*part(t, 3))
                dve.scalar_tensor_tensor(C, d[:, 2:4], a * a - 1.0, C, ALU.mult, ALU.add).then_inc(part.sem, 1)
                if gi == 3:
                    dve.wait_ge(*part(t))
                    dve.tensor_tensor(Bk, Bk, acc[:, it % 2, 0:2], ALU.subtract).then_inc(last.sem, 1)

            with dve.Fori(0, NH) as hh:
                for n in range(8):
                    residue(vb[:, n // 4], [(v_ld[n // 4], hh * 48 + 16)], item(hh, None, n // 4), fstep(hh, None, n), n)
                with dve.Fori(0, B) as b:
                    def res(n):
                        m = n // 4
                        ready = [(k_ld[m], batch(hh, b) * 16 + 16)] if m < 2 else [post(batch(hh, b), m - 1)]
                        residue(kb[:, m % 2], ready, item(hh, b, m), fstep(hh, b, n), n)

                    res(0)
                    res(1)
                    spectrum(hh, b, 0)
                    for n in range(STEPS):
                        if n + 2 < STEPS:
                            res(n + 2)
                        if n + 1 < STEPS:
                            spectrum(hh, b, n + 1)
                        sums(hh, b, n)

        @block.gpsimd
        def _(pool):
            for c in (x_done, gained, summed, post):
                c.start(pool)
            xr_done = st.sem("xr_done")

            def cross(hh, b, n):
                g, conv, seg = ORDER[n % 4], n // 8, (n // 4) % 2
                t = tstep(hh, b, n)
                if seg == 0:
                    z = prev[:, g]
                    pool.wait_ge(*kept(kstep(hh, b, n)))
                else:
                    z = zb[:, n % 2]
                    pool.wait_ge(*z_done(zstep(hh, b, n)))
                pool.wait_ge(*y_done(t - 1))
                pool.tensor_tensor(x[:, 0:2], z[:, 0:2], hat[:, conv, g, 2:4], ALU.mult).then_inc(xr_done, 1)
                pool.tensor_tensor(x[:, 2:4], z[:, 2:4], hat[:, conv, g, 0:2], ALU.mult).then_inc(x_done.sem, 1)

            with pool.Fori(0, NH) as hh:
                pool.wait_ge(gain_in, hh * 32 + 32)
                st.plain(pool)
                with pool.Fori(0, B) as b:
                    for n in range(STEPS + 1):
                        if n < STEPS:
                            cross(hh, b, n)
                        if n % 4 == 0 and n:
                            m = n // 4 - 1
                            s = m % 2
                            nb = batch(hh, b)
                            pool.wait_ge(*last(nb * 4 + m))
                            kd_b = gain[:, m // 2].unsqueeze(1).to_broadcast([P, TS, CW])
                            pool.tensor_tensor(kb[:, s], kb[:, s], kd_b, ALU.mult).then_inc(gained.sem, 1)
                            pool.wait_ge(*gained(nb * 4 + m))
                            if m < 2:
                                pool.tensor_tensor(kb[:, s], kb[:, s], acc[:, s], ALU.add).then_inc(summed.sem, 1)
                                pool.wait_ge(*summed(nb * 2 + m))
                                pool.wait_ge(v_ld[s], nb * 16 + (hh * 16 + 32))
                                pool.tensor_tensor(kb[:, s], kb[:, s], vb[:, s], ALU.mult).then_inc(post.sem, 1)
                            else:
                                pool.tensor_tensor(acc[:, s], acc[:, s], kb[:, s], ALU.add).then_inc(post.sem, 1)


def stage_gated_out(nc, tag, x_in, y_in, q_in, x_out, ident_d, wo, bo):
    with Stage(nc, tag) as st:
        ps = st.banks()
        ident = st.sb("ident", [P, P])
        w = st.sb("w", [P, KD, D])
        bias = st.sb("bias", [P, D])
        qb = st.sb("q", [P, 2, TJ, D])
        xr = st.sb("xr", [P, 2, TJ, D])
        xb = st.sb("xb", [P, 2, TJ, D])
        out = st.sb("out", [P, 2, TJ, D])
        f = Front(st, ps, 6, y_in)
        consts_in = st.sem("consts_in")
        q_ld = [st.sem("q_ld0"), st.sem("q_ld1")]
        x_ld = [st.sem("x_ld0"), st.sem("x_ld1")]
        xb_done = st.count("xb_done", 1)
        o_mm = st.count("o_mm", TJ)
        o_done = st.count("o_done", TJ)
        stored = st.count("stored", 1, 16)
        block = st.ctx.enter_context(nc.Block())

        def landed(sem, c, p):
            return sem[p], 16 * (c // 2 + 1) if isinstance(c, int) else (c - p) * 8 + 16

        @block.sync
        def _(sp):
            stored.start(sp)
            sp.dma_start(w[:, :, :], weight_view(wo)).then_inc(consts_in, 16)
            sp.dma_start(bias[:, :], bo.rearrange("(o n) -> o n", o=1).to_broadcast([P, D])).then_inc(consts_in, 16)
            sp.dma_start(ident[:, :], ident_d).then_inc(consts_in, 16)

            def front(c, p):
                sp.wait_ge(*f.xn_done(c - 2))
                f.load(sp, c, p)
                sp.dma_start(qb[:, p], chunk_rows(q_in, c)).then_inc(q_ld[p], 16)
                sp.wait_ge(*xb_done(c - 2))
                st.plain(sp)
                sp.dma_start(xr[:, p], chunk_rows(x_in, c)).then_inc(x_ld[p], 16)

            def main(c, p):
                sp.wait_ge(*o_done(c))
                st.plain(sp)
                sp.dma_start(chunk_rows(x_out, c), out[:, p]).then_inc(stored.sem, 16)

            over_chunks(sp, NC, front, main)
            sp.wait_ge(*stored(NC - 1))

        @block.gpsimd
        def _(pool):
            xb_done.start(pool)
            pool.wait_ge(consts_in, 48)

            def main(c, p):
                pool.wait_ge(*landed(x_ld, c, p))
                pool.wait_ge(*o_done(c - 2))
                pool.tensor_tensor(xb[:, p], xr[:, p], bias[:, :].unsqueeze(1).to_broadcast([P, TJ, D]), ALU.add).then_inc(xb_done.sem, 1)

            over_chunks(pool, NC, None, main)

        @block.vector
        def _(dve):
            f.xn_done.start(dve)
            o_done.start(dve)

            def front(c, p):
                dve.wait_ge(*f.x_ready(c, p))
                dve.wait_ge(*landed(q_ld, c, p))
                dve.wait_ge(*f.tp_done(c - 2))
                for j in range(TJ):
                    dve.tensor_tensor(f.xn[:, p, j, :], f.x[:, p, j, :], qb[:, p, j, :], ALU.mult).then_inc(f.xn_done.sem, 1)

            def main(c, p):
                dve.wait_ge(*xb_done(c))
                dve.wait_ge(*stored(c - 2))
                for j in range(TJ):
                    dve.wait_ge(*o_mm(c, j + 1))
                    dve.tensor_tensor(out[:, p, j, :], ps[:, j % 2, :], xb[:, p, j, :], ALU.add).then_inc(o_done.sem, 1)

            over_chunks(dve, NC, front, main)

        @block.scalar
        def _(act):
            f.xT_done.start(act)
            over_chunks(act, NC, lambda c, p: f.keep(act, c, p, o_mm(c - 2)), None)

        @block.tensor
        def _(pe):
            f.tp_done.start(pe)
            o_mm.start(pe)
            pe.wait_ge(consts_in, 48)

            def main(c, p):
                pe.wait_ge(*f.xT_done(c))
                for j in range(TJ):
                    pe.wait_ge(*o_done(c, j - 1))
                    for k in range(KD):
                        i = pe.matmul(ps[:, j % 2, :], f.xT[:, p, k, j * P:(j + 1) * P], w[:, k, :], start=k == 0, stop=k == KD - 1)
                    i.then_inc(o_mm.sem, 1)

            over_chunks(pe, NC, lambda c, p: f.turn(pe, c, p, ident), main)


NE, FF = 64, 1024
NTL = N // P
SLOT_TILES = 2 * N // P + NE


def stage_route(nc, tag, x_in, xn_out, ident_d, gate, table, route_d, weight_d, expert_d, rows_d, consts):
    E3 = [P, NTL, NE]
    before_d, iota_d, steps_d, upto_d, tiles_d, token_d = consts
    with Stage(nc, tag) as st:
        ps = st.banks()
        ident = st.sb("ident", [P, P])
        gate_s = st.sb("gate", [P, KD, NE])
        f = Front(st, ps, 6, x_in)
        lg = st.sb("lg", E3)
        consts_in = st.sem("consts_in")
        l_mm = st.count("l_mm", TJ)
        l_done = st.count("l_done", TJ)
        stored = st.count("stored", 1, 16)

        before = st.sb("before", [P, P])
        ones = st.sb("ones", [P, P])
        iota = st.sb("iota", [P, NE])
        steps = st.sb("steps", [P, NTL])
        upto = st.sb("upto", [P, NE, NE])
        tiles = st.sb("tiles", [1, SLOT_TILES])
        token = st.sb("token", [P, NTL])
        t1 = st.sb("t1", [P, NE, NE])
        oh = st.sb("oh", [P, 2, NTL, NE])
        m = st.sb("m", [P, 2, NTL])
        ix = st.sb("ix", [P, NTL])
        dd = st.sb("dd", [P, NTL])
        ex = st.sb("ex", [P, NTL])
        den = st.sb("den", [P, NTL])
        wt = st.sb("wt", [P, 2, NTL])
        cum = st.sb("cum", [P, NTL + 1, NE])
        nt = st.sb("nt", [P, NE])
        end = st.sb("end", [P, NE])
        first = st.sb("first", [P, NE])
        slot_f = st.sb("slot_f", [P, 2, NTL])
        slot = st.sb("slot", [P, 2, NTL], U32)
        own_f = st.sb("own_f", [1, SLOT_TILES + 1])
        own = st.sb("own", [1, SLOT_TILES + 1], I32)
        zero = st.sb("zero", [P, D])
        cleared = st.sem("cleared")
        one_set = st.sem("one_set")
        step_done = st.sem("step_done")
        exp_done = st.sem("exp_done")
        rank_mm = st.sem("rank_mm")
        table_clear = st.sem("table_clear")
        scattered = st.sem("scattered")
        route_st = st.sem("route_st")
        STEPS_END = 38 + NTL
        block = st.ctx.enter_context(nc.Block())

        @block.sync
        def _(sp):
            stored.start(sp)
            sp.dma_start(gate_s[:, :, :], weight_view(gate)).then_inc(consts_in, 16)
            for dst, src in ((ident, ident_d), (before, before_d), (token, token_d), (tiles, tiles_d)):
                sp.dma_start(dst[:, :], src).then_inc(consts_in, 16)
            for dst, src in ((iota, iota_d), (steps, steps_d)):
                sp.dma_start(dst[:, :], src.to_broadcast([P, src.shape[1]])).then_inc(consts_in, 16)
            sp.dma_start(upto[:, :, :].rearrange("p a b -> p (a b)"), upto_d.to_broadcast([P, NE * NE])).then_inc(consts_in, 16)

            def front(c, p):
                sp.wait_ge(*f.xn_done(c - 2))
                f.load(sp, c, p)

            def main(c, p):
                sp.wait_ge(*f.xn_done(c))
                st.plain(sp)
                sp.dma_start(chunk_rows(xn_out, c), f.xn[:, p]).then_inc(stored.sem, 16)

            over_chunks(sp, NC, front, main)
            sp.wait_ge(one_set, 2)
            spare = SLOT_TILES - 2 * N // P
            sp.dma_start(rows_d[2 * N:, :].rearrange("(p a) d -> p a d", p=P),
                         zero[:, :].unsqueeze(1).to_broadcast([P, spare, D])).then_inc(cleared, 16)
            sp.dma_start(table.rearrange("(p t) o -> p (t o)", p=P), zero[:, 0:SLOT_TILES]).then_inc(table_clear, 16)
            sp.wait_ge(step_done, STEPS_END)
            sp.dma_start(route_d, slot[:, :, :]).then_inc(route_st, 16)
            sp.dma_start(weight_d, wt[:, :, :]).then_inc(route_st, 16)
            sp.dma_start(expert_d, own[:, :]).then_inc(route_st, 16)
            sp.wait_ge(route_st, 48)
            sp.wait_ge(cleared, 16)
            sp.wait_ge(*stored(NC - 1))

        @block.gpsimd
        def _(pool):
            f.start_pool(pool)
            pool.memset(ones[:, :], 1.0).then_inc(one_set, 1)
            pool.memset(zero[:, :], 0.0).then_inc(one_set, 1)
            over_chunks(pool, NC, lambda c, p: f.rstd(pool, c, p), None)
            pool.wait_ge(step_done, STEPS_END)
            pool.wait_ge(table_clear, 16)
            for i in range(2):
                for t in range(NTL):
                    pool.indirect_dma_start(out=table, out_offset=bass.IndirectOffsetOnAxis(ap=slot[:, i, t:t + 1], axis=0),
                                            in_=token[:, t:t + 1], in_offset=None).then_inc(scattered, 16)
            pool.wait_ge(scattered, 16 * 2 * NTL)

        @block.vector
        def _(dve):
            f.start_dve(dve)
            l_done.start(dve)
            dve.wait_ge(consts_in, 16 * 8)

            def front(c, p):
                f.stats(dve, c, p)
                f.normalise(dve, c, p, extra=[stored(c - 2)])

            def main(c, p):
                for j in range(TJ):
                    dve.wait_ge(*l_mm(c, j + 1))
                    dve.tensor_copy(lg[:, bass.ds(c * TJ + j, 1), :] if not isinstance(c, int) else lg[:, c * TJ + j:c * TJ + j + 1, :],
                                    ps[:, j % 2, 0:NE].unsqueeze(1)).then_inc(l_done.sem, 1)

            over_chunks(dve, NC, front, main)
            dve.wait_ge(*l_done(NC - 1))

            done = [0]

            def step(instruction):
                done[0] += 1
                instruction.then_inc(step_done, 1)
                dve.wait_ge(step_done, done[0])

            over_e = lambda a: a.unsqueeze(1).to_broadcast(E3)
            over_t = lambda a: a.unsqueeze(2).to_broadcast(E3)
            work = t1[:, 0:NTL, :]
            for i in range(2):
                step(dve.tensor_reduce(m[:, i], lg[:, :, :], AX.X, ALU.max))
                step(dve.tensor_tensor(work, lg[:, :, :], over_t(m[:, i]), ALU.is_ge))
                step(dve.tensor_tensor(work, work, over_e(iota[:, :]), ALU.mult))
                step(dve.tensor_reduce(ix[:, :], work, AX.X, ALU.min))
                step(dve.tensor_tensor(oh[:, i], over_e(iota[:, :]), over_t(ix[:, :]), ALU.is_equal))
                if i == 0:
                    step(dve.scalar_tensor_tensor(lg[:, :, :], oh[:, 0], -3e38, lg[:, :, :], ALU.mult, ALU.add))
            step(dve.tensor_tensor(dd[:, :], m[:, 1], m[:, 0], ALU.subtract))
            dve.wait_ge(exp_done, 1)
            step(dve.tensor_scalar(den[:, :], ex[:, :], 1.0, None, ALU.add))
            step(dve.reciprocal(wt[:, 0], den[:, :]))
            step(dve.tensor_tensor(wt[:, 1], ex[:, :], wt[:, 0], ALU.mult))
            step(dve.tensor_tensor(lg[:, :, :], oh[:, 0], oh[:, 1], ALU.add))
            step(dve.memset(cum[:, 0, :], 0.0))
            dve.wait_ge(rank_mm, 2)
            tot = ps[:, 4:8, :].rearrange("p b (t e) -> p (b t) e", e=NE)
            for t in range(NTL):
                step(dve.tensor_tensor(cum[:, t + 1, :], cum[:, t, :], tot[:, t, :], ALU.add))
            nw = t1[:, :, 0:NTL]
            step(dve.tensor_tensor(nw, cum[:, NTL, :].unsqueeze(2).to_broadcast([P, NE, NTL]),
                                   steps[:, :].unsqueeze(1).to_broadcast([P, NE, NTL]), ALU.is_gt))
            step(dve.tensor_reduce(nt[:, :], nw, AX.X, ALU.add))
            step(dve.tensor_tensor(t1[:, :, :], upto[:, :, :], nt[:, :].unsqueeze(1).to_broadcast([P, NE, NE]), ALU.mult))
            step(dve.tensor_reduce(end[:, :], t1[:, :, :], AX.X, ALU.add))
            step(dve.tensor_tensor(first[:, :], end[:, :], nt[:, :], ALU.subtract))
            step(dve.tensor_scalar(first[:, :], first[:, :], float(P), None, ALU.mult))
            pre = ps[:, 0:4, :].rearrange("p b (t e) -> p (b t) e", e=NE)
            step(dve.tensor_tensor(lg[:, :, :], pre, cum[:, 0:NTL, :], ALU.add))
            step(dve.tensor_tensor(lg[:, :, :], lg[:, :, :], over_e(first[:, :]), ALU.add))
            for i in range(2):
                step(dve.tensor_tensor(oh[:, i], oh[:, i], lg[:, :, :], ALU.mult))
                step(dve.tensor_reduce(slot_f[:, i], oh[:, i], AX.X, ALU.add))
            step(dve.tensor_copy(slot[:, :, :], slot_f[:, :, :]))
            for h in range(SLOT_TILES // NE):
                sl = slice(h * NE, (h + 1) * NE)
                step(dve.tensor_tensor(t1[0:1, :, :], tiles[0:1, sl].unsqueeze(2).to_broadcast([1, NE, NE]),
                                       end[0:1, :].unsqueeze(1).to_broadcast([1, NE, NE]), ALU.is_ge))
                step(dve.tensor_reduce(own_f[0:1, sl], t1[0:1, :, :], AX.X, ALU.add))
            step(dve.tensor_scalar(own_f[0:1, SLOT_TILES:], end[0:1, NE - 1:NE], float(P // 4), None, ALU.mult))
            step(dve.tensor_tensor(ex[0:1, :], own_f[0:1, SLOT_TILES:].to_broadcast([1, NTL]), steps[0:1, :], ALU.is_gt))
            step(dve.tensor_reduce(own_f[0:1, SLOT_TILES:], ex[0:1, :], AX.X, ALU.add))
            step(dve.tensor_scalar(own[0:1, :], own_f[0:1, :], float(NE - 1), None, ALU.min))
            assert done[0] == STEPS_END

        @block.scalar
        def _(act):
            f.xT_done.start(act)
            over_chunks(act, NC, lambda c, p: f.keep(act, c, p, l_mm(c - 2)), None)
            act.wait_ge(step_done, 12)
            act.activation(ex[:, :], dd[:, :], ACT.Exp).then_inc(exp_done, 1)

        @block.tensor
        def _(pe):
            f.tp_done.start(pe)
            l_mm.start(pe)
            pe.wait_ge(consts_in, 16 * 8)

            def main(c, p):
                pe.wait_ge(*f.xT_done(c))
                for j in range(TJ):
                    pe.wait_ge(*l_done(c, j - 1))
                    for k in range(KD):
                        i = pe.matmul(ps[:, j % 2, 0:NE], f.xT[:, p, k, j * P:(j + 1) * P], gate_s[:, k, :], start=k == 0, stop=k == KD - 1)
                    i.then_inc(l_mm.sem, 1)

            over_chunks(pe, NC, lambda c, p: f.turn(pe, c, p, ident), main)
            pe.wait_ge(one_set, 2)
            pe.wait_ge(step_done, 16)
            both = lg[:, :, :].rearrange("p t e -> p (t e)")
            for w, bank in ((before, 0), (ones, 4)):
                for b in range(4):
                    i = pe.matmul(ps[:, bank + b, :], w[:, :], both[:, b * 512:(b + 1) * 512], start=True, stop=True)
                i.then_inc(rank_mm, 1)


def stage_experts(nc, tag, xn_d, table, expert_d, w0, w1, wo, ident_d, out_d):
    NT = SLOT_TILES
    HF = FF // 2
    with Stage(nc, tag) as st:
        ps = st.banks()
        ident = st.sb("ident", [P, P])
        tab = st.sb("tab", [NT, P])
        slots = st.sb("slots", [P, NT + 4], U32)
        own = st.sb("own", [1, NT + 1], I32)
        ix = st.sb("ix", [P, 4], U32)
        w0_s = st.sb("w0", [P, 2, KD, FF])
        w1_s = st.sb("w1", [P, 2, KD, FF])
        wo_s = st.sb("wo", [P, 2, FF // P, D])
        x = st.sb("x", [P, 4, D])
        xT = st.sb("xT", [P, 2, KD, P])
        g = st.sb("g", [P, 2, HF])
        h = st.sb("h", [P, 2, HF])
        hT = st.sb("hT", [P, 2, 4, P])
        y = st.sb("y", [P, 2, D])
        consts_in = st.sem("consts_in")
        tab_mm = st.sem("tab_mm")
        slots_done = st.sem("slots_done")
        tail_set = st.sem("tail_set")
        w_in = [[st.sem(f"{n}_in{p}") for p in range(2)] for n in ("w0", "w1", "wo")]
        ix_done = st.count("ix_done", 1)
        x_in = [st.sem(f"x_in{p}") for p in range(4)]
        x_mm = st.count("x_mm", 1, lead=3)
        xT_done = st.count("xT_done", 1)
        h_mm = st.count("h_mm", 4)
        g_done = st.count("g_done", 2)
        h_done = st.count("h_done", 2)
        t_mm = st.count("t_mm", 2)
        hT_done = st.count("hT_done", 2)
        y_mm = st.count("y_mm", 1)
        y_done = st.count("y_done", 1)
        stored = [st.sem("stored0"), st.sem("stored1")]
        block = st.ctx.enter_context(nc.Block())

        def before(i, p):
            return i * 32 + 16 * (p // 2)

        def rounds(eng, front, main):
            n = eng.value_load(own[0:1, NT:NT + 1], min_val=1, max_val=NT // 4)
            if front:
                front(0, 0, 0)
            with eng.Fori(0, n) as i:
                for p in range(4):
                    if front:
                        front(i + 1 if p == 3 else i, i * 4 + (p + 1), (p + 1) % 4)
                    main(i, i * 4 + p, p)
            return n

        def tile_rows(t, c):
            return t.rearrange("(c p) d -> c p d", p=P)[bass.ds(c, 1)].rearrange("o p d -> p (o d)")

        @block.sync
        def _(sp):
            sp.dma_start(ident[:, :], ident_d).then_inc(consts_in, 16)
            sp.dma_start(tab[:, :], table.rearrange("(t p) o -> t (p o)", p=P)).then_inc(consts_in, 16)
            sp.dma_start(own[:, :], expert_d).then_inc(consts_in, 16)
            sp.wait_ge(consts_in, 48)

            def main(i, c, p):
                e = sp.value_load(own[0:1, bass.ds(c, 1)], min_val=0, max_val=NE - 1)
                for n, (dst, src) in enumerate(((w0_s, w0), (w1_s, w1), (wo_s, wo))):
                    sp.wait_ge(*(y_mm if n == 2 else h_mm)(c - 2))
                    st.plain(sp)
                    sp.dma_start(dst[:, p % 2], src[bass.ds(e, 1)].rearrange("o (k p) n -> p (o k) n", p=P)).then_inc(w_in[n][p % 2], 16)

            rounds(sp, None, main)

        @block.gpsimd
        def _(pool):
            ix_done.start(pool)
            pool.memset(slots[:, NT:], 0).then_inc(tail_set, 1)
            pool.wait_ge(tail_set, 1)
            pool.wait_ge(slots_done, 1)
            pool.wait_ge(consts_in, 48)

            def gather(c, p):
                pool.wait_ge(*x_mm(c - 4))
                st.plain(pool)
                pool.tensor_copy(ix[:, p:p + 1], slots[:, bass.ds(c, 1)]).then_inc(ix_done.sem, 1)
                pool.wait_ge(*ix_done(c))
                st.plain(pool)
                pool.indirect_dma_start(out=x[:, p, :], out_offset=None, in_=xn_d,
                                        in_offset=bass.IndirectOffsetOnAxis(ap=ix[:, p:p + 1], axis=0)).then_inc(x_in[p], 16)

            n = rounds(pool, None, lambda i, c, p: gather(c, p))
            gather(n * 4, 0)
            pool.wait_ge(x_in[0], n * 16 + 16)
            st.plain(pool)

        @block.vector
        def _(dve):
            for s in (h_done, y_done):
                s.start(dve)
            dve.wait_ge(tab_mm, 1)
            dve.tensor_copy(slots[:, 0:NT], ps[:, 0, 0:NT]).then_inc(slots_done, 1)
            dve.wait_ge(consts_in, 48)

            def main(i, c, p):
                for a in range(2):
                    dve.wait_ge(*g_done(c, a + 1))
                    dve.wait_ge(*h_mm(c, 2 * a + 2))
                    dve.wait_ge(*t_mm(c - 1, a + 1))
                    dve.tensor_tensor(h[:, a], g[:, a], ps[:, 2 * a + 1, :], ALU.mult).then_inc(h_done.sem, 1)
                dve.wait_ge(*y_mm(c))
                dve.wait_ge(stored[p % 2], before(i, p))
                dve.tensor_copy(y[:, p % 2, :], ps[:, 7, :]).then_inc(y_done.sem, 1)

            rounds(dve, None, main)

        @block.scalar
        def _(act):
            for s in (xT_done, g_done, hT_done):
                s.start(act)
            act.wait_ge(consts_in, 48)

            def front(i, c, p):
                act.wait_ge(*x_mm(c))
                act.wait_ge(*h_mm(c - 2))
                act.activation(xT[:, p % 2], ps[:, 6, :].rearrange("p (k t) -> p k t", k=KD), ACT.Copy).then_inc(xT_done.sem, 1)

            def main(i, c, p):
                def silu(a):
                    act.wait_ge(*h_mm(c, 2 * a + 1))
                    act.wait_ge(*h_done(c - 1, a + 1))
                    act.activation(g[:, a], ps[:, 2 * a, :], ACT.Silu).then_inc(g_done.sem, 1)

                def keep(a):
                    act.wait_ge(*t_mm(c, a + 1))
                    act.wait_ge(*y_mm(c - 1))
                    act.activation(hT[:, a], ps[:, 4 + a, :].rearrange("p (k t) -> p k t", k=4), ACT.Copy).then_inc(hT_done.sem, 1)

                silu(0)
                silu(1)
                keep(0)
                keep(1)
                act.wait_ge(*y_done(c))
                st.plain(act)
                act.dma_start(tile_rows(out_d, c), y[:, p % 2, :]).then_inc(stored[p % 2], 16)

            n = rounds(act, front, main)
            for p in range(2):
                act.wait_ge(stored[p], n * 32)
                st.plain(act)

        @block.tensor
        def _(pe):
            for s in (x_mm, h_mm, t_mm, y_mm):
                s.start(pe)
            pe.wait_ge(consts_in, 48)
            pe.transpose(ps[:, 0, 0:NT], tab[:, :], ident[0:NT, 0:NT]).then_inc(tab_mm, 1)
            pe.wait_ge(slots_done, 1)

            def front(i, c, p):
                pe.wait_ge(x_in[p], i * 16 + 16)
                pe.wait_ge(*xT_done(c - 1))
                for k in range(KD):
                    mm = pe.transpose(ps[:, 6, k * P:(k + 1) * P], x[:, p, k * P:(k + 1) * P], ident[:, :])
                mm.then_inc(x_mm.sem, 1)

            def main(i, c, p):
                def up(a, which):
                    w = (w0_s, w1_s)[which]
                    if a == 0:
                        pe.wait_ge(w_in[which][p % 2], before(i, p) + 16)
                    pe.wait_ge(*h_done(c - 1, a + 1))
                    for k in range(KD):
                        mm = pe.matmul(ps[:, 2 * a + which, :], xT[:, p % 2, k, :], w[:, p % 2, k, a * HF:(a + 1) * HF], start=k == 0, stop=k == KD - 1)
                    mm.then_inc(h_mm.sem, 1)

                def turn(a):
                    pe.wait_ge(*h_done(c, a + 1))
                    pe.wait_ge(*hT_done(c - 1, a + 1))
                    for k in range(4):
                        mm = pe.transpose(ps[:, 4 + a, k * P:(k + 1) * P], h[:, a, k * P:(k + 1) * P], ident[:, :])
                    mm.then_inc(t_mm.sem, 1)

                def down(k):
                    return pe.matmul(ps[:, 7, :], hT[:, k // 4, k % 4, :], wo_s[:, p % 2, k, :], start=k == 0, stop=k == 7)

                pe.wait_ge(*xT_done(c))
                up(0, 0)
                up(0, 1)
                up(1, 0)
                turn(0)
                up(1, 1)
                pe.wait_ge(w_in[2][p % 2], before(i, p) + 16)
                pe.wait_ge(*hT_done(c, 1))
                pe.wait_ge(*y_done(c - 1))
                for k in range(3):
                    down(k)
                turn(1)
                down(3)
                pe.wait_ge(*hT_done(c, 2))
                for k in range(4, 8):
                    mm = down(k)
                mm.then_inc(y_mm.sem, 1)

            rounds(pe, front, main)


def stage_combine(nc, tag, x_in, rows_d, route_d, weight_d, x_out):
    with Stage(nc, tag) as st:
        slot = st.sb("slot", [P, 2, NTL], U32)
        wt = st.sb("wt", [P, 2, NTL])
        ix = st.sb("ix", [P, 2, 2], U32)
        cw = st.sb("cw", [P, 2, 2])
        g = st.sb("g", [P, 2, 2, D])
        x = st.sb("x", [P, 2, D])
        mid = st.sb("mid", [P, 2, D])
        out = st.sb("out", [P, 2, D])
        consts_in = st.sem("consts_in")
        ix_done = st.count("ix_done", 1)
        g_in = [[st.sem(f"g_in{p}{i}") for i in range(2)] for p in range(2)]
        x_ld = [st.sem("x_ld0"), st.sem("x_ld1")]
        cw_done = st.count("cw_done", 1)
        mid_done = st.count("mid_done", 1)
        out_done = st.count("out_done", 1)
        stored = [st.sem("stored0"), st.sem("stored1")]
        block = st.ctx.enter_context(nc.Block())

        def column(t, c):
            return t[:, :, c:c + 1] if isinstance(c, int) else t[:, :, bass.ds(c, 1)]

        def tile_rows(t, c):
            v = t.rearrange("(c p) d -> c p d", p=P)
            return v[c] if isinstance(c, int) else v[bass.ds(c, 1)].rearrange("o p d -> p (o d)")

        def before(c, p):
            return 16 * (c // 2) if isinstance(c, int) else (c - p) * 8

        @block.sync
        def _(sp):
            sp.dma_start(slot[:, :, :], route_d).then_inc(consts_in, 16)
            sp.dma_start(wt[:, :, :], weight_d).then_inc(consts_in, 16)

            def main(c, p):
                sp.wait_ge(*mid_done(c - 2))
                st.plain(sp)
                sp.dma_start(x[:, p, :], tile_rows(x_in, c)).then_inc(x_ld[p], 16)

            over_chunks(sp, NTL, None, main)

        @block.vector
        def _(dve):
            for s in (ix_done, cw_done, mid_done, out_done):
                s.start(dve)
            dve.wait_ge(consts_in, 32)

            def front(c, p):
                for i in range(2):
                    dve.wait_ge(g_in[p][i], before(c, p))
                dve.tensor_copy(ix[:, p].unsqueeze(2), column(slot, c)).then_inc(ix_done.sem, 1)
                dve.wait_ge(*out_done(c - 2))
                dve.tensor_copy(cw[:, p].unsqueeze(2), column(wt, c)).then_inc(cw_done.sem, 1)

            def main(c, p):
                dve.wait_ge(x_ld[p], before(c, p) + 16)
                dve.wait_ge(g_in[p][0], before(c, p) + 16)
                dve.wait_ge(*cw_done(c))
                dve.scalar_tensor_tensor(mid[:, p, :], g[:, p, 0, :], cw[:, p, 0:1], x[:, p, :], ALU.mult, ALU.add).then_inc(mid_done.sem, 1)
                dve.wait_ge(*mid_done(c))
                dve.wait_ge(g_in[p][1], before(c, p) + 16)
                dve.wait_ge(stored[p], before(c, p))
                dve.scalar_tensor_tensor(out[:, p, :], g[:, p, 1, :], cw[:, p, 1:2], mid[:, p, :], ALU.mult, ALU.add).then_inc(out_done.sem, 1)

            over_chunks(dve, NTL, front, main)

        @block.gpsimd
        def _(pool):
            def front(c, p):
                pool.wait_ge(*ix_done(c))
                pool.wait_ge(*out_done(c - 2))
                st.plain(pool)
                for i in range(2):
                    pool.indirect_dma_start(out=g[:, p, i, :], out_offset=None, in_=rows_d,
                                            in_offset=bass.IndirectOffsetOnAxis(ap=ix[:, p, i:i + 1], axis=0)).then_inc(g_in[p][i], 16)

            over_chunks(pool, NTL, front, None)

        @block.scalar
        def _(act):
            def main(c, p):
                act.wait_ge(*out_done(c))
                st.plain(act)
                act.dma_start(tile_rows(x_out, c), out[:, p, :]).then_inc(stored[p], 16)

            over_chunks(act, NTL, None, main)
            for p in range(2):
                act.wait_ge(stored[p], 16 * (NTL // 2))


def shape_constants():
    f = np.float32
    j = np.arange(P)
    e = np.arange(NE)
    causal = np.where(np.arange(SK)[None] <= np.arange(S)[:, None], 0.0, NEG).astype(f)
    fwd, inv = transform_tables()
    return {
        "ident": np.eye(P, dtype=f),
        "tri": np.where(j[None] < j[:, None], NEG, 0.0).astype(f),
        "causal": np.concatenate([causal] * B),
        "fwd": fwd, "inv": inv,
        "before": (j[:, None] < j[None]).astype(f),
        "iota": (e - NE).astype(f)[None],
        "steps": (P * np.arange(NTL)).astype(f)[None],
        "upto": (e[None] <= e[:, None]).astype(f).reshape(1, NE * NE),
        "tiles": np.arange(SLOT_TILES).astype(f)[None],
        "token": (j[:, None] + P * np.arange(NTL)[None]).astype(f),
    }


def build_decoder(nc, t, out):
    def rows(name, n=N, w=D, dt=F32):
        return nc.dram_tensor(name, (n, w), dt).ap()

    x1, x2, h1, h2, x3, x4, x5 = (rows(n) for n in ("x1", "x2", "h1", "h2", "x3", "x4", "x5"))
    k, v, q, y = (rows(n) for n in ("conv_k", "conv_v", "conv_q", "conv_y"))
    ident = t["ident"]
    a = lambda n: t["L0_attn_" + n]
    stage_attention(nc, t["x"], x1, ident, t["tri"], a("Wq"), a("Wk"), a("Wv"), a("bq"), a("bk"), a("bv"))
    a = lambda n: t["L0_xattn_" + n]
    stage_cross(nc, "xa", x1, x2, ident, t["ctxT"], t["mask"], a("Wq"), a("Wk"), a("Wv"), a("bq"), a("bk"), a("bv"))
    a = lambda n: t["L0_ffn_" + n]
    for blk, (src, dst) in enumerate(((x2, h1), (h1, h2), (h2, x3))):
        i = slice(2 * blk, 2 * blk + 2)
        stage_ffn(nc, f"ff{blk}", src, dst, ident, a("qweights")[i], a("scales")[i], a("lora_a")[i], a("lora_b")[i],
                  a("biases")[i], a("ln_gamma")[blk], a("ln_beta")[blk], blk == 0, x2 if blk == 2 else None)
    a = lambda n: t["L1_attn_" + n]
    stage_project(nc, "pr", x3, [k, v, q], ident, [a("Wk"), a("Wv"), a("Wq")], [a("bk"), a("bv"), a("bq")])
    stage_conv(nc, k, v, y, a("k_kernel"), a("ssm_kernel"), a("k_D"), a("D"), t["fwd"], t["inv"])
    stage_gated_out(nc, "go", x3, y, q, x4, ident, a("Wo"), a("bo"))
    a = lambda n: t["L1_xattn_" + n]
    stage_cross(nc, "xb", x4, x5, ident, t["ctxT"], t["causal"], a("Wq"), a("Wk"), a("Wv"), wo=a("Wo"))
    a = lambda n: t["L1_ffn_" + n]
    xn = rows("moe_xn")
    slot_rows = rows("slot_rows", SLOT_TILES * P)
    table = rows("slot_token", SLOT_TILES * P, 1)
    own = rows("tile_expert", 1, SLOT_TILES + 1, I32)
    route = nc.dram_tensor("token_slots", (P, 2, NTL), U32).ap()
    weight = nc.dram_tensor("token_weights", (P, 2, NTL), F32).ap()
    stage_route(nc, "ro", x5, xn, ident, a("gate_kernel"), table, route, weight, own, slot_rows,
                [t[n] for n in ("before", "iota", "steps", "upto", "tiles", "token")])
    stage_experts(nc, "ex", xn, table, own, a("w0"), a("w1"), a("wo"), ident, slot_rows)
    stage_combine(nc, "co", x5, slot_rows, route, weight, out)


def laid_out(inputs):
    t = {n: np.asarray(v) for n, v in inputs.items()}
    t["x"] = t["x"].reshape(N, D)
    t["mask"] = t.pop("mask_BxSxS2_ff1").reshape(N, SK)
    t["ctxT"] = t.pop("ctx_1024").reshape(B * SK, D).T
    for n in ("L0_xattn_Wq", "L0_xattn_Wk", "L0_xattn_Wv", "L1_attn_Wq", "L1_attn_Wk", "L1_attn_Wv", "L1_attn_Wo",
              "L1_attn_k_kernel", "L1_attn_ssm_kernel", "L1_xattn_Wq", "L1_xattn_Wk", "L1_xattn_Wv", "L1_xattn_Wo"):
        t[n] = t[n].T
    for n in ("L0_ffn_qweights", "L0_ffn_scales", "L0_ffn_lora_b"):
        t[n] = t[n].transpose(0, 2, 1)
    t.update(shape_constants())
    return {n: np.ascontiguousarray(v) for n, v in t.items()}


def kernel(**inputs):
    from concourse import bacc
    from concourse.bass_utils import run_bass_kernel_spmd

    nc = bacc.Bacc("TRN2", target_bir_lowering=False, num_devices=1)
    arrays = laid_out(inputs)
    t = {n: nc.dram_tensor(n, v.shape, mybir.dt.from_np(v.dtype), kind="ExternalInput").ap() for n, v in arrays.items()}
    out = nc.dram_tensor("out", (N, D), F32, kind="ExternalOutput").ap()
    build_decoder(nc, t, out)
    r = run_bass_kernel_spmd(nc, [arrays], core_ids=[0])
    return r.results[0]["out"].reshape(B, S, D)
```

```python
import numpy as np
import concourse.bass as bass
from concourse import mybir
from contextlib import ExitStack

F32 = mybir.dt.float32
I32 = mybir.dt.int32
U32 = mybir.dt.uint32
ALU = mybir.AluOpType
ACT = mybir.ActivationFunctionType
AX = mybir.AxisListType

P = 128
B, S, D = 2, 2048, 512
N = B * S
KD = D // P
TJ = 4
CH = TJ * P
NC = N // CH
CB = S // CH
SK = 77
H, HD = 16, 32
EPS = 1e-5
NEG = -1e30


class Count:

    def __init__(self, st, name, per, unit=1, lead=1):
        self.sem = st.sem(name)
        self.per, self.unit, self.lead = per, unit, lead

    def start(self, eng):
        eng.sem_inc(self.sem, self.lead * self.per * self.unit)

    def __call__(self, c, k=None):
        k = self.per if k is None else k
        return self.sem, (c * self.per + (self.lead * self.per + k)) * self.unit


class Stage:

    def __init__(self, nc, name):
        self.nc, self.name, self.ctx, self.sems = nc, name, ExitStack(), []
        self.passed = self.sem("passed")

    def __enter__(self):
        return self

    def __exit__(self, *a):
        self.ctx.close()
        self.nc.clear_and_free_semaphores(self.sems)
        self.nc.all_engine_barrier()

    def sb(self, name, shape, dt=F32):
        return self.ctx.enter_context(self.nc.sbuf_tensor(f"{self.name}_{name}", shape, dt))

    def banks(self):
        return self.ctx.enter_context(self.nc.psum_tensor(f"{self.name}_ps", [P, 8, 512], F32))

    def sem(self, name):
        self.sems.append(self.nc.alloc_semaphore(f"{self.name}_{name}"))
        return self.sems[-1]

    def plain(self, eng):
        eng.sem_inc(self.passed, 1)

    def count(self, name, per, unit=1, lead=1):
        return Count(self, name, per, unit, lead)


def chunk_rows(t, c):
    v = t.rearrange("(c j p) d -> c p j d", p=P, j=TJ)
    if isinstance(c, int):
        return v[c]
    return v[bass.ds(c, 1)].rearrange("o p j d -> p (o j) d")


def over_chunks(eng, n, front, main):
    if front:
        front(0, 0)
    with eng.Fori(0, n // 2 - 1) as i:
        for p in range(2):
            if front:
                front(i * 2 + (p + 1), 1 - p)
            if main:
                main(i * 2 + p, p)
    if front:
        front(n - 1, 1)
    for p in range(2):
        if main:
            main(n - 2 + p, p)


def over_whole(eng, n, first, main):
    first()
    with eng.Fori(0, n // 2 - 1) as i:
        for p in range(2):
            main(i * 2 + p, p, 2)
    main(n - 2, 0, 1)
    main(n - 1, 1, 0)


def weight_view(w):
    return w.rearrange("(k p) n -> p k n", p=P)


class Front:

    def __init__(self, st, ps, bank, src, x=None, xn=None, xT=None, norm=True):
        self.st, self.src, self.norm = st, src, norm
        self.x = x if x is not None else st.sb("x", [P, 2, TJ, D])
        self.xn = (xn if xn is not None else st.sb("xn", [P, 2, TJ, D])) if norm else self.x
        self.xT = xT if xT is not None else st.sb("xT", [P, 2, KD, CH])
        self.bank, self.ps = bank, ps
        self.bn = st.sb("bn", [P, 2, TJ, 6])
        self.mv = st.sb("mv", [P, 2, TJ, 2])
        self.rs = st.sb("rs", [P, 2, TJ])
        self.half = st.sb("mhalf", [P, TJ])
        self.half_set = st.sem("half_set")
        self.x_in = [st.sem("x_in0"), st.sem("x_in1")]
        self.bn_done = st.count("bn_done", TJ)
        self.mv_done = st.count("mv_done", TJ)
        self.var_done = st.count("var_done", 1)
        self.rs_done = st.count("rs_done", 1)
        self.xn_done = st.count("xn_done", TJ)
        self.tp_done = st.count("tp_done", TJ)
        self.xT_done = st.count("xT_done", TJ)

    def start_dve(self, dve):
        for c in (self.bn_done, self.mv_done, self.xn_done):
            c.start(dve)

    def start_pool(self, pool):
        for c in (self.var_done, self.rs_done):
            c.start(pool)
        pool.memset(self.half[:, :], -0.5).then_inc(self.half_set, 1)

    def load(self, sp, c, p):
        self.st.plain(sp)
        sp.dma_start(self.x[:, p], chunk_rows(self.src, c)).then_inc(self.x_in[p], 16)

    def x_ready(self, c, p):
        if isinstance(c, int):
            return self.x_in[p], 16 * (c // 2 + 1)
        return self.x_in[p], (c - p) * 8 + 16

    def stats(self, dve, c, p):
        dve.wait_ge(*self.x_ready(c, p))
        dve.wait_ge(*self.mv_done(c - 2))
        for j in range(TJ):
            dve.bn_stats(self.bn[:, p, j, :], self.x[:, p, j, :]).then_inc(self.bn_done.sem, 1)
        dve.wait_ge(*self.var_done(c - 2))
        dve.wait_ge(*self.xn_done(c - 2))
        for j in range(TJ):
            dve.wait_ge(*self.bn_done(c, j + 1))
            self.st.plain(dve)
            dve.bn_aggr(self.mv[:, p, j, :], self.bn[:, p, j, :]).then_inc(self.mv_done.sem, 1)

    def rstd(self, pool, c, p):
        pool.wait_ge(*self.mv_done(c))
        pool.wait_ge(*self.xn_done(c - 2))
        self.st.plain(pool)
        pool.tensor_scalar(self.rs[:, p], self.mv[:, p, :, 1], EPS, None, ALU.add).then_inc(self.var_done.sem, 1)
        pool.wait_ge(*self.var_done(c))
        pool.wait_ge(self.half_set, 1)
        pool.tensor_tensor(self.rs[:, p], self.rs[:, p], self.half[:, :], ALU.pow).then_inc(self.rs_done.sem, 1)

    def normalise(self, dve, c, p, extra=()):
        for j in range(TJ):
            self.normalise_tile(dve, c, p, j, extra)

    def normalise_tile(self, dve, c, p, j, extra=()):
        if j == 0:
            dve.wait_ge(*self.rs_done(c))
            dve.wait_ge(*self.tp_done(c - 2))
            for w in extra:
                dve.wait_ge(*w)
        dve.tensor_scalar(self.xn[:, p, j, :], self.x[:, p, j, :], self.mv[:, p, j, 0:1],
                          self.rs[:, p, j:j + 1], ALU.subtract, ALU.mult).then_inc(self.xn_done.sem, 1)

    def turn(self, pe, c, p, ident, nb=2):
        for j in range(TJ):
            self.turn_tile(pe, c, p, j, ident, nb)

    def turn_tile(self, pe, c, p, j, ident, nb=2):
        if self.norm:
            pe.wait_ge(*self.xn_done(c, j + 1))
        elif j == 0:
            pe.wait_ge(*self.x_ready(c, p))
        pe.wait_ge(*self.xT_done(c, j + 1 - nb))
        bank = self.ps[:, self.bank + j % nb, :]
        for k in range(KD):
            i = pe.transpose(bank[:, k * P:(k + 1) * P], self.xn[:, p, j, k * P:(k + 1) * P], ident[:, :])
        i.then_inc(self.tp_done.sem, 1)

    def keep(self, act, c, p, used, nb=2):
        act.wait_ge(*used)
        for j in range(TJ):
            self.keep_tile(act, c, p, j, nb)

    def keep_tile(self, act, c, p, j, nb=2):
        act.wait_ge(*self.tp_done(c, j + 1))
        act.activation(self.xT[:, p, :, j * P:(j + 1) * P],
                       self.ps[:, self.bank + j % nb, :].rearrange("p (k t) -> p k t", k=KD),
                       ACT.Copy).then_inc(self.xT_done.sem, 1)


def stage_attention(nc, x_in, x_out, ident_d, tri_d, wq, wk, wv, bq, bk, bv):
    NJ = S // P
    with Stage(nc, "at") as st:
        ps = st.banks()
        ident = st.sb("ident", [P, P])
        tri = st.sb("tri", [P, P])
        bqT = st.sb("bqT", [P, KD])
        bkT = st.sb("bkT", [P, KD])
        bvB = st.sb("bvB", [P, D])
        qT = st.sb("qT", [P, KD, S])
        kT = st.sb("kT", [P, KD, S])
        v = st.sb("v", [P, NJ, D])
        acc = st.sb("acc", [P, NJ, D])
        region = st.sb("region", [P, 18 * 1024])
        cut = lambda i, n: region[:, i * 1024:(i + n) * 1024]
        xb = cut(0, 4).rearrange("p (b j d) -> p b j d", b=2, j=TJ)
        xnb = cut(4, 4).rearrange("p (b j d) -> p b j d", b=2, j=TJ)
        xTb = cut(8, 4).rearrange("p (b k t) -> p b k t", b=2, k=KD)
        w_sb = [cut(12 + 2 * i, 2).rearrange("p (k n) -> p k n", k=KD) for i in range(3)]
        prob = [cut(0, 8).rearrange("p (j i) -> p j i", j=4), cut(8, 6).rearrange("p (j i) -> p j i", j=4)]
        nmax = st.sb("nmax", [P, NJ])
        rmax = st.sb("rmax", [P, NJ])
        rsum = st.sb("rsum", [P, NJ])
        rinv = st.sb("rinv", [P, NJ])
        f = Front(st, ps, 6, x_in, xb, xnb, xTb)
        consts_in = st.sem("consts_in")
        w_in = st.sem("w_in")
        qk_mm = st.count("qk_mm", 12)
        qk_done = st.count("qk_done", 8)
        v_done = st.count("v_done", TJ)
        m_done = st.count("m_done", 1)
        PV = [(g, it) for g in range(4) for it in range(4 * g, NJ)]
        s_mm = st.count("s_mm", NJ)
        tri_done = st.count("tri_done", NJ)
        max_done = st.count("max_done", NJ)
        nmax_done = st.count("nmax_done", NJ)
        exp_done = st.count("exp_done", NJ)
        inv_done = st.count("inv_done", NJ)
        vs_done = st.count("vs_done", NJ)
        pv_mm = st.count("pv_mm", len(PV))
        acc_done = st.count("acc_done", len(PV))
        out_done = st.count("out_done", CB, 16)

        def pv_after(j):
            g, jj = j // 4 - 1, j % 4
            if g < 0:
                return []
            mine = [n for n, (gg, _) in enumerate(PV) if gg == g]
            if j == NJ:
                return mine
            q = len(mine) // 4
            return mine[q * jj:q * jj + q]

        rinv_done = st.sem("rinv_done")

        block = st.ctx.enter_context(nc.Block())

        @block.sync
        def _(sp):
            out_done.start(sp)
            for dst, src in ((ident, ident_d), (tri, tri_d)):
                sp.dma_start(dst[:, :], src).then_inc(consts_in, 16)
            sp.dma_start(bqT[:, :], bq.rearrange("(k p) -> p k", p=P), allow_slow_non_contiguous=True).then_inc(consts_in, 16)
            sp.dma_start(bkT[:, :], bk.rearrange("(k p) -> p k", p=P), allow_slow_non_contiguous=True).then_inc(consts_in, 16)
            sp.dma_start(bvB[:, :], bv.rearrange("(o n) -> o n", o=1).to_broadcast([P, D])).then_inc(consts_in, 16)
            with sp.Fori(0, B) as b:
                sp.wait_ge(*pv_mm(b - 1))
                for ci in range(CB):
                    if ci >= 2:
                        sp.wait_ge(*f.xn_done(b * CB + (ci - 2)))
                        st.plain(sp)
                        sp.wait_ge(*m_done(b * CB + (ci - 2)))
                    f.load(sp, b * CB + ci, ci % 2)
                    if ci == 0:
                        for i, w in enumerate((wq, wk, wv)):
                            sp.dma_start(w_sb[i], weight_view(w)).then_inc(w_in, 16)
                for ci in range(CB):
                    sp.wait_ge(*acc_done(b, PV.index((ci, 4 * ci + 3)) + 1))
                    st.plain(sp)
                    sp.dma_start(chunk_rows(x_out, b * CB + ci), acc[:, 4 * ci:4 * ci + 4, :]).then_inc(out_done.sem, 16)
            sp.wait_ge(*out_done(B - 1))

        @block.gpsimd
        def _(pool):
            f.start_pool(pool)
            m_done.start(pool)
            with pool.Fori(0, B) as b:
                pool.wait_ge(*out_done(b - 1))
                for ci in range(CB):
                    c = b * CB + ci
                    f.rstd(pool, c, ci % 2)
                    pool.wait_ge(*f.xn_done(c))
                    pool.tensor_tensor(acc[:, 4 * ci:4 * ci + 4, :], f.x[:, ci % 2], f.xn[:, ci % 2],
                                       ALU.add).then_inc(m_done.sem, 1)

        @block.vector
        def _(dve):
            f.start_dve(dve)
            for s in (v_done, tri_done, max_done, nmax_done, inv_done, vs_done, acc_done):
                s.start(dve)
            dve.wait_ge(consts_in, 16 * 5)
            with dve.Fori(0, B) as b:
                def front(ci):
                    c = b * CB + ci
                    f.stats(dve, c, ci % 2)
                    f.normalise(dve, c, ci % 2, extra=[m_done(c - 2)])

                front(0)
                for ci in range(CB):
                    if ci + 1 < CB:
                        front(ci + 1)
                    for j in range(TJ):
                        dve.wait_ge(*qk_mm(b * CB + ci, 8 + j + 1))
                        dve.tensor_tensor(v[:, TJ * ci + j, :], ps[:, j, :], bvB[:, :], ALU.add).then_inc(v_done.sem, 1)

                def add_out(n):
                    g, it = PV[n]
                    dve.wait_ge(*pv_mm(b, n + 1))
                    if g == 0 and it % TJ == 0:
                        dve.wait_ge(*m_done(b * CB + it // TJ))
                    if g:
                        dve.wait_ge(*acc_done(b, PV.index((g - 1, it)) + 1))
                    dve.tensor_tensor(acc[:, it, :], acc[:, it, :], ps[:, 4 + n % 4, :], ALU.add).then_inc(acc_done.sem, 1)

                for j in range(NJ):
                    row = ps[:, 0:4, :].rearrange("p b i -> p (b i)")
                    dve.wait_ge(*s_mm(b, j + 1))
                    diag = row[:, j * P:(j + 1) * P]
                    dve.tensor_tensor(diag, diag, tri[:, :], ALU.add).then_inc(tri_done.sem, 1)
                    dve.wait_ge(*tri_done(b, j + 1))
                    dve.tensor_reduce(rmax[:, j:j + 1], row[:, j * P:], AX.X, ALU.max).then_inc(max_done.sem, 1)
                    dve.wait_ge(*max_done(b, j + 1))
                    dve.tensor_scalar(nmax[:, j:j + 1], rmax[:, j:j + 1], -1.0, None, ALU.mult).then_inc(nmax_done.sem, 1)
                    for n in pv_after(j):
                        add_out(n)
                    dve.wait_ge(*exp_done(b, j + 1))
                    dve.tensor_scalar(rsum[:, j:j + 1], rsum[:, j:j + 1], float(D) ** 0.5, None,
                                      ALU.mult).then_inc(inv_done.sem, 1)
                    dve.wait_ge(*inv_done(b, j + 1))
                    dve.reciprocal(rinv[:, j:j + 1], rsum[:, j:j + 1]).then_inc(rinv_done, 1)
                    dve.wait_ge(rinv_done, b * NJ + (j + 1))
                    dve.tensor_scalar(v[:, j, :], v[:, j, :], rinv[:, j:j + 1], None, ALU.mult).then_inc(vs_done.sem, 1)
                for n in pv_after(NJ):
                    add_out(n)


        @block.scalar
        def _(act):
            for s in (f.xT_done, qk_done, exp_done):
                s.start(act)
            act.wait_ge(consts_in, 16 * 5)
            with act.Fori(0, B) as b:
                front = lambda ci: f.keep(act, b * CB + ci, ci % 2, qk_mm(b * CB + (ci - 2)))
                front(0)
                for ci in range(CB):
                    if ci + 1 < CB:
                        front(ci + 1)
                    for u in range(8):
                        dst, bias = ((qT, bqT), (kT, bkT))[u // 4]
                        m = u % 4
                        act.wait_ge(*qk_mm(b * CB + ci, u + 1))
                        act.activation(dst[:, m, ci * CH:(ci + 1) * CH], ps[:, u % 4, :], ACT.Identity,
                                       bias=bias[:, m:m + 1]).then_inc(qk_done.sem, 1)
                for j in range(NJ):
                    g, jj = j // 4, j % 4
                    row = ps[:, 0:4, :].rearrange("p b i -> p (b i)")
                    act.wait_ge(*nmax_done(b, j + 1))
                    if j == 0:
                        act.wait_ge(*m_done(b * CB + (CB - 1)))
                    if g >= 2 and jj == 0:
                        act.wait_ge(*pv_mm(b, PV.index((g - 2, NJ - 1)) + 1))
                    act.activation(prob[g % 2][:, jj, (j - 4 * g) * P:S - 4 * g * P], row[:, j * P:], ACT.Exp,
                                   bias=nmax[:, j:j + 1], accum_out=rsum[:, j:j + 1]).then_inc(exp_done.sem, 1)

        @block.tensor
        def _(pe):
            for s in (f.tp_done, qk_mm, s_mm, pv_mm):
                s.start(pe)
            pe.wait_ge(consts_in, 16 * 5)
            with pe.Fori(0, B) as b:
                f.turn(pe, b * CB, 0, ident)
                pe.wait_ge(w_in, (b + 1) * 48)
                for ci in range(CB):
                    c = b * CB + ci
                    if ci + 1 < CB:
                        f.turn(pe, c + 1, (ci + 1) % 2, ident)
                    pe.wait_ge(*f.xT_done(c))
                    for u in range(12):
                        if u < 4:
                            pe.wait_ge(*v_done(c - 1, u + 1))
                        else:
                            pe.wait_ge(*qk_done(c, u - 4 + 1))
                        for k in range(KD):
                            if u < 8:
                                i = pe.matmul(ps[:, u % 4, :], w_sb[u // 4][:, k, (u % 4) * P:(u % 4 + 1) * P],
                                              f.xT[:, ci % 2, k, :], start=k == 0, stop=k == KD - 1)
                            else:
                                i = pe.matmul(ps[:, u % 4, :], f.xT[:, ci % 2, k, (u % 4) * P:(u % 4 + 1) * P],
                                              w_sb[2][:, k, :], start=k == 0, stop=k == KD - 1)
                        i.then_inc(qk_mm.sem, 1)

                def product(n):
                    g, it = PV[n]
                    if n >= 4:
                        pe.wait_ge(*acc_done(b, n - 3))
                    js = [j for j in range(4 * g, 4 * g + 4) if j <= it]
                    pe.wait_ge(*vs_done(b, js[-1] + 1))
                    for j in js:
                        i = pe.matmul(ps[:, 4 + n % 4, :], prob[g % 2][:, j % 4, (it - 4 * g) * P:(it - 4 * g + 1) * P],
                                      v[:, j, :], start=j == js[0], stop=j == js[-1])
                    i.then_inc(pv_mm.sem, 1)

                for j in range(NJ):
                    if j == 0:
                        pe.wait_ge(*v_done(b * CB + (CB - 1)))
                        pe.wait_ge(*qk_done(b * CB + (CB - 1)))
                        pe.wait_ge(*f.xT_done(b * CB + (CB - 1)))
                    else:
                        pe.wait_ge(*exp_done(b, j))
                    for ic in range(j // 4, 4):
                        lo = max(ic * CH, j * P)
                        for k in range(KD):
                            i = pe.matmul(ps[:, ic, lo - ic * CH:], kT[:, k, j * P:(j + 1) * P],
                                          qT[:, k, lo:(ic + 1) * CH], start=k == 0, stop=k == KD - 1)
                    i.then_inc(s_mm.sem, 1)
                    for n in pv_after(j):
                        product(n)
                for n in pv_after(NJ):
                    product(n)


def pick(t, b):
    if isinstance(b, int):
        return t[:, b]
    v = t[:, bass.ds(b, 1)]
    n = len(v.shape)
    rest = [f"d{i}" for i in range(n - 2)]
    return v.rearrange(f"p o {' '.join(rest)} -> p (o {rest[0]}) {' '.join(rest[1:])}")


def stage_cross(nc, tag, x_in, x_out, ident_d, ctxT_d, mask_d, wq, wk, wv, bq=None, bk=None, bv=None, wo=None):
    HB = H // 2
    U = 2 * TJ
    LT, LV = 2, 3
    LF = 3 if wo is None else 2
    q_steps = [LF + TJ + (m if wo is None else m // 2) for m in range(KD)]
    STEPS = U + LV if wo is None else U + 7
    W4 = 4 * SK
    scale = 1.0 / float(np.sqrt(HD))
    biased = bq is not None
    with Stage(nc, tag) as st:
        ps = st.banks()
        ident = st.sb("ident", [P, P])
        wq_s = st.sb("wq", [P, KD, D])
        wk_s = st.sb("wk", [P, KD, D])
        wv_s = st.sb("wv", [P, KD, D])
        wo_s = st.sb("wo", [P, KD, D]) if wo is not None else None
        ctxT = st.sb("ctxT", [P, KD, B * SK])
        kblk = st.sb("kblk", [P, B, KD, W4])
        v1 = st.sb("v1", [SK, B, H, HD + 1])
        bias = st.sb("bias", [P, 3, KD])
        bvB = st.sb("bvB", [SK, D])
        mask = st.sb("mask", [P, 2, TJ, SK])
        qT = st.sb("qT", [P, 2, KD, CH])
        s_sb = st.sb("s", [P, 4, HB, SK])
        mx = st.sb("mx", [P, 2, HB])
        rec = st.sb("rec", [P, 2, HB])
        pT = st.sb("pT", [SK, 2, HB, P])
        o = st.sb("o", [P, 2, TJ, D])
        y = st.sb("y", [P, 2, TJ, D])
        oT = st.sb("oT", [P, 2, KD, P]) if wo is not None else None
        f = Front(st, ps, 5, x_in)
        loads = 5 + (3 if biased else 0) + (1 if wo is not None else 0)
        consts_in = st.sem("consts_in")
        kv_mm = st.sem("kv_mm")
        zeroed = st.sem("zeroed")
        bias_set = st.sem("bias_set")
        kv_set = st.sem("kv_set")
        mask_in = [st.sem("mask_in0"), st.sem("mask_in1")]
        mask_set = st.count("mask_set", 1)
        q_mm = st.count("q_mm", KD)
        q_done = st.count("q_done", KD)
        s_mm = st.count("s_mm", U)
        add_done = st.count("add_done", U)
        max_done = st.count("max_done", U)
        sub_done = st.count("sub_done", U)
        exp_done = st.count("exp_done", U)
        p_mm = st.count("p_mm", U)
        pT_done = st.count("pT_done", U)
        pv_mm = st.count("pv_mm", U)
        rec_done = st.count("rec_done", U)
        o_done = st.count("o_done", U)
        y_done = st.count("y_done", TJ)
        oT_mm = st.count("oT_mm", TJ)
        oT_done = st.count("oT_done", TJ)
        wo_mm = st.count("wo_mm", TJ)
        stored = st.count("stored", 1, 16)
        counted_dve = [add_done, max_done, rec_done, o_done, mask_set] + ([y_done] if wo is not None else [])

        block = st.ctx.enter_context(nc.Block())

        @block.sync
        def _(sp):
            stored.start(sp)
            for dst, src in ((wk_s, wk), (wv_s, wv), (wq_s, wq), (ctxT, ctxT_d)) + (((wo_s, wo),) if wo is not None else ()):
                sp.dma_start(dst[:, :, :], weight_view(src)).then_inc(consts_in, 16)
            sp.dma_start(ident[:, :], ident_d).then_inc(consts_in, 16)
            if biased:
                for i, v in enumerate((bq, bk)):
                    sp.dma_start(bias[:, i, :], v.rearrange("(k p) -> p k", p=P), allow_slow_non_contiguous=True).then_inc(consts_in, 16)
                sp.dma_start(bvB[:, :], bv.rearrange("(o n) -> o n", o=1).to_broadcast([SK, D])).then_inc(consts_in, 16)

            def front(c, p):
                sp.wait_ge(*f.xn_done(c - 2))
                sp.wait_ge(*y_done(c - 2))
                f.load(sp, c, p)
                sp.wait_ge(*add_done(c - 2))
                sp.wait_ge(*mask_set(c - 2))
                st.plain(sp)
                sp.dma_start(mask[:, p], chunk_rows(mask_d, c)).then_inc(mask_in[p], 16)

            def main(c, p):
                sp.wait_ge(*y_done(c))
                st.plain(sp)
                sp.dma_start(chunk_rows(x_out, c), y[:, p]).then_inc(stored.sem, 16)

            over_chunks(sp, NC, front, main)
            sp.wait_ge(*stored(NC - 1))

        @block.gpsimd
        def _(pool):
            f.start_pool(pool)
            sub_done.start(pool)
            pool.memset(kblk[:, :, :, :], 0.0).then_inc(zeroed, 1)
            pool.memset(v1[:, :, :, HD:HD + 1], 1.0).then_inc(zeroed, 1)
            if wo is None:
                y_done.start(pool)

            def main(c, p, more):
                for u in range(U + LV):
                    if more and u == LF - 1:
                        f.rstd(pool, c + 1, 1 - p)
                    if u < U:
                        pool.wait_ge(*max_done(c, u + 1))
                        s3 = s_sb[:, u % 4]
                        pool.tensor_tensor(s3, s3, mx[:, u % 2].unsqueeze(2).to_broadcast([P, HB, SK]),
                                           ALU.subtract).then_inc(sub_done.sem, 1)
                    if wo is None and u >= LV + 1 and u % 2 == 0:
                        j = (u - LV - 1) // 2
                        pool.wait_ge(*o_done(c, 2 * j + 2))
                        if j == 0:
                            pool.wait_ge(*stored(c - 2))
                        pool.tensor_tensor(y[:, p, j, :], f.x[:, p, j, :], o[:, p, j, :], ALU.add).then_inc(y_done.sem, 1)

            over_whole(pool, NC, lambda: f.rstd(pool, 0, 0), main)

        @block.vector
        def _(dve):
            f.start_dve(dve)
            for s in counted_dve:
                s.start(dve)
            dve.wait_ge(consts_in, 16 * loads)
            for b in range(B):
                dve.wait_ge(kv_mm, KD + b + 1)
                src = ps[0:SK, 4 + b, :].rearrange("s (h d) -> s h d", h=H)
                if biased:
                    dve.tensor_tensor(v1[:, b, :, 0:HD], src, bvB[:, :].rearrange("s (h d) -> s h d", h=H),
                                      ALU.add).then_inc(kv_set, 1)
                else:
                    dve.tensor_copy(v1[:, b, :, 0:HD], src).then_inc(kv_set, 1)

            def ahead(c, p):
                f.stats(dve, c, p)
                dve.wait_ge(mask_in[p], 16 * (c // 2 + 1) if isinstance(c, int) else (c - p) * 8 + 16)
                if biased:
                    dve.tensor_scalar(mask[:, p], mask[:, p], 10000.0, -10000.0, ALU.mult, ALU.add).then_inc(mask_set.sem, 1)
                else:
                    dve.sem_inc(mask_set.sem, 1)

            def first():
                ahead(0, 0)
                f.normalise(dve, 0, 0)

            def main(c, p, more):
                for u in range(STEPS):
                    if u < U:
                        j = u // 2
                        dve.wait_ge(*s_mm(c, u + 1))
                        if u == 0:
                            dve.wait_ge(*mask_set(c))
                        dve.wait_ge(*p_mm(c, u - 3))
                        dve.tensor_tensor(s_sb[:, u % 4].rearrange("p (m h) s -> p m h s", m=2),
                                          ps[:, 0:2, 0:W4].rearrange("p m (h s) -> p m h s", h=4),
                                          mask[:, p, j].unsqueeze(1).unsqueeze(1).to_broadcast([P, 2, 4, SK]),
                                          ALU.add).then_inc(add_done.sem, 1)
                        dve.wait_ge(*add_done(c, u + 1))
                        dve.wait_ge(*sub_done(c, u - 1))
                        dve.tensor_reduce(mx[:, u % 2], s_sb[:, u % 4], AX.X, ALU.max).then_inc(max_done.sem, 1)
                    if more and u == LF - 2:
                        ahead(c + 1, 1 - p)
                    if more and LF <= u + 1 < LF + TJ:
                        f.normalise_tile(dve, c + 1, 1 - p, u + 1 - LF)
                    v = u - LV
                    if 0 <= v < U:
                        j, half = v // 2, v % 2
                        pv = ps[:, 4, 0:HB * (HD + 1)].rearrange("p (h d) -> p h d", h=HB)
                        dve.wait_ge(*pv_mm(c, v + 1))
                        dve.wait_ge(*o_done(c, v - 1))
                        dve.reciprocal(rec[:, v % 2], pv[:, :, HD]).then_inc(rec_done.sem, 1)
                        dve.wait_ge(*rec_done(c, v + 1))
                        if v == 0:
                            dve.wait_ge(*(y_done if wo is None else oT_mm)(c - 2))
                        dve.tensor_tensor(o[:, p, j, half * 256:half * 256 + 256].rearrange("p (h d) -> p h d", h=HB),
                                          pv[:, :, 0:HD], rec[:, v % 2].unsqueeze(2).to_broadcast([P, HB, HD]),
                                          ALU.mult).then_inc(o_done.sem, 1)
                    if wo is not None and u >= 8 and u % 2 == 0:
                        j = (u - 8) // 2
                        dve.wait_ge(*wo_mm(c, j + 1))
                        if j == 0:
                            dve.wait_ge(*stored(c - 2))
                        dve.tensor_tensor(y[:, p, j, :], ps[:, 6 + j % 2, :], f.x[:, p, j, :], ALU.add).then_inc(y_done.sem, 1)

            over_whole(dve, NC, first, main)

        @block.scalar
        def _(act):
            for s in (f.xT_done, q_done, exp_done, pT_done) + ((oT_done,) if wo is not None else ()):
                s.start(act)
            act.wait_ge(consts_in, 16 * loads)
            act.wait_ge(zeroed, 2)
            if biased:
                act.activation(bias[:, 2, :], bias[:, 0, :], ACT.Copy, scale=scale).then_inc(bias_set, 1)
            for m in range(KD):
                act.wait_ge(kv_mm, m + 1)
                for h in range(4):
                    q = slice(h * HD, (h + 1) * HD)
                    dst = kblk[q, :, m, h * SK:(h + 1) * SK]
                    src = ps[q, m, 0:B * SK].rearrange("p (b s) -> p b s", b=B)
                    if biased:
                        i = act.activation(dst, src, ACT.Identity, bias=bias[q, 1, m:m + 1])
                    else:
                        i = act.activation(dst, src, ACT.Copy)
                i.then_inc(kv_set, 1)
            if biased:
                act.wait_ge(bias_set, 1)

            def keep_q(c, p, m):
                if m == 0:
                    act.wait_ge(*s_mm(c - 2))
                act.wait_ge(*q_mm(c, m + 1))
                if biased:
                    i = act.activation(qT[:, p, m, :], ps[:, 6 + m % 2, :], ACT.Identity, bias=bias[:, 2, m:m + 1], scale=scale)
                else:
                    i = act.activation(qT[:, p, m, :], ps[:, 6 + m % 2, :], ACT.Copy, scale=scale)
                i.then_inc(q_done.sem, 1)

            def first():
                f.keep(act, 0, 0, q_mm(-2), nb=1)
                for m in range(KD):
                    keep_q(0, 0, m)

            def main(c, p, more):
                for u in range(STEPS):
                    v = u - LT
                    if 0 <= v < U:
                        act.wait_ge(*p_mm(c, v + 1))
                        act.wait_ge(*pv_mm(c, v - 1))
                        act.activation(pT[:, v % 2].rearrange("s (b h) t -> s b h t", b=2),
                                       ps[0:SK, 2:4, :].rearrange("s b (h t) -> s b h t", h=4),
                                       ACT.Copy).then_inc(pT_done.sem, 1)
                    if u < U:
                        act.wait_ge(*sub_done(c, u + 1))
                        act.activation(s_sb[:, u % 4], s_sb[:, u % 4], ACT.Exp).then_inc(exp_done.sem, 1)
                    if more and LF <= u < LF + TJ:
                        if u == LF:
                            act.wait_ge(*q_mm(c - 1))
                        f.keep_tile(act, c + 1, 1 - p, u - LF, nb=1)
                    for m in range(KD):
                        if more and u == q_steps[m]:
                            keep_q(c + 1, 1 - p, m)
                    if wo is not None and u >= 6 and u % 2 == 0 and (u - 6) // 2 < TJ:
                        j = (u - 6) // 2
                        act.wait_ge(*oT_mm(c, j + 1))
                        act.wait_ge(*wo_mm(c, j - 1))
                        act.activation(oT[:, j % 2], ps[:, 5, :].rearrange("p (k t) -> p k t", k=KD), ACT.Copy).then_inc(oT_done.sem, 1)

            over_whole(act, NC, first, main)

        @block.tensor
        def _(pe):
            for s in (f.tp_done, q_mm, s_mm, p_mm, pv_mm) + ((oT_mm, wo_mm) if wo is not None else ()):
                s.start(pe)
            pe.wait_ge(consts_in, 16 * loads)
            for m in range(KD):
                for k in range(KD):
                    i = pe.matmul(ps[:, m, 0:B * SK], wk_s[:, k, m * P:(m + 1) * P], ctxT[:, k, :], start=k == 0, stop=k == KD - 1)
                i.then_inc(kv_mm, 1)
            for b in range(B):
                for k in range(KD):
                    i = pe.matmul(ps[0:SK, 4 + b, :], ctxT[:, k, b * SK:(b + 1) * SK], wv_s[:, k, :], start=k == 0, stop=k == KD - 1)
                i.then_inc(kv_mm, 1)
            pe.wait_ge(kv_set, KD + B)

            def project_q(c, p, m):
                if m == 0:
                    pe.wait_ge(*f.xT_done(c))
                if m >= 2:
                    pe.wait_ge(*q_done(c, m - 1))
                elif wo is not None:
                    pe.wait_ge(*y_done(c - 2))
                else:
                    pe.wait_ge(*q_done(c - 1))
                for k in range(KD):
                    i = pe.matmul(ps[:, 6 + m % 2, :], wq_s[:, k, m * P:(m + 1) * P], f.xT[:, p, k, :], start=k == 0, stop=k == KD - 1)
                i.then_inc(q_mm.sem, 1)

            def first():
                f.turn(pe, 0, 0, ident, nb=1)
                for m in range(KD):
                    project_q(0, 0, m)

            def main(c, p, more):
                b = c // CB
                pe.wait_ge(*q_done(c))
                for u in range(STEPS):
                    if u < U:
                        j, half = u // 2, u % 2
                        pe.wait_ge(*add_done(c, u))
                        for mm in range(2):
                            m = 2 * half + mm
                            i = pe.matmul(ps[:, mm, 0:W4], qT[:, p, m, j * P:(j + 1) * P], pick(kblk, b)[:, m, :], start=True, stop=True)
                        i.then_inc(s_mm.sem, 1)
                    v = u - LT
                    if 0 <= v < U:
                        pe.wait_ge(*exp_done(c, v + 1))
                        pe.wait_ge(*pT_done(c, v))
                        for h in range(HB):
                            i = pe.transpose(ps[0:SK, 2 + h // 4, (h % 4) * P:(h % 4 + 1) * P], s_sb[:, v % 4, h, :], ident[:, :])
                        i.then_inc(p_mm.sem, 1)
                    if more and LF <= u < LF + TJ:
                        if u == LF and wo is not None:
                            pe.wait_ge(*oT_done(c - 1))
                        f.turn_tile(pe, c + 1, 1 - p, u - LF, ident, nb=1)
                    v = u - LV
                    if 0 <= v < U:
                        pe.wait_ge(*pT_done(c, v + 1))
                        pe.wait_ge(*o_done(c, v))
                        for h in range(HB):
                            i = pe.matmul(ps[:, 4, h * (HD + 1):(h + 1) * (HD + 1)], pT[:, v % 2, h, :],
                                          pick(v1, b)[:, (v % 2) * HB + h, :], start=True, stop=True)
                        i.then_inc(pv_mm.sem, 1)
                    for m in range(KD):
                        if more and u == q_steps[m]:
                            project_q(c + 1, 1 - p, m)
                    if wo is not None and u >= 8 and u % 2 == 0 and (u - 8) // 2 < TJ:
                        j = (u - 8) // 2
                        pe.wait_ge(*oT_done(c, j + 1))
                        if j >= 2:
                            pe.wait_ge(*y_done(c, j - 1))
                        elif more:
                            pe.wait_ge(*q_done(c + 1))
                        for k in range(KD):
                            i = pe.matmul(ps[:, 6 + j % 2, :], oT[:, j % 2, k, :], wo_s[:, k, :], start=k == 0, stop=k == KD - 1)
                        i.then_inc(wo_mm.sem, 1)
                    if wo is not None and u >= 6 and u % 2 == 0 and (u - 6) // 2 < TJ:
                        j = (u - 6) // 2
                        pe.wait_ge(*o_done(c, 2 * j + 2))
                        if j:
                            pe.wait_ge(*oT_done(c, j))
                        elif more:
                            pe.wait_ge(*f.xT_done(c + 1))
                        for k in range(KD):
                            i = pe.transpose(ps[:, 5, k * P:(k + 1) * P], o[:, p, j, k * P:(k + 1) * P], ident[:, :])
                        i.then_inc(oT_mm.sem, 1)

            over_whole(pe, NC, first, main)


def stage_ffn(nc, tag, x_in, x_out, ident_d, qw, scT, la, lbT, bias, gamma, beta, first, add_to=None):
    R = la.shape[1]
    with Stage(nc, tag) as st:
        ps = st.banks()
        ident = st.sb("ident", [P, P])
        w = st.sb("w", [P, 2, KD, D])
        qi = st.sb("qi", [P, KD, D], I32)
        sc = st.sb("sc", [P, KD, D])
        la_s = st.sb("la", [R, 2, D])
        lb_s = st.sb("lb", [R, 2, D])
        b0 = st.sb("b0", [P, D])
        b1 = st.sb("b1", [P, D])
        gam = st.sb("gam", [P, KD])
        bet = st.sb("bet", [P, KD])
        y = st.sb("y", [P, TJ, D])
        gT = st.sb("gT", [P, 2, KD, P])
        out = st.sb("out", [P, 2, TJ, D])
        r = st.sb("r", [P, TJ, D]) if add_to is not None else None
        bn = st.sb("bn2", [P, TJ, 6])
        mv = st.sb("mv2", [P, TJ, 2])
        rs = st.sb("rs2", [P, TJ])
        f = Front(st, ps, 6, x_in, norm=first)
        consts_in = st.sem("consts_in")
        q_in = st.sem("q_in")
        lora_mm = st.sem("lora_mm")
        deq_done = st.sem("deq_done")
        scaled = st.sem("scaled")
        w_done = st.sem("w_done")
        r_in = st.sem("r_in")
        y_mm = st.count("y_mm", TJ)
        y_done = st.count("y_done", TJ)
        bn_done = st.count("bn_done2", TJ)
        mv_done = st.count("mv_done2", TJ)
        var_done = st.count("var_done2", TJ)
        rs_done = st.count("rs_done2", TJ)
        z_done = st.count("z_done", TJ)
        gT_mm = st.count("gT_mm", TJ)
        gT_done = st.count("gT_done", TJ)
        hb_done = st.count("hb_done", 1)
        hr_done = st.count("hr_done", 1)
        o_mm = st.count("o_mm", TJ)
        o_done = st.count("o_done", TJ)
        stored = [st.sem("stored0"), st.sem("stored1")]
        NCONST = 7
        block = st.ctx.enter_context(nc.Block())
        row = lambda v, n: v.rearrange("(o n) -> o n", o=1).to_broadcast([P, n])
        base_done = hb_done if add_to is None else hr_done

        @block.sync
        def _(sp):
            sp.dma_start(la_s[:, :, :], la.rearrange("i r d -> r i d")).then_inc(consts_in, 16)
            sp.dma_start(lb_s[:, :, :], lbT.rearrange("i r d -> r i d")).then_inc(consts_in, 16)
            sp.dma_start(ident[:, :], ident_d).then_inc(consts_in, 16)
            for dst, v in ((b0, bias[0]), (b1, bias[1])):
                sp.dma_start(dst[:, :], row(v, D)).then_inc(consts_in, 16)
            for dst, v in ((gam, gamma), (bet, beta)):
                sp.dma_start(dst[:, :], v.rearrange("(k p) -> p k", p=P), allow_slow_non_contiguous=True).then_inc(consts_in, 16)
            f.load(sp, 0, 0)
            for i in range(2):
                if i:
                    sp.wait_ge(scaled, 1)
                sp.dma_start(qi[:, :, :], weight_view(qw[i])).then_inc(q_in, 16)
                for k in range(KD):
                    sp.dma_start(sc[:, k, :], scT[i][8 * k:8 * k + 8, :].unsqueeze(1).to_broadcast([8, 16, D])).then_inc(q_in, 16)

            def load_r(c):
                if add_to is not None:
                    sp.wait_ge(*hr_done(c - 1))
                    st.plain(sp)
                    sp.dma_start(r[:, :, :], chunk_rows(add_to, c)).then_inc(r_in, 16)

            def start():
                f.load(sp, 1, 1)
                load_r(0)

            def main(c, p, more):
                if more > 1:
                    if first:
                        sp.wait_ge(*f.xn_done(c))
                    else:
                        sp.wait_ge(*f.tp_done(c))
                        st.plain(sp)
                        sp.wait_ge(*hb_done(c))
                    f.load(sp, c + 2, p)
                if more:
                    load_r(c + 1)
                sp.wait_ge(*o_done(c))
                st.plain(sp)
                sp.dma_start(chunk_rows(x_out, c), out[:, p]).then_inc(stored[p], 16)

            over_whole(sp, NC, start, main)
            for p in range(2):
                sp.wait_ge(stored[p], 16 * (NC // 2))

        @block.gpsimd
        def _(pool):
            f.start_pool(pool)
            for s in (var_done, rs_done, hb_done, hr_done):
                s.start(pool)
            pool.wait_ge(consts_in, 16 * NCONST)
            pool.wait_ge(f.half_set, 1)

            def rstd(c, j):
                pool.wait_ge(*mv_done(c, j + 1))
                pool.wait_ge(*z_done(c - 1, j + 1))
                st.plain(pool)
                pool.tensor_scalar(rs[:, j:j + 1], mv[:, j, 1:2], EPS, None, ALU.add).then_inc(var_done.sem, 1)
                pool.wait_ge(*var_done(c, j + 1))
                pool.tensor_tensor(rs[:, j:j + 1], rs[:, j:j + 1], f.half[:, 0:1], ALU.pow).then_inc(rs_done.sem, 1)

            def base(c, p):
                if first:
                    pool.wait_ge(*f.xn_done(c))
                else:
                    pool.wait_ge(*f.x_ready(c, p))
                pool.wait_ge(stored[p], (c - p) * 8)
                pool.tensor_tensor(out[:, p], f.xn[:, p], b1[:, :].unsqueeze(1).to_broadcast([P, TJ, D]), ALU.add).then_inc(hb_done.sem, 1)
                if add_to is not None:
                    pool.wait_ge(r_in, c * 16 + 16)
                    pool.wait_ge(*hb_done(c))
                    pool.tensor_tensor(out[:, p], out[:, p], r[:, :, :], ALU.add).then_inc(hr_done.sem, 1)

            def start():
                if first:
                    f.rstd(pool, 0, 0)
                    f.rstd(pool, 1, 1)
                base(0, 0)
                for j in range(TJ):
                    rstd(0, j)

            def main(c, p, more):
                for j in range(1, TJ + 1):
                    if more:
                        rstd(c + 1, j - 1)
                    if more > 1 and first and j == 2:
                        f.rstd(pool, c + 2, p)
                if more:
                    base(c + 1, 1 - p)

            over_whole(pool, NC, start, main)

        @block.vector
        def _(dve):
            f.start_dve(dve)
            for s in (y_done, bn_done, mv_done, z_done, o_done):
                s.start(dve)
            dve.wait_ge(consts_in, 16 * NCONST)

            def dequantise(i, lora):
                dve.wait_ge(q_in, 16 * (1 + KD) * (i + 1))
                dve.tensor_scalar(w[:, i], qi[:, :, :], 1.0 / 7.5, -1.0, ALU.mult, ALU.add).then_inc(deq_done, 1)
                dve.wait_ge(deq_done, i + 1)
                dve.tensor_tensor(w[:, i], w[:, i], sc[:, :, :], ALU.mult).then_inc(scaled, 1)
                dve.wait_ge(scaled, i + 1)
                dve.wait_ge(lora_mm, i + 1)
                dve.tensor_tensor(w[:, i], w[:, i], lora, ALU.add).then_inc(w_done, 1)

            def moments(c, j):
                dve.wait_ge(*y_mm(c, j + 1))
                dve.wait_ge(*gT_mm(c - 1, j + 1))
                dve.tensor_tensor(y[:, j, :], ps[:, j % 2, :], b0[:, :], ALU.add).then_inc(y_done.sem, 1)
                dve.wait_ge(*y_done(c, j + 1))
                dve.bn_stats(bn[:, j, :], y[:, j, :]).then_inc(bn_done.sem, 1)
                dve.wait_ge(*bn_done(c, j + 1))
                dve.wait_ge(*var_done(c - 1, j + 1))
                st.plain(dve)
                dve.bn_aggr(mv[:, j, :], bn[:, j, :]).then_inc(mv_done.sem, 1)

            def normal(c, j):
                dve.wait_ge(*rs_done(c, j + 1))
                dve.tensor_scalar(y[:, j, :], y[:, j, :], mv[:, j, 0:1], rs[:, j:j + 1],
                                  ALU.subtract, ALU.mult).then_inc(z_done.sem, 1)

            def start():
                if first:
                    f.stats(dve, 0, 0)
                    f.normalise(dve, 0, 0)
                dequantise(0, ps[:, 0:KD, :])
                if first:
                    f.stats(dve, 1, 1)
                    f.normalise(dve, 1, 1)
                for j in range(TJ):
                    moments(0, j)
                    normal(0, j)
                dequantise(1, ps[:, 2:2 + KD, :])

            def main(c, p, more):
                for j in range(1, TJ + 1):
                    if more:
                        moments(c + 1, j - 1)
                    if more > 1 and first and j == 2:
                        f.stats(dve, c + 2, p)
                    dve.wait_ge(*o_mm(c, j))
                    if j == 1:
                        dve.wait_ge(*base_done(c))
                    dve.tensor_tensor(out[:, p, j - 1, :], ps[:, 4 + (j - 1) % 2, :], out[:, p, j - 1, :],
                                      ALU.add).then_inc(o_done.sem, 1)
                    if more:
                        normal(c + 1, j - 1)
                    if more > 1 and first and j > 2:
                        for t in (2 * j - 6, 2 * j - 5):
                            f.normalise_tile(dve, c + 2, p, t, [hb_done(c)])

            over_whole(dve, NC, start, main)

        @block.scalar
        def _(act):
            for s in (f.xT_done, gT_done):
                s.start(act)
            act.wait_ge(consts_in, 16 * NCONST)

            def main(c, p, more):
                for j in range(TJ):
                    if more:
                        if j == 0:
                            act.wait_ge(*y_mm(c - 1))
                        f.keep_tile(act, c + 1, 1 - p, j)
                    act.wait_ge(*gT_mm(c, j + 1))
                    act.wait_ge(*o_mm(c, j - 1))
                    for k in range(KD):
                        i = act.activation(gT[:, j % 2, k, :], ps[:, 2 + j % 2, k * P:(k + 1) * P], ACT.Gelu,
                                           bias=bet[:, k:k + 1], scale=gam[:, k:k + 1])
                    i.then_inc(gT_done.sem, 1)

            over_whole(act, NC, lambda: f.keep(act, 0, 0, y_mm(-2)), main)

        @block.tensor
        def _(pe):
            for s in (f.tp_done, y_mm, gT_mm, o_mm):
                s.start(pe)
            pe.wait_ge(consts_in, 16 * NCONST)

            def lora(i, bank):
                for k in range(KD):
                    m = pe.matmul(ps[:, bank + k, :], la_s[:, i, k * P:(k + 1) * P], lb_s[:, i, :], start=True, stop=True)
                m.then_inc(lora_mm, 1)

            def product0(c, p, j):
                pe.wait_ge(*f.xT_done(c, j + 1))
                pe.wait_ge(*y_done(c, j - 1))
                for k in range(KD):
                    i = pe.matmul(ps[:, j % 2, :], f.xT[:, p, k, j * P:(j + 1) * P], w[:, 0, k, :], start=k == 0, stop=k == KD - 1)
                i.then_inc(y_mm.sem, 1)

            def start():
                lora(0, 0)
                f.turn(pe, 0, 0, ident)
                pe.wait_ge(w_done, 1)
                lora(1, 2)
                for j in range(TJ):
                    product0(0, 0, j)
                pe.wait_ge(w_done, 2)

            def main(c, p, more):
                for j in range(TJ + 1):
                    if j < TJ:
                        if more:
                            f.turn_tile(pe, c + 1, 1 - p, j, ident)
                        pe.wait_ge(*z_done(c, j + 1))
                        pe.wait_ge(*gT_done(c, j - 1))
                        for k in range(KD):
                            i = pe.transpose(ps[:, 2 + j % 2, k * P:(k + 1) * P], y[:, j, k * P:(k + 1) * P], ident[:, :])
                        i.then_inc(gT_mm.sem, 1)
                    if j:
                        pe.wait_ge(*gT_done(c, j))
                        pe.wait_ge(*o_done(c, j - 2))
                        for k in range(KD):
                            i = pe.matmul(ps[:, 4 + (j - 1) % 2, :], gT[:, (j - 1) % 2, k, :], w[:, 1, k, :], start=k == 0, stop=k == KD - 1)
                        i.then_inc(o_mm.sem, 1)
                        if more:
                            product0(c + 1, 1 - p, j - 1)

            over_whole(pe, NC, start, main)




def stage_project(nc, tag, x_in, outs, ident_d, ws, biases):
    M = len(ws)
    with Stage(nc, tag) as st:
        ps = st.banks()
        ident = st.sb("ident", [P, P])
        w = st.sb("w", [P, M, KD, D])
        bias = st.sb("bias", [P, M, D])
        y = st.sb("y", [P, 2, M, TJ, D])
        f = Front(st, ps, 6, x_in)
        consts_in = st.sem("consts_in")
        y_mm = st.count("y_mm", M * TJ)
        y_done = st.count("y_done", M * TJ)
        stored = st.count("stored", M, 16)
        block = st.ctx.enter_context(nc.Block())

        @block.sync
        def _(sp):
            stored.start(sp)
            for i in range(M):
                sp.dma_start(w[:, i], weight_view(ws[i])).then_inc(consts_in, 16)
                sp.dma_start(bias[:, i], biases[i].rearrange("(o n) -> o n", o=1).to_broadcast([P, D])).then_inc(consts_in, 16)
            sp.dma_start(ident[:, :], ident_d).then_inc(consts_in, 16)

            def front(c, p):
                sp.wait_ge(*f.xn_done(c - 2))
                f.load(sp, c, p)

            def main(c, p):
                for i in range(M):
                    sp.wait_ge(*y_done(c, (i + 1) * TJ))
                    st.plain(sp)
                    sp.dma_start(chunk_rows(outs[i], c), y[:, p, i]).then_inc(stored.sem, 16)

            over_chunks(sp, NC, front, main)
            sp.wait_ge(*stored(NC - 1))

        @block.gpsimd
        def _(pool):
            f.start_pool(pool)
            over_chunks(pool, NC, lambda c, p: f.rstd(pool, c, p), None)

        @block.vector
        def _(dve):
            f.start_dve(dve)
            y_done.start(dve)
            dve.wait_ge(consts_in, 16 * (2 * M + 1))

            def front(c, p):
                f.stats(dve, c, p)
                f.normalise(dve, c, p)

            def main(c, p):
                dve.wait_ge(*stored(c - 2))
                for u in range(M * TJ):
                    dve.wait_ge(*y_mm(c, u + 1))
                    dve.tensor_tensor(y[:, p, u // TJ, u % TJ, :], ps[:, u % 4, :], bias[:, u // TJ, :], ALU.add).then_inc(y_done.sem, 1)

            over_chunks(dve, NC, front, main)

        @block.scalar
        def _(act):
            f.xT_done.start(act)
            over_chunks(act, NC, lambda c, p: f.keep(act, c, p, y_mm(c - 2)), None)

        @block.tensor
        def _(pe):
            f.tp_done.start(pe)
            y_mm.start(pe)
            pe.wait_ge(consts_in, 16 * (2 * M + 1))

            def main(c, p):
                pe.wait_ge(*f.xT_done(c))
                for u in range(M * TJ):
                    pe.wait_ge(*y_done(c, u - 3))
                    for k in range(KD):
                        i = pe.matmul(ps[:, u % 4, :], f.xT[:, p, k, (u % TJ) * P:(u % TJ + 1) * P], w[:, u // TJ, k, :],
                                      start=k == 0, stop=k == KD - 1)
                    i.then_inc(y_mm.sem, 1)

            over_chunks(pe, NC, lambda c, p: f.turn(pe, c, p, ident), main)


SEG = 1024
QUAD = [-2.0 * float(np.cos((2 * g + 1) * np.pi / 8)) for g in range(4)]


def transform_tables():
    n = np.arange(512)
    fwd, inv = [], []
    for g in range(4):
        theta = 2 * np.pi * (g + 8 * np.arange(256) + 0.5) / 2048
        c, s = np.cos(np.outer(n, theta)), np.sin(np.outer(n, theta))
        fwd.append(np.concatenate([c, -s], 1))
        inv.append(np.concatenate([c, -s], 1).T / 1024)
    return np.stack(fwd).astype(np.float32), np.stack(inv).astype(np.float32)


def stage_conv(nc, k_in, v_in, y_out, kkT, ssT, kd, dd, fwd_d, inv_d):
    CW = 256
    NH = D // CW
    TS = SEG // P
    ORDER = [0, 3, 1, 2]
    SIGN = [1.0, -1.0, 1.0, -1.0]
    STEPS = 16
    with Stage(nc, "cv") as st:
        ps = st.banks()
        fwd = st.sb("fwd", [P, 4, 4, 512])
        inv = st.sb("inv", [P, 4, 4, 512])
        hat = st.sb("hat", [P, 2, 4, 4, CW])
        prev = st.sb("prev", [P, 4, 4, CW])
        kb = st.sb("kb", [P, 2, TS, CW])
        vb = st.sb("vb", [P, 2, TS, CW])
        acc = st.sb("acc", [P, 2, TS, CW])
        gain = st.sb("gain", [P, 2, CW])
        e = st.sb("e", [P, 2, CW])
        ff = st.sb("ff", [P, 2, CW])
        r = st.sb("r", [P, 2, 4, CW])
        zb = st.sb("z", [P, 2, 4, CW])
        yb = st.sb("y", [P, 2, 4, CW])
        q = st.sb("q", [P, 4, CW])
        x = st.sb("x", [P, 4, CW])
        tab_in = st.sem("tab_in")
        gain_in = st.sem("gain_in")
        k_ld = [st.sem("k_ld0"), st.sem("k_ld1")]
        v_ld = [st.sem("v_ld0"), st.sem("v_ld1")]
        ef_done = st.count("ef_done", 3)
        res_done = st.count("res_done", 1)
        r0_done = st.sem("r0_done")
        fwd_mm = st.count("fwd_mm", 1)
        kept = st.count("kept", 1)
        z_done = st.count("z_done", 1, lead=3)
        q_done = st.count("q_done", 1)
        x_done = st.count("x_done", 1)
        yr_done = st.count("yr_done", 1)
        y_done = st.count("y_done", 1)
        inv_mm = st.count("inv_mm", 1)
        part = st.count("part", 4)
        last = st.count("last", 1)
        gained = st.count("gained", 1)
        summed = st.count("summed", 1)
        post = st.count("post", 4)
        y_st = [st.count("y_st0", 1, 16), st.count("y_st1", 1, 16)]
        block = st.ctx.enter_context(nc.Block())

        def seg_view(t, b, s, hh):
            v = t.rearrange("(b s j p) (h d) -> p b s h j d", b=B, s=2, p=P, h=NH)
            return v[:, bass.ds(b, 1), s, bass.ds(hh, 1)].rearrange("p b h j d -> p (b h j) d")

        def kernel_view(t, hh):
            return t.rearrange("(j p) (h d) -> p h j d", p=P, h=NH)[:, bass.ds(hh, 1)].rearrange("p h j d -> p (h j) d")

        batch = lambda hh, b: hh * B + b
        fstep = lambda hh, b, n: hh * (8 + B * STEPS) + (b * STEPS + 8 + n) if b is not None else hh * (8 + B * STEPS) + n
        tstep = lambda hh, b, n: batch(hh, b) * STEPS + n
        kstep = lambda hh, b, n: hh * (8 + B * 8) + (b * 8 + 8 + (n // 8) * 4 + n % 4) if b is not None else hh * (8 + B * 8) + n
        zstep = lambda hh, b, n: batch(hh, b) * 8 + ((n // 8) * 4 + n % 4)
        item = lambda hh, b, m: hh * (2 + B * 4) + (b * 4 + 2 + m) if b is not None else hh * (2 + B * 4) + m

        @block.sync
        def _(sp):
            for dst, src in ((fwd, fwd_d), (inv, inv_d)):
                for g in range(4):
                    sp.dma_start(dst[:, g], weight_view(src[g])).then_inc(tab_in, 16)
            with sp.Fori(0, NH) as hh:
                for i, t in enumerate((kkT, ssT)):
                    sp.wait_ge(*post(batch(hh, -1)))
                    st.plain(sp)
                    sp.dma_start(vb[:, i], kernel_view(t, hh)).then_inc(v_ld[i], 16)
                for i, t in enumerate((kd, dd)):
                    sp.dma_start(gain[:, i], t.rearrange("(h o d) -> h o d", h=NH, o=1)[bass.ds(hh, 1)]
                                 .rearrange("h o d -> (h o) d").to_broadcast([P, CW])).then_inc(gain_in, 16)
                with sp.Fori(0, B) as b:
                    for s in range(2):
                        sp.wait_ge(*post(batch(hh, b) - 1, 3 + s))
                        st.plain(sp)
                        sp.dma_start(kb[:, s], seg_view(k_in, b, s, hh)).then_inc(k_ld[s], 16)
                    for s in range(2):
                        sp.wait_ge(*post(batch(hh, b) - 1, 1 + s))
                        st.plain(sp)
                        sp.wait_ge(*res_done(fstep(hh, None, 4 * s + 3)))
                        st.plain(sp)
                        sp.dma_start(vb[:, s], seg_view(v_in, b, s, hh)).then_inc(v_ld[s], 16)

        @block.scalar
        def _(act):
            kept.start(act)
            for c in y_st:
                c.start(act)

            def keep(dst, f, n):
                act.wait_ge(*fwd_mm(f))
                act.activation(dst, ps[:, 2 * (n % 2):2 * (n % 2) + 2, :].rearrange("p b (m d) -> p (b m) d", m=2),
                               ACT.Copy).then_inc(kept.sem, 1)

            with act.Fori(0, NH) as hh:
                act.wait_ge(*y_done(tstep(hh, 0, -1)))
                for n in range(8):
                    keep(hat[:, n // 4, ORDER[n % 4]], fstep(hh, None, n), n)
                with act.Fori(0, B) as b:
                    for n in range(STEPS):
                        if (n // 4) % 2 == 0:
                            act.wait_ge(*z_done(zstep(hh, b, n) - 4))
                            act.wait_ge(*y_done(tstep(hh, b, n) - 1))
                            keep(prev[:, ORDER[n % 4]], fstep(hh, b, n), n)
                    for s in range(2):
                        act.wait_ge(*post(batch(hh, b), 3 + s))
                        act.dma_start(seg_view(y_out, b, s, hh), acc[:, s]).then_inc(y_st[s].sem, 16)
            for s in range(2):
                act.wait_ge(*y_st[s](NH * B - 1))

        @block.tensor
        def _(pe):
            for c in (fwd_mm, inv_mm):
                c.start(pe)
            pe.wait_ge(tab_in, 16 * 8)

            def forward(f, n, free):
                pe.wait_ge(*res_done(f))
                for w in free:
                    pe.wait_ge(*w)
                for m in range(4):
                    for k in range(4):
                        i = pe.matmul(ps[:, 2 * (n % 2) + m // 2, (m % 2) * CW:(m % 2 + 1) * CW],
                                      fwd[:, ORDER[n % 4], k, m * P:(m + 1) * P], r[:, n % 2, k, :], start=k == 0, stop=k == 3)
                i.then_inc(fwd_mm.sem, 1)

            def inverse(t, n):
                pe.wait_ge(*y_done(t))
                pe.wait_ge(*part(t - 2))
                for m in range(4):
                    for k in range(4):
                        i = pe.matmul(ps[:, 4 + 2 * (n % 2) + m // 2, (m % 2) * CW:(m % 2 + 1) * CW],
                                      inv[:, ORDER[n % 4], k, m * P:(m + 1) * P], yb[:, n % 2, k, :], start=k == 0, stop=k == 3)
                i.then_inc(inv_mm.sem, 1)

            def free_of(hh, b, n):
                if n < 2:
                    return [kept(kstep(hh, b, 0) - 1), z_done(zstep(hh, b, 0) - 1)]
                n -= 2
                return [kept(kstep(hh, b, n))] if (n // 4) % 2 == 0 else [z_done(zstep(hh, b, n))]

            with pe.Fori(0, NH) as hh:
                for n in range(8):
                    forward(fstep(hh, None, n), n, [kept(kstep(hh, None, n - 2)) if n >= 2 else z_done(zstep(hh, 0, 0) - 1)])
                with pe.Fori(0, B) as b:
                    forward(fstep(hh, b, 0), 0, free_of(hh, b, 0))
                    for n in range(STEPS):
                        if n + 1 < STEPS:
                            forward(fstep(hh, b, n + 1), n + 1, free_of(hh, b, n + 1))
                        inverse(tstep(hh, b, n), n)

        @block.vector
        def _(dve):
            for c in (ef_done, res_done, z_done, q_done, yr_done, y_done, part, last):
                c.start(dve)

            def residue(src, ready, i, f, n):
                gi = n % 4
                a = QUAD[ORDER[gi]]
                xq = [src[:, 2 * m:2 * m + 2, :] for m in range(4)]
                if gi % 2 == 0:
                    dve.wait_ge(*res_done(f - 1))
                if gi == 0:
                    for w in ready:
                        dve.wait_ge(*w)
                    dve.tensor_tensor(e[:, :, :], xq[0], xq[2], ALU.subtract).then_inc(ef_done.sem, 1)
                if gi % 2 == 0:
                    dve.scalar_tensor_tensor(ff[:, :, :], xq[3], a * a - 1.0, xq[1], ALU.mult, ALU.add).then_inc(ef_done.sem, 1)
                dve.wait_ge(*ef_done(i, 2 + gi // 2))
                dve.wait_ge(*fwd_mm(f - 2))
                dve.scalar_tensor_tensor(r[:, n % 2, 0:2], xq[3], a, e[:, :, :], ALU.mult, ALU.add).then_inc(r0_done, 1)
                dve.scalar_tensor_tensor(r[:, n % 2, 2:4], xq[2], -a, ff[:, :, :], ALU.mult, ALU.add).then_inc(res_done.sem, 1)

            def spectrum(hh, b, n):
                g, conv, seg = ORDER[n % 4], n // 8, (n // 4) % 2
                t = tstep(hh, b, n)
                if seg == 0:
                    z = prev[:, g]
                    dve.wait_ge(*kept(kstep(hh, b, n)))
                else:
                    z = zb[:, n % 2]
                    d = ps[:, 2 * (n % 2):2 * (n % 2) + 2, :].rearrange("p b (m d) -> p b m d", m=2)
                    dve.wait_ge(*fwd_mm(fstep(hh, b, n)))
                    dve.wait_ge(*x_done(t - 2))
                    re = (ALU.subtract, ALU.add) if SIGN[g] > 0 else (ALU.add, ALU.subtract)
                    dve.tensor_tensor(z[:, 0:2], d[:, 0], prev[:, g, 2:4], re[0]).then_inc(r0_done, 1)
                    dve.tensor_tensor(z[:, 2:4], d[:, 1], prev[:, g, 0:2], re[1]).then_inc(z_done.sem, 1)
                    dve.wait_ge(*z_done(zstep(hh, b, n)))
                dve.wait_ge(*y_done(t - 1))
                dve.tensor_tensor(q[:, :, :], z, hat[:, conv, g], ALU.mult).then_inc(q_done.sem, 1)
                dve.wait_ge(*q_done(t))
                dve.wait_ge(*x_done(t))
                dve.wait_ge(*inv_mm(t - 2))
                dve.tensor_tensor(yb[:, n % 2, 0:2], q[:, 0:2], q[:, 2:4], ALU.subtract).then_inc(yr_done.sem, 1)
                dve.tensor_tensor(yb[:, n % 2, 2:4], x[:, 0:2], x[:, 2:4], ALU.add).then_inc(y_done.sem, 1)

            def sums(hh, b, n):
                gi, it = n % 4, n // 4
                a = QUAD[ORDER[gi]]
                t = tstep(hh, b, n)
                d = ps[:, 4 + 2 * (n % 2):6 + 2 * (n % 2), :].rearrange("p b (m d) -> p (b m) d", m=2)
                A, Bk, C = acc[:, it % 2, 0:4], acc[:, it % 2, 4:6], acc[:, it % 2, 6:8]
                dve.wait_ge(*inv_mm(t))
                if gi == 0:
                    if it >= 2:
                        dve.wait_ge(*post(batch(hh, b), it - 1))
                    else:
                        dve.wait_ge(*y_st[it](batch(hh, b) - 1))
                    dve.tensor_copy(A, d).then_inc(part.sem, 1)
                    dve.tensor_scalar(Bk, d[:, 2:4], -a, None, ALU.mult).then_inc(part.sem, 1)
                    dve.tensor_scalar(C, d[:, 0:2], a, None, ALU.mult).then_inc(part.sem, 1)
                else:
                    dve.wait_ge(*part(t - 1))
                    dve.tensor_tensor(A, d, A, ALU.add).then_inc(part.sem, 1)
                    dve.scalar_tensor_tensor(Bk, d[:, 2:4], -a, Bk, ALU.mult, ALU.add).then_inc(part.sem, 1)
                    dve.scalar_tensor_tensor(C, d[:, 0:2], a, C, ALU.mult, ALU.add).then_inc(part.sem, 1)
                dve.wait_ge(*part(t, 3))
                dve.scalar_tensor_tensor(C, d[:, 2:4], a * a - 1.0, C, ALU.mult, ALU.add).then_inc(part.sem, 1)
                if gi == 3:
                    dve.wait_ge(*part(t))
                    dve.tensor_tensor(Bk, Bk, acc[:, it % 2, 0:2], ALU.subtract).then_inc(last.sem, 1)

            with dve.Fori(0, NH) as hh:
                for n in range(8):
                    residue(vb[:, n // 4], [(v_ld[n // 4], hh * 48 + 16)], item(hh, None, n // 4), fstep(hh, None, n), n)
                with dve.Fori(0, B) as b:
                    def res(n):
                        m = n // 4
                        ready = [(k_ld[m], batch(hh, b) * 16 + 16)] if m < 2 else [post(batch(hh, b), m - 1)]
                        residue(kb[:, m % 2], ready, item(hh, b, m), fstep(hh, b, n), n)

                    res(0)
                    res(1)
                    spectrum(hh, b, 0)
                    for n in range(STEPS):
                        if n + 2 < STEPS:
                            res(n + 2)
                        if n + 1 < STEPS:
                            spectrum(hh, b, n + 1)
                        sums(hh, b, n)

        @block.gpsimd
        def _(pool):
            for c in (x_done, gained, summed, post):
                c.start(pool)
            xr_done = st.sem("xr_done")

            def cross(hh, b, n):
                g, conv, seg = ORDER[n % 4], n // 8, (n // 4) % 2
                t = tstep(hh, b, n)
                if seg == 0:
                    z = prev[:, g]
                    pool.wait_ge(*kept(kstep(hh, b, n)))
                else:
                    z = zb[:, n % 2]
                    pool.wait_ge(*z_done(zstep(hh, b, n)))
                pool.wait_ge(*y_done(t - 1))
                pool.tensor_tensor(x[:, 0:2], z[:, 0:2], hat[:, conv, g, 2:4], ALU.mult).then_inc(xr_done, 1)
                pool.tensor_tensor(x[:, 2:4], z[:, 2:4], hat[:, conv, g, 0:2], ALU.mult).then_inc(x_done.sem, 1)

            with pool.Fori(0, NH) as hh:
                pool.wait_ge(gain_in, hh * 32 + 32)
                st.plain(pool)
                with pool.Fori(0, B) as b:
                    for n in range(STEPS + 1):
                        if n < STEPS:
                            cross(hh, b, n)
                        if n % 4 == 0 and n:
                            m = n // 4 - 1
                            s = m % 2
                            nb = batch(hh, b)
                            pool.wait_ge(*last(nb * 4 + m))
                            kd_b = gain[:, m // 2].unsqueeze(1).to_broadcast([P, TS, CW])
                            pool.tensor_tensor(kb[:, s], kb[:, s], kd_b, ALU.mult).then_inc(gained.sem, 1)
                            pool.wait_ge(*gained(nb * 4 + m))
                            if m < 2:
                                pool.tensor_tensor(kb[:, s], kb[:, s], acc[:, s], ALU.add).then_inc(summed.sem, 1)
                                pool.wait_ge(*summed(nb * 2 + m))
                                pool.wait_ge(v_ld[s], nb * 16 + (hh * 16 + 32))
                                pool.tensor_tensor(kb[:, s], kb[:, s], vb[:, s], ALU.mult).then_inc(post.sem, 1)
                            else:
                                pool.tensor_tensor(acc[:, s], acc[:, s], kb[:, s], ALU.add).then_inc(post.sem, 1)


def stage_gated_out(nc, tag, x_in, y_in, q_in, x_out, ident_d, wo, bo):
    with Stage(nc, tag) as st:
        ps = st.banks()
        ident = st.sb("ident", [P, P])
        w = st.sb("w", [P, KD, D])
        bias = st.sb("bias", [P, D])
        qb = st.sb("q", [P, 2, TJ, D])
        xr = st.sb("xr", [P, 2, TJ, D])
        xb = st.sb("xb", [P, 2, TJ, D])
        out = st.sb("out", [P, 2, TJ, D])
        f = Front(st, ps, 6, y_in)
        consts_in = st.sem("consts_in")
        q_ld = [st.sem("q_ld0"), st.sem("q_ld1")]
        x_ld = [st.sem("x_ld0"), st.sem("x_ld1")]
        xb_done = st.count("xb_done", 1)
        o_mm = st.count("o_mm", TJ)
        o_done = st.count("o_done", TJ)
        stored = st.count("stored", 1, 16)
        block = st.ctx.enter_context(nc.Block())

        def landed(sem, c, p):
            return sem[p], 16 * (c // 2 + 1) if isinstance(c, int) else (c - p) * 8 + 16

        @block.sync
        def _(sp):
            stored.start(sp)
            sp.dma_start(w[:, :, :], weight_view(wo)).then_inc(consts_in, 16)
            sp.dma_start(bias[:, :], bo.rearrange("(o n) -> o n", o=1).to_broadcast([P, D])).then_inc(consts_in, 16)
            sp.dma_start(ident[:, :], ident_d).then_inc(consts_in, 16)

            def front(c, p):
                sp.wait_ge(*f.xn_done(c - 2))
                f.load(sp, c, p)
                sp.dma_start(qb[:, p], chunk_rows(q_in, c)).then_inc(q_ld[p], 16)
                sp.wait_ge(*xb_done(c - 2))
                st.plain(sp)
                sp.dma_start(xr[:, p], chunk_rows(x_in, c)).then_inc(x_ld[p], 16)

            def main(c, p):
                sp.wait_ge(*o_done(c))
                st.plain(sp)
                sp.dma_start(chunk_rows(x_out, c), out[:, p]).then_inc(stored.sem, 16)

            over_chunks(sp, NC, front, main)
            sp.wait_ge(*stored(NC - 1))

        @block.gpsimd
        def _(pool):
            xb_done.start(pool)
            pool.wait_ge(consts_in, 48)

            def main(c, p):
                pool.wait_ge(*landed(x_ld, c, p))
                pool.wait_ge(*o_done(c - 2))
                pool.tensor_tensor(xb[:, p], xr[:, p], bias[:, :].unsqueeze(1).to_broadcast([P, TJ, D]), ALU.add).then_inc(xb_done.sem, 1)

            over_chunks(pool, NC, None, main)

        @block.vector
        def _(dve):
            f.xn_done.start(dve)
            o_done.start(dve)

            def front(c, p):
                dve.wait_ge(*f.x_ready(c, p))
                dve.wait_ge(*landed(q_ld, c, p))
                dve.wait_ge(*f.tp_done(c - 2))
                for j in range(TJ):
                    dve.tensor_tensor(f.xn[:, p, j, :], f.x[:, p, j, :], qb[:, p, j, :], ALU.mult).then_inc(f.xn_done.sem, 1)

            def main(c, p):
                dve.wait_ge(*xb_done(c))
                dve.wait_ge(*stored(c - 2))
                for j in range(TJ):
                    dve.wait_ge(*o_mm(c, j + 1))
                    dve.tensor_tensor(out[:, p, j, :], ps[:, j % 2, :], xb[:, p, j, :], ALU.add).then_inc(o_done.sem, 1)

            over_chunks(dve, NC, front, main)

        @block.scalar
        def _(act):
            f.xT_done.start(act)
            over_chunks(act, NC, lambda c, p: f.keep(act, c, p, o_mm(c - 2)), None)

        @block.tensor
        def _(pe):
            f.tp_done.start(pe)
            o_mm.start(pe)
            pe.wait_ge(consts_in, 48)

            def main(c, p):
                pe.wait_ge(*f.xT_done(c))
                for j in range(TJ):
                    pe.wait_ge(*o_done(c, j - 1))
                    for k in range(KD):
                        i = pe.matmul(ps[:, j % 2, :], f.xT[:, p, k, j * P:(j + 1) * P], w[:, k, :], start=k == 0, stop=k == KD - 1)
                    i.then_inc(o_mm.sem, 1)

            over_chunks(pe, NC, lambda c, p: f.turn(pe, c, p, ident), main)


NE, FF = 64, 1024
NTL = N // P
SLOT_TILES = 2 * N // P + NE


def stage_route(nc, tag, x_in, xn_out, ident_d, gate, table, route_d, weight_d, expert_d, rows_d, consts):
    E3 = [P, NTL, NE]
    before_d, iota_d, steps_d, upto_d, tiles_d, token_d = consts
    with Stage(nc, tag) as st:
        ps = st.banks()
        ident = st.sb("ident", [P, P])
        gate_s = st.sb("gate", [P, KD, NE])
        f = Front(st, ps, 6, x_in)
        lg = st.sb("lg", E3)
        consts_in = st.sem("consts_in")
        l_mm = st.count("l_mm", TJ)
        l_done = st.count("l_done", TJ)
        stored = st.count("stored", 1, 16)

        before = st.sb("before", [P, P])
        ones = st.sb("ones", [P, P])
        iota = st.sb("iota", [P, NE])
        steps = st.sb("steps", [P, NTL])
        upto = st.sb("upto", [P, NE, NE])
        tiles = st.sb("tiles", [1, SLOT_TILES])
        token = st.sb("token", [P, NTL])
        t1 = st.sb("t1", [P, NE, NE])
        oh = st.sb("oh", [P, 2, NTL, NE])
        m = st.sb("m", [P, 2, NTL])
        ix = st.sb("ix", [P, NTL])
        dd = st.sb("dd", [P, NTL])
        ex = st.sb("ex", [P, NTL])
        den = st.sb("den", [P, NTL])
        wt = st.sb("wt", [P, 2, NTL])
        cum = st.sb("cum", [P, NTL + 1, NE])
        nt = st.sb("nt", [P, NE])
        end = st.sb("end", [P, NE])
        first = st.sb("first", [P, NE])
        slot_f = st.sb("slot_f", [P, 2, NTL])
        slot = st.sb("slot", [P, 2, NTL], U32)
        own_f = st.sb("own_f", [1, SLOT_TILES + 1])
        own = st.sb("own", [1, SLOT_TILES + 1 + NE], I32)
        zero = st.sb("zero", [P, D])
        cleared = st.sem("cleared")
        one_set = st.sem("one_set")
        step_done = st.sem("step_done")
        exp_done = st.sem("exp_done")
        rank_mm = st.sem("rank_mm")
        table_clear = st.sem("table_clear")
        scattered = st.sem("scattered")
        route_st = st.sem("route_st")
        STEPS_END = 39 + NTL
        block = st.ctx.enter_context(nc.Block())

        @block.sync
        def _(sp):
            stored.start(sp)
            sp.dma_start(gate_s[:, :, :], weight_view(gate)).then_inc(consts_in, 16)
            for dst, src in ((ident, ident_d), (before, before_d), (token, token_d), (tiles, tiles_d)):
                sp.dma_start(dst[:, :], src).then_inc(consts_in, 16)
            for dst, src in ((iota, iota_d), (steps, steps_d)):
                sp.dma_start(dst[:, :], src.to_broadcast([P, src.shape[1]])).then_inc(consts_in, 16)
            sp.dma_start(upto[:, :, :].rearrange("p a b -> p (a b)"), upto_d.to_broadcast([P, NE * NE])).then_inc(consts_in, 16)

            def front(c, p):
                sp.wait_ge(*f.xn_done(c - 2))
                f.load(sp, c, p)

            def main(c, p):
                sp.wait_ge(*f.xn_done(c))
                st.plain(sp)
                sp.dma_start(chunk_rows(xn_out, c), f.xn[:, p]).then_inc(stored.sem, 16)

            over_chunks(sp, NC, front, main)
            sp.wait_ge(one_set, 2)
            spare = SLOT_TILES - 2 * N // P
            sp.dma_start(rows_d[2 * N:, :].rearrange("(p a) d -> p a d", p=P),
                         zero[:, :].unsqueeze(1).to_broadcast([P, spare, D])).then_inc(cleared, 16)
            sp.dma_start(table.rearrange("(p t) o -> p (t o)", p=P), zero[:, 0:SLOT_TILES]).then_inc(table_clear, 16)
            sp.wait_ge(step_done, STEPS_END)
            sp.dma_start(route_d, slot[:, :, :]).then_inc(route_st, 16)
            sp.dma_start(weight_d, wt[:, :, :]).then_inc(route_st, 16)
            sp.dma_start(expert_d, own[:, :]).then_inc(route_st, 16)
            sp.wait_ge(route_st, 48)
            sp.wait_ge(cleared, 16)
            sp.wait_ge(*stored(NC - 1))

        @block.gpsimd
        def _(pool):
            f.start_pool(pool)
            pool.memset(ones[:, :], 1.0).then_inc(one_set, 1)
            pool.memset(zero[:, :], 0.0).then_inc(one_set, 1)
            over_chunks(pool, NC, lambda c, p: f.rstd(pool, c, p), None)
            pool.wait_ge(step_done, STEPS_END)
            pool.wait_ge(table_clear, 16)
            for i in range(2):
                for t in range(NTL):
                    pool.indirect_dma_start(out=table, out_offset=bass.IndirectOffsetOnAxis(ap=slot[:, i, t:t + 1], axis=0),
                                            in_=token[:, t:t + 1], in_offset=None).then_inc(scattered, 16)
            pool.wait_ge(scattered, 16 * 2 * NTL)

        @block.vector
        def _(dve):
            f.start_dve(dve)
            l_done.start(dve)
            dve.wait_ge(consts_in, 16 * 8)

            def front(c, p):
                f.stats(dve, c, p)
                f.normalise(dve, c, p, extra=[stored(c - 2)])

            def main(c, p):
                for j in range(TJ):
                    dve.wait_ge(*l_mm(c, j + 1))
                    dve.tensor_copy(lg[:, bass.ds(c * TJ + j, 1), :] if not isinstance(c, int) else lg[:, c * TJ + j:c * TJ + j + 1, :],
                                    ps[:, j % 2, 0:NE].unsqueeze(1)).then_inc(l_done.sem, 1)

            over_chunks(dve, NC, front, main)
            dve.wait_ge(*l_done(NC - 1))

            done = [0]

            def step(instruction):
                done[0] += 1
                instruction.then_inc(step_done, 1)
                dve.wait_ge(step_done, done[0])

            over_e = lambda a: a.unsqueeze(1).to_broadcast(E3)
            over_t = lambda a: a.unsqueeze(2).to_broadcast(E3)
            work = t1[:, 0:NTL, :]
            for i in range(2):
                step(dve.tensor_reduce(m[:, i], lg[:, :, :], AX.X, ALU.max))
                step(dve.tensor_tensor(work, lg[:, :, :], over_t(m[:, i]), ALU.is_ge))
                step(dve.tensor_tensor(work, work, over_e(iota[:, :]), ALU.mult))
                step(dve.tensor_reduce(ix[:, :], work, AX.X, ALU.min))
                step(dve.tensor_tensor(oh[:, i], over_e(iota[:, :]), over_t(ix[:, :]), ALU.is_equal))
                if i == 0:
                    step(dve.scalar_tensor_tensor(lg[:, :, :], oh[:, 0], -3e38, lg[:, :, :], ALU.mult, ALU.add))
            step(dve.tensor_tensor(dd[:, :], m[:, 1], m[:, 0], ALU.subtract))
            dve.wait_ge(exp_done, 1)
            step(dve.tensor_scalar(den[:, :], ex[:, :], 1.0, None, ALU.add))
            step(dve.reciprocal(wt[:, 0], den[:, :]))
            step(dve.tensor_tensor(wt[:, 1], ex[:, :], wt[:, 0], ALU.mult))
            step(dve.tensor_tensor(lg[:, :, :], oh[:, 0], oh[:, 1], ALU.add))
            step(dve.memset(cum[:, 0, :], 0.0))
            dve.wait_ge(rank_mm, 2)
            tot = ps[:, 4:8, :].rearrange("p b (t e) -> p (b t) e", e=NE)
            for t in range(NTL):
                step(dve.tensor_tensor(cum[:, t + 1, :], cum[:, t, :], tot[:, t, :], ALU.add))
            nw = t1[:, :, 0:NTL]
            step(dve.tensor_tensor(nw, cum[:, NTL, :].unsqueeze(2).to_broadcast([P, NE, NTL]),
                                   steps[:, :].unsqueeze(1).to_broadcast([P, NE, NTL]), ALU.is_gt))
            step(dve.tensor_reduce(nt[:, :], nw, AX.X, ALU.add))
            step(dve.tensor_tensor(t1[:, :, :], upto[:, :, :], nt[:, :].unsqueeze(1).to_broadcast([P, NE, NE]), ALU.mult))
            step(dve.tensor_reduce(end[:, :], t1[:, :, :], AX.X, ALU.add))
            step(dve.tensor_tensor(first[:, :], end[:, :], nt[:, :], ALU.subtract))
            step(dve.tensor_scalar(first[:, :], first[:, :], float(P), None, ALU.mult))
            pre = ps[:, 0:4, :].rearrange("p b (t e) -> p (b t) e", e=NE)
            step(dve.tensor_tensor(lg[:, :, :], pre, cum[:, 0:NTL, :], ALU.add))
            step(dve.tensor_tensor(lg[:, :, :], lg[:, :, :], over_e(first[:, :]), ALU.add))
            for i in range(2):
                step(dve.tensor_tensor(oh[:, i], oh[:, i], lg[:, :, :], ALU.mult))
                step(dve.tensor_reduce(slot_f[:, i], oh[:, i], AX.X, ALU.add))
            step(dve.tensor_copy(slot[:, :, :], slot_f[:, :, :]))
            for h in range(SLOT_TILES // NE):
                sl = slice(h * NE, (h + 1) * NE)
                step(dve.tensor_tensor(t1[0:1, :, :], tiles[0:1, sl].unsqueeze(2).to_broadcast([1, NE, NE]),
                                       end[0:1, :].unsqueeze(1).to_broadcast([1, NE, NE]), ALU.is_ge))
                step(dve.tensor_reduce(own_f[0:1, sl], t1[0:1, :, :], AX.X, ALU.add))
            step(dve.tensor_scalar(own_f[0:1, SLOT_TILES:], end[0:1, NE - 1:NE], float(P // 4), None, ALU.mult))
            step(dve.tensor_tensor(ex[0:1, :], own_f[0:1, SLOT_TILES:].to_broadcast([1, NTL]), steps[0:1, :], ALU.is_gt))
            step(dve.tensor_reduce(own_f[0:1, SLOT_TILES:], ex[0:1, :], AX.X, ALU.add))
            step(dve.tensor_scalar(own[0:1, 0:SLOT_TILES + 1], own_f[0:1, :], float(NE - 1), None, ALU.min))
            step(dve.tensor_copy(own[0:1, SLOT_TILES + 1:], end[0:1, :]))
            assert done[0] == STEPS_END

        @block.scalar
        def _(act):
            f.xT_done.start(act)
            over_chunks(act, NC, lambda c, p: f.keep(act, c, p, l_mm(c - 2)), None)
            act.wait_ge(step_done, 12)
            act.activation(ex[:, :], dd[:, :], ACT.Exp).then_inc(exp_done, 1)

        @block.tensor
        def _(pe):
            f.tp_done.start(pe)
            l_mm.start(pe)
            pe.wait_ge(consts_in, 16 * 8)

            def main(c, p):
                pe.wait_ge(*f.xT_done(c))
                for j in range(TJ):
                    pe.wait_ge(*l_done(c, j - 1))
                    for k in range(KD):
                        i = pe.matmul(ps[:, j % 2, 0:NE], f.xT[:, p, k, j * P:(j + 1) * P], gate_s[:, k, :], start=k == 0, stop=k == KD - 1)
                    i.then_inc(l_mm.sem, 1)

            over_chunks(pe, NC, lambda c, p: f.turn(pe, c, p, ident), main)
            pe.wait_ge(one_set, 2)
            pe.wait_ge(step_done, 16)
            both = lg[:, :, :].rearrange("p t e -> p (t e)")
            for w, bank in ((before, 0), (ones, 4)):
                for b in range(4):
                    i = pe.matmul(ps[:, bank + b, :], w[:, :], both[:, b * 512:(b + 1) * 512], start=True, stop=True)
                i.then_inc(rank_mm, 1)


def stage_experts(nc, tag, xn_d, table, expert_d, w0, w1, wo, ident_d, out_d):
    NT = SLOT_TILES
    HF = FF // 2
    with Stage(nc, tag) as st:
        ps = st.banks()
        ident = st.sb("ident", [P, P])
        tab = st.sb("tab", [NT, P])
        slots = st.sb("slots", [P, NT + 4], U32)
        own = st.sb("own", [1, NT + 1 + NE], I32)
        ix = st.sb("ix", [P, 4], U32)
        w0_s = st.sb("w0", [P, 2, KD, FF])
        w1_s = st.sb("w1", [P, 2, KD, FF])
        wo_s = st.sb("wo", [P, 2, FF // P, D])
        x = st.sb("x", [P, 4, D])
        xT = st.sb("xT", [P, 2, KD, P])
        g = st.sb("g", [P, 2, HF])
        h = st.sb("h", [P, 2, HF])
        hT = st.sb("hT", [P, 2, 4, P])
        y = st.sb("y", [P, 2, D])
        consts_in = st.sem("consts_in")
        tab_mm = st.sem("tab_mm")
        slots_done = st.sem("slots_done")
        tail_set = st.sem("tail_set")
        w_in = [st.sem(f"{n}_in") for n in ("w0", "w1", "wo")]
        ix_done = st.count("ix_done", 1)
        x_in = [st.sem(f"x_in{p}") for p in range(4)]
        x_mm = st.count("x_mm", 1, lead=3)
        xT_done = st.count("xT_done", 1)
        h_mm = st.count("h_mm", 4)
        g_done = st.count("g_done", 2)
        h_done = st.count("h_done", 2)
        t_mm = st.count("t_mm", 2)
        hT_done = st.count("hT_done", 2)
        y_mm = st.count("y_mm", 1)
        y_done = st.count("y_done", 1)
        stored = [st.sem("stored0"), st.sem("stored1")]
        block = st.ctx.enter_context(nc.Block())

        def before(i, p):
            return i * 32 + 16 * (p // 2)

        def rounds(eng, front, main):
            n = eng.value_load(own[0:1, NT:NT + 1], min_val=1, max_val=NT // 4)
            if front:
                front(0, 0, 0)
            with eng.Fori(0, n) as i:
                for p in range(4):
                    if front:
                        front(i + 1 if p == 3 else i, i * 4 + (p + 1), (p + 1) % 4)
                    main(i, i * 4 + p, p)
            return n

        def tile_rows(t, c):
            return t.rearrange("(c p) d -> c p d", p=P)[bass.ds(c, 1)].rearrange("o p d -> p (o d)")

        @block.sync
        def _(sp):
            sp.dma_start(ident[:, :], ident_d).then_inc(consts_in, 16)
            sp.dma_start(tab[:, :], table.rearrange("(t p) o -> t (p o)", p=P)).then_inc(consts_in, 16)
            sp.dma_start(own[:, :], expert_d).then_inc(consts_in, 16)
            sp.wait_ge(consts_in, 48)

            def load(e, p, ended):
                for n, (dst, src) in enumerate(((w0_s, w0), (w1_s, w1), (wo_s, wo))):
                    if ended is not None:
                        sp.wait_ge(*(y_mm if n == 2 else h_mm)(ended - 1))
                        st.plain(sp)
                    if not isinstance(e, int) or e:
                        sp.wait_ge(w_in[n], e * 16)
                        st.plain(sp)
                    src_e = src[e:e + 1] if isinstance(e, int) else src[bass.ds(e, 1)]
                    sp.dma_start(dst[:, p], src_e.rearrange("o (k p) n -> p (o k) n", p=P)).then_inc(w_in[n], 16)

            load(0, 0, None)
            load(1, 1, None)
            with sp.Fori(1, NE // 2) as i:
                for p in range(2):
                    load(i * 2 + p, p, sp.value_load(own[0:1, bass.ds(i * 2 + (NT + 1 - 2 + p), 1)], min_val=0, max_val=NT))
            for n in range(3):
                sp.wait_ge(w_in[n], 16 * NE)

        @block.gpsimd
        def _(pool):
            ix_done.start(pool)
            pool.memset(slots[:, NT:], 0).then_inc(tail_set, 1)
            pool.wait_ge(tail_set, 1)
            pool.wait_ge(slots_done, 1)
            pool.wait_ge(consts_in, 48)

            def gather(c, p):
                pool.wait_ge(*x_mm(c - 4))
                st.plain(pool)
                pool.tensor_copy(ix[:, p:p + 1], slots[:, bass.ds(c, 1)]).then_inc(ix_done.sem, 1)
                pool.wait_ge(*ix_done(c))
                st.plain(pool)
                pool.indirect_dma_start(out=x[:, p, :], out_offset=None, in_=xn_d,
                                        in_offset=bass.IndirectOffsetOnAxis(ap=ix[:, p:p + 1], axis=0)).then_inc(x_in[p], 16)

            n = rounds(pool, None, lambda i, c, p: gather(c, p))
            gather(n * 4, 0)
            pool.wait_ge(x_in[0], n * 16 + 16)
            st.plain(pool)

        @block.vector
        def _(dve):
            for s in (h_done, y_done):
                s.start(dve)
            dve.wait_ge(tab_mm, 1)
            dve.tensor_copy(slots[:, 0:NT], ps[:, 0, 0:NT]).then_inc(slots_done, 1)
            dve.wait_ge(consts_in, 48)

            def main(i, c, p):
                for a in range(2):
                    dve.wait_ge(*g_done(c, a + 1))
                    dve.wait_ge(*h_mm(c, 2 * a + 2))
                    dve.wait_ge(*t_mm(c - 1, a + 1))
                    dve.tensor_tensor(h[:, a], g[:, a], ps[:, 2 * a + 1, :], ALU.mult).then_inc(h_done.sem, 1)
                dve.wait_ge(*y_mm(c))
                dve.wait_ge(stored[p % 2], before(i, p))
                dve.tensor_copy(y[:, p % 2, :], ps[:, 7, :]).then_inc(y_done.sem, 1)

            rounds(dve, None, main)

        @block.scalar
        def _(act):
            for s in (xT_done, g_done, hT_done):
                s.start(act)
            act.wait_ge(consts_in, 48)

            def front(i, c, p):
                act.wait_ge(*x_mm(c))
                act.wait_ge(*h_mm(c - 2))
                act.activation(xT[:, p % 2], ps[:, 6, :].rearrange("p (k t) -> p k t", k=KD), ACT.Copy).then_inc(xT_done.sem, 1)

            def main(i, c, p):
                def silu(a):
                    act.wait_ge(*h_mm(c, 2 * a + 1))
                    act.wait_ge(*h_done(c - 1, a + 1))
                    act.activation(g[:, a], ps[:, 2 * a, :], ACT.Silu).then_inc(g_done.sem, 1)

                def keep(a):
                    act.wait_ge(*t_mm(c, a + 1))
                    act.wait_ge(*y_mm(c - 1))
                    act.activation(hT[:, a], ps[:, 4 + a, :].rearrange("p (k t) -> p k t", k=4), ACT.Copy).then_inc(hT_done.sem, 1)

                silu(0)
                silu(1)
                keep(0)
                keep(1)
                act.wait_ge(*y_done(c))
                st.plain(act)
                act.dma_start(tile_rows(out_d, c), y[:, p % 2, :]).then_inc(stored[p % 2], 16)

            n = rounds(act, front, main)
            for p in range(2):
                act.wait_ge(stored[p], n * 32)
                st.plain(act)

        @block.tensor
        def _(pe):
            for s in (x_mm, h_mm, t_mm, y_mm):
                s.start(pe)
            pe.wait_ge(consts_in, 48)
            pe.transpose(ps[:, 0, 0:NT], tab[:, :], ident[0:NT, 0:NT]).then_inc(tab_mm, 1)
            pe.wait_ge(slots_done, 1)

            def front(i, c, p):
                pe.wait_ge(x_in[p], i * 16 + 16)
                pe.wait_ge(*xT_done(c - 1))
                for k in range(KD):
                    mm = pe.transpose(ps[:, 6, k * P:(k + 1) * P], x[:, p, k * P:(k + 1) * P], ident[:, :])
                mm.then_inc(x_mm.sem, 1)

            def main(i, c, p):
                e = pe.value_load(own[0:1, bass.ds(c, 1)], min_val=0, max_val=NE - 1)
                odd = e % 2

                def up(a, which):
                    w = pick((w0_s, w1_s)[which], odd)
                    if a == 0:
                        pe.wait_ge(w_in[which], e * 16 + 16)
                    pe.wait_ge(*h_done(c - 1, a + 1))
                    for k in range(KD):
                        mm = pe.matmul(ps[:, 2 * a + which, :], xT[:, p % 2, k, :], w[:, k, a * HF:(a + 1) * HF], start=k == 0, stop=k == KD - 1)
                    mm.then_inc(h_mm.sem, 1)

                def turn(a):
                    pe.wait_ge(*h_done(c, a + 1))
                    pe.wait_ge(*hT_done(c - 1, a + 1))
                    for k in range(4):
                        mm = pe.transpose(ps[:, 4 + a, k * P:(k + 1) * P], h[:, a, k * P:(k + 1) * P], ident[:, :])
                    mm.then_inc(t_mm.sem, 1)

                def down(k):
                    return pe.matmul(ps[:, 7, :], hT[:, k // 4, k % 4, :], pick(wo_s, odd)[:, k, :], start=k == 0, stop=k == 7)

                pe.wait_ge(*xT_done(c))
                up(0, 0)
                up(0, 1)
                up(1, 0)
                turn(0)
                up(1, 1)
                pe.wait_ge(w_in[2], e * 16 + 16)
                pe.wait_ge(*hT_done(c, 1))
                pe.wait_ge(*y_done(c - 1))
                for k in range(3):
                    down(k)
                turn(1)
                down(3)
                pe.wait_ge(*hT_done(c, 2))
                for k in range(4, 8):
                    mm = down(k)
                mm.then_inc(y_mm.sem, 1)

            rounds(pe, front, main)


def stage_combine(nc, tag, x_in, rows_d, route_d, weight_d, x_out):
    RING = 4
    TURNS = NTL // RING
    with Stage(nc, tag) as st:
        slot = st.sb("slot", [P, 2, NTL], U32)
        wt = st.sb("wt", [P, 2, NTL])
        ix = st.sb("ix", [P, RING, 2], U32)
        cw = st.sb("cw", [P, RING, 2])
        g = st.sb("g", [P, RING, 2, D])
        x = st.sb("x", [P, RING, D])
        mid = st.sb("mid", [P, RING, D])
        out = st.sb("out", [P, RING, D])
        consts_in = st.sem("consts_in")
        ix_done = st.count("ix_done", 1)
        g_in = [[st.sem(f"g_in{p}{i}") for i in range(2)] for p in range(RING)]
        x_ld = [st.sem(f"x_ld{p}") for p in range(RING)]
        cw_done = st.count("cw_done", 1)
        mid_done = st.count("mid_done", 1)
        out_done = st.count("out_done", 1)
        stored = [st.sem(f"stored{p}") for p in range(RING)]
        block = st.ctx.enter_context(nc.Block())

        def column(t, c):
            return t[:, :, c:c + 1] if isinstance(c, int) else t[:, :, bass.ds(c, 1)]

        def tile_rows(t, c):
            v = t.rearrange("(c p) d -> c p d", p=P)
            return v[c] if isinstance(c, int) else v[bass.ds(c, 1)].rearrange("o p d -> p (o d)")

        def turns(eng, body):
            for p in range(RING):
                body(0, p, p)
            with eng.Fori(1, TURNS) as i:
                for p in range(RING):
                    body(i, i * RING + p, p)

        @block.sync
        def _(sp):
            sp.dma_start(slot[:, :, :], route_d).then_inc(consts_in, 16)
            sp.dma_start(wt[:, :, :], weight_d).then_inc(consts_in, 16)

            def load(i, c, p):
                if not isinstance(i, int):
                    sp.wait_ge(*mid_done(c - RING))
                    st.plain(sp)
                sp.dma_start(x[:, p, :], tile_rows(x_in, c)).then_inc(x_ld[p], 16)

            turns(sp, load)

        @block.vector
        def _(dve):
            for s in (ix_done, cw_done, mid_done, out_done):
                s.start(dve)
            dve.wait_ge(consts_in, 32)

            def prepare(c, p):
                dve.tensor_copy(ix[:, p].unsqueeze(2), column(slot, c)).then_inc(ix_done.sem, 1)
                dve.tensor_copy(cw[:, p].unsqueeze(2), column(wt, c)).then_inc(cw_done.sem, 1)

            def add(i, c, p):
                dve.wait_ge(x_ld[p], i * 16 + 16)
                dve.wait_ge(g_in[p][0], i * 16 + 16)
                dve.wait_ge(*cw_done(c))
                dve.scalar_tensor_tensor(mid[:, p, :], g[:, p, 0, :], cw[:, p, 0:1], x[:, p, :], ALU.mult, ALU.add).then_inc(mid_done.sem, 1)
                dve.wait_ge(*mid_done(c))
                dve.wait_ge(g_in[p][1], i * 16 + 16)
                dve.wait_ge(stored[p], i * 16)
                dve.scalar_tensor_tensor(out[:, p, :], g[:, p, 1, :], cw[:, p, 1:2], mid[:, p, :], ALU.mult, ALU.add).then_inc(out_done.sem, 1)

            for p in range(RING):
                prepare(p, p)
            with dve.Fori(0, TURNS - 1) as i:
                for p in range(RING):
                    add(i, i * RING + p, p)
                    dve.wait_ge(*out_done(i * RING + p))
                    prepare(i * RING + (p + RING), p)
            for p in range(RING):
                add(TURNS - 1, NTL - RING + p, p)

        @block.gpsimd
        def _(pool):
            def gather(i, c, p):
                pool.wait_ge(*ix_done(c))
                if not isinstance(i, int):
                    pool.wait_ge(*out_done(c - RING))
                st.plain(pool)
                for k in range(2):
                    pool.indirect_dma_start(out=g[:, p, k, :], out_offset=None, in_=rows_d,
                                            in_offset=bass.IndirectOffsetOnAxis(ap=ix[:, p, k:k + 1], axis=0)).then_inc(g_in[p][k], 16)

            turns(pool, gather)

        @block.scalar
        def _(act):
            def store(i, c, p):
                act.wait_ge(*out_done(c))
                st.plain(act)
                act.dma_start(tile_rows(x_out, c), out[:, p, :]).then_inc(stored[p], 16)

            turns(act, store)
            for p in range(RING):
                act.wait_ge(stored[p], 16 * TURNS)


def shape_constants():
    f = np.float32
    j = np.arange(P)
    e = np.arange(NE)
    causal = np.where(np.arange(SK)[None] <= np.arange(S)[:, None], 0.0, NEG).astype(f)
    fwd, inv = transform_tables()
    return {
        "ident": np.eye(P, dtype=f),
        "tri": np.where(j[None] < j[:, None], NEG, 0.0).astype(f),
        "causal": np.concatenate([causal] * B),
        "fwd": fwd, "inv": inv,
        "before": (j[:, None] < j[None]).astype(f),
        "iota": (e - NE).astype(f)[None],
        "steps": (P * np.arange(NTL)).astype(f)[None],
        "upto": (e[None] <= e[:, None]).astype(f).reshape(1, NE * NE),
        "tiles": np.arange(SLOT_TILES).astype(f)[None],
        "token": (j[:, None] + P * np.arange(NTL)[None]).astype(f),
    }


def build_decoder(nc, t, out):
    def rows(name, n=N, w=D, dt=F32):
        return nc.dram_tensor(name, (n, w), dt).ap()

    x1, x2, h1, h2, x3, x4, x5 = (rows(n) for n in ("x1", "x2", "h1", "h2", "x3", "x4", "x5"))
    k, v, q, y = (rows(n) for n in ("conv_k", "conv_v", "conv_q", "conv_y"))
    ident = t["ident"]
    a = lambda n: t["L0_attn_" + n]
    stage_attention(nc, t["x"], x1, ident, t["tri"], a("Wq"), a("Wk"), a("Wv"), a("bq"), a("bk"), a("bv"))
    a = lambda n: t["L0_xattn_" + n]
    stage_cross(nc, "xa", x1, x2, ident, t["ctxT"], t["mask"], a("Wq"), a("Wk"), a("Wv"), a("bq"), a("bk"), a("bv"))
    a = lambda n: t["L0_ffn_" + n]
    for blk, (src, dst) in enumerate(((x2, h1), (h1, h2), (h2, x3))):
        i = slice(2 * blk, 2 * blk + 2)
        stage_ffn(nc, f"ff{blk}", src, dst, ident, a("qweights")[i], a("scales")[i], a("lora_a")[i], a("lora_b")[i],
                  a("biases")[i], a("ln_gamma")[blk], a("ln_beta")[blk], blk == 0, x2 if blk == 2 else None)
    a = lambda n: t["L1_attn_" + n]
    stage_project(nc, "pr", x3, [k, v, q], ident, [a("Wk"), a("Wv"), a("Wq")], [a("bk"), a("bv"), a("bq")])
    stage_conv(nc, k, v, y, a("k_kernel"), a("ssm_kernel"), a("k_D"), a("D"), t["fwd"], t["inv"])
    stage_gated_out(nc, "go", x3, y, q, x4, ident, a("Wo"), a("bo"))
    a = lambda n: t["L1_xattn_" + n]
    stage_cross(nc, "xb", x4, x5, ident, t["ctxT"], t["causal"], a("Wq"), a("Wk"), a("Wv"), wo=a("Wo"))
    a = lambda n: t["L1_ffn_" + n]
    xn = rows("moe_xn")
    slot_rows = rows("slot_rows", SLOT_TILES * P)
    table = rows("slot_token", SLOT_TILES * P, 1)
    own = rows("tile_expert", 1, SLOT_TILES + 1 + NE, I32)
    route = nc.dram_tensor("token_slots", (P, 2, NTL), U32).ap()
    weight = nc.dram_tensor("token_weights", (P, 2, NTL), F32).ap()
    stage_route(nc, "ro", x5, xn, ident, a("gate_kernel"), table, route, weight, own, slot_rows,
                [t[n] for n in ("before", "iota", "steps", "upto", "tiles", "token")])
    stage_experts(nc, "ex", xn, table, own, a("w0"), a("w1"), a("wo"), ident, slot_rows)
    stage_combine(nc, "co", x5, slot_rows, route, weight, out)


def laid_out(inputs):
    t = {n: np.asarray(v) for n, v in inputs.items()}
    t["x"] = t["x"].reshape(N, D)
    t["mask"] = t.pop("mask_BxSxS2_ff1").reshape(N, SK)
    t["ctxT"] = t.pop("ctx_1024").reshape(B * SK, D).T
    for n in ("L0_xattn_Wq", "L0_xattn_Wk", "L0_xattn_Wv", "L1_attn_Wq", "L1_attn_Wk", "L1_attn_Wv", "L1_attn_Wo",
              "L1_attn_k_kernel", "L1_attn_ssm_kernel", "L1_xattn_Wq", "L1_xattn_Wk", "L1_xattn_Wv", "L1_xattn_Wo"):
        t[n] = t[n].T
    for n in ("L0_ffn_qweights", "L0_ffn_scales", "L0_ffn_lora_b"):
        t[n] = t[n].transpose(0, 2, 1)
    t.update(shape_constants())
    return {n: np.ascontiguousarray(v) for n, v in t.items()}


def kernel(**inputs):
    from concourse import bacc
    from concourse.bass_utils import run_bass_kernel_spmd

    nc = bacc.Bacc("TRN2", target_bir_lowering=False, num_devices=1)
    arrays = laid_out(inputs)
    t = {n: nc.dram_tensor(n, v.shape, mybir.dt.from_np(v.dtype), kind="ExternalInput").ap() for n, v in arrays.items()}
    out = nc.dram_tensor("out", (N, D), F32, kind="ExternalOutput").ap()
    build_decoder(nc, t, out)
    r = run_bass_kernel_spmd(nc, [arrays], core_ids=[0])
    return r.results[0]["out"].reshape(B, S, D)
```
